# Optimizing a Trainium2 kernel written in Bass

```python
import numpy as np
import jax
import jax.numpy as jnp

def _softmax(x, axis=-1):
    return jax.nn.softmax(x, axis=axis)

def _gelu(x):
    return jax.nn.gelu(x, approximate=True)

def _silu(x):
    return jax.nn.silu(x)

def _sigmoid(x):
    return jax.nn.sigmoid(x)

def _layernorm(x, axis=-1, eps=1e-05):
    m = jnp.mean(x, axis=axis, keepdims=True)
    v = jnp.var(x, axis=axis, keepdims=True)
    return (x - m) / jnp.sqrt(v + eps)

def _scatter_add(tgt, idx, src, axis=0):
    return tgt.at[idx].add(src)

def _segment_sum(src, seg, n):
    return jax.ops.segment_sum(src, seg, n)
kernel_name = 'mk_decoder_preln_d1_seqx_r4_babcd8'

def setup_inputs(seed: int=0):
    np.random.seed(seed)
    _w = jnp.asarray

    def _rec_inputs():
        import jax
        import jax.numpy as jnp
        _rk = jax.random.key(seed)
        x = 7.22e-05 + 1 * jax.random.normal(jax.random.fold_in(_rk, 1), (2, 1024, 256), jnp.float32)
        _lenS = 1024 - jax.random.randint(jax.random.fold_in(_rk, 7), (2,), 0, max(1, 1024 // 4) + 1, jnp.int32)
        _lenS2 = 77 - jax.random.randint(jax.random.fold_in(_rk, 8), (2,), 0, max(1, 77 // 4) + 1, jnp.int32)
        _ctx_768P = jax.random.normal(jax.random.fold_in(_rk, 11), (2, 16, 192), jnp.float32)
        _ctx_768c = jax.random.dirichlet(jax.random.fold_in(_rk, 511), 0.3 * jnp.ones((16,), jnp.float32), (2, 77))
        _ctx_768t = jnp.einsum('bsk,bkd->bsd', _ctx_768c, _ctx_768P)
        _ctx_768t = _ctx_768t * jax.lax.rsqrt(jnp.mean(jnp.square(_ctx_768t)) + 1e-12) * 0.953939
        ctx_768 = 2.09791e-05 + 1.00001 * (_ctx_768t + 0.3 * jax.random.normal(jax.random.fold_in(_rk, 611), (2, 77, 192), jnp.float32))
        return (x, ctx_768)
    x, ctx_768 = _rec_inputs()

    def _L0_attn_setup():
        import jax, jax.numpy as jnp
        import numpy as np
        B, L, D, H = (4, 256, 256, 16)
        HD = D // H
        MAX_LEN = 256
        SCALE = HD ** 0.5

        def _rel_idx(seq_len):
            r = jnp.arange(seq_len)
            dist = r[None, :] - r[:, None]
            return jnp.clip(dist, -MAX_LEN, MAX_LEN) + MAX_LEN
        key = jax.random.key(seed)
        ks = jax.random.split(key, 7)
        sd = 1.0 / np.sqrt(D)
        x = jax.random.normal(ks[0], (B, L, D), dtype=jnp.float32)
        Wq = jax.random.normal(ks[1], (D, D), dtype=jnp.float32) * sd
        Wk = jax.random.normal(ks[2], (D, D), dtype=jnp.float32) * sd
        Wv = jax.random.normal(ks[3], (D, D), dtype=jnp.float32) * sd
        Wo = jax.random.normal(ks[4], (D, D), dtype=jnp.float32) * sd
        pek = jax.random.normal(ks[5], (2 * MAX_LEN + 1, HD), dtype=jnp.float32) / np.sqrt(HD)
        pev = jax.random.normal(ks[6], (2 * MAX_LEN + 1, HD), dtype=jnp.float32) / np.sqrt(HD)
        return {'x': x, 'Wq': Wq, 'Wk': Wk, 'Wv': Wv, 'Wo': Wo, 'pek': pek, 'pev': pev}
    _L0_attn_all = _L0_attn_setup()
    _L0_attn_in = {k: v for k, v in _L0_attn_all.items() if k in ('Wq', 'Wk', 'Wv', 'Wo', 'pek', 'pev')}
    del _L0_attn_all

    def _L0_xattn_setup():
        import jax, jax.numpy as jnp
        import numpy as np
        HEADS = 16
        DIM_HEAD = 64
        key = jax.random.key(seed)
        ks = jax.random.split(key, 7)
        B, Nq, Dq = (4, 512, 256)
        Nk, Dc = (256, 192)
        inner = HEADS * DIM_HEAD
        sq = 1.0 / np.sqrt(Dq)
        sc = 1.0 / np.sqrt(Dc)
        si = 1.0 / np.sqrt(inner)
        return {'x': jax.random.normal(ks[0], (B, Nq, Dq), dtype=jnp.float32), 'context': jax.random.normal(ks[1], (B, Nk, Dc), dtype=jnp.float32), 'Wq': jax.random.normal(ks[2], (Dq, inner), dtype=jnp.float32) * sq, 'Wk': jax.random.normal(ks[3], (Dc, inner), dtype=jnp.float32) * sc, 'Wv': jax.random.normal(ks[4], (Dc, inner), dtype=jnp.float32) * sc, 'Wo': jax.random.normal(ks[5], (inner, Dq), dtype=jnp.float32) * si, 'bo': jax.random.normal(ks[6], (Dq,), dtype=jnp.float32) * 0.01}
    _L0_xattn_all = _L0_xattn_setup()
    _L0_xattn_in = {k: v for k, v in _L0_xattn_all.items() if k in ('Wq', 'Wk', 'Wv', 'Wo', 'bo')}
    del _L0_xattn_all

    def _L0_ffn_setup():
        import jax, jax.numpy as jnp
        import numpy as np
        H = 256
        E = 8
        B, S = (4, 512)
        key = jax.random.key(seed)
        k1, k2, k3, k4 = jax.random.split(key, 4)
        x = jax.random.normal(k1, (B, S, H), dtype=jnp.float32)
        wg = jax.random.normal(k2, (H, E), dtype=jnp.float32) * 0.02
        W = jax.random.normal(k3, (E, H, H), dtype=jnp.float32) * 0.02
        b = jax.random.normal(k4, (E, H), dtype=jnp.float32) * 0.02
        return {'x': x, 'wg': wg, 'W': W, 'b': b}
    _L0_ffn_all = _L0_ffn_setup()
    _L0_ffn_in = {k: v for k, v in _L0_ffn_all.items() if k in ('wg', 'W', 'b')}
    del _L0_ffn_all
    return {'x': x, 'ctx_768': ctx_768, 'L0_attn_Wq': _L0_attn_in['Wq'], 'L0_attn_Wk': _L0_attn_in['Wk'], 'L0_attn_Wv': _L0_attn_in['Wv'], 'L0_attn_Wo': _L0_attn_in['Wo'], 'L0_attn_pek': _L0_attn_in['pek'], 'L0_attn_pev': _L0_attn_in['pev'], 'L0_xattn_Wq': _L0_xattn_in['Wq'], 'L0_xattn_Wk': _L0_xattn_in['Wk'], 'L0_xattn_Wv': _L0_xattn_in['Wv'], 'L0_xattn_Wo': _L0_xattn_in['Wo'], 'L0_xattn_bo': _L0_xattn_in['bo'], 'L0_ffn_wg': _L0_ffn_in['wg'], 'L0_ffn_W': _L0_ffn_in['W'], 'L0_ffn_b': _L0_ffn_in['b']}

def reference(x, ctx_768, L0_attn_Wq, L0_attn_Wk, L0_attn_Wv, L0_attn_Wo, L0_attn_pek, L0_attn_pev, L0_xattn_Wq, L0_xattn_Wk, L0_xattn_Wv, L0_xattn_Wo, L0_xattn_bo, L0_ffn_wg, L0_ffn_W, L0_ffn_b):
    import jax
    import jax.numpy as jnp

    def _L0_attn_ref(x, Wq, Wk, Wv, Wo, pek, pev):
        import jax, jax.numpy as jnp
        import numpy as np
        B, L, D, H = (4, 256, 256, 16)
        HD = D // H
        MAX_LEN = 256
        SCALE = HD ** 0.5

        def _rel_idx(seq_len):
            r = jnp.arange(seq_len)
            dist = r[None, :] - r[:, None]
            return jnp.clip(dist, -MAX_LEN, MAX_LEN) + MAX_LEN
        b, s, _ = x.shape

        def proj(W):
            return (x @ W.T).reshape(b, s, H, HD).transpose(0, 2, 1, 3)
        Q, K, V = (proj(Wq), proj(Wk), proj(Wv))
        scores = jnp.einsum('bhqd,bhkd->bhqk', Q, K) / SCALE
        idx = _rel_idx(s)
        rel_k = pek[idx]
        scores = scores + jnp.einsum('bhqd,qkd->bhqk', Q, rel_k) / SCALE
        causal = jnp.tril(jnp.ones((s, s), dtype=bool))
        scores = jnp.where(causal[None, None], scores, -jnp.inf)
        attn = jax.nn.softmax(scores, axis=-1)
        out = jnp.einsum('bhqk,bhkd->bhqd', attn, V)
        rel_v = pev[idx]
        out = out + jnp.einsum('bhqk,qkd->bhqd', attn, rel_v)
        out = out.transpose(0, 2, 1, 3).reshape(b, s, D)
        return out @ Wo.T

    def _L0_xattn_ref(x, context, Wq, Wk, Wv, Wo, bo):
        import jax, jax.numpy as jnp
        import numpy as np
        HEADS = 16
        DIM_HEAD = 64
        B, Nq, _ = x.shape
        Nk = context.shape[1]
        h, dh = (HEADS, DIM_HEAD)
        q = (x @ Wq).reshape(B, Nq, h, dh)
        k = (context @ Wk).reshape(B, Nk, h, dh)
        v = (context @ Wv).reshape(B, Nk, h, dh)
        scale = 1.0 / jnp.sqrt(jnp.asarray(dh, dtype=x.dtype))
        scores = jnp.einsum('bqhd,bkhd->bhqk', q, k) * scale
        attn = jax.nn.softmax(scores, axis=-1)
        out = jnp.einsum('bhqk,bkhd->bqhd', attn, v).reshape(B, Nq, h * dh)
        return out @ Wo + bo

    def _L0_ffn_ref(x, wg, W, b):
        import jax, jax.numpy as jnp
        import numpy as np
        H = 256
        E = 8
        B, S = (4, 512)
        Bb, Ss, Hh = x.shape
        Ee = wg.shape[1]
        T = Bb * Ss
        C = T // Ee
        xt = x.reshape(T, Hh)
        logits = xt @ wg
        probs = jax.nn.softmax(logits, axis=-1)
        idx = jnp.argmax(probs, axis=-1)
        mask = jax.nn.one_hot(idx, Ee, dtype=xt.dtype)
        locations = jnp.cumsum(mask, axis=0) - mask
        mask = mask * (locations < C).astype(xt.dtype)
        gate = jnp.sum(probs * mask, axis=-1)
        loc_s = jnp.sum(locations * mask, axis=-1).astype(jnp.int32)
        loc_oh = jax.nn.one_hot(loc_s, C, dtype=xt.dtype)
        dispatch = mask[:, :, None] * loc_oh[:, None, :]
        combine = gate[:, None, None] * dispatch
        exp_in = jnp.einsum('tec,th->ech', dispatch, xt)
        exp_out = jnp.einsum('ech,efh->ecf', exp_in, W) + b[:, None, :]
        out = jnp.einsum('tec,ecf->tf', combine, exp_out)
        return out.reshape(Bb, Ss, Hh)
    x = x + _L0_attn_ref(_layernorm(x, axis=-1), L0_attn_Wq, L0_attn_Wk, L0_attn_Wv, L0_attn_Wo, L0_attn_pek, L0_attn_pev)
    x = x + _L0_xattn_ref(_layernorm(x, axis=-1), ctx_768, L0_xattn_Wq, L0_xattn_Wk, L0_xattn_Wv, L0_xattn_Wo, L0_xattn_bo)
    x = x + _L0_ffn_ref(_layernorm(x, axis=-1), L0_ffn_wg, L0_ffn_W, L0_ffn_b)
    return x

_drawn_inputs = setup_inputs


def setup_inputs(seed=0):
    import zlib

    import numpy as np

    out = dict(_drawn_inputs(seed))
    spreads = {}
    factors = {'L0_xattn_bo': 5.611, 'L0_ffn_b': 22.201}
    for name, (base, spread) in spreads.items():
        noise = np.random.default_rng([zlib.crc32(name.encode()), seed]).standard_normal(out[name].shape)
        drawn = base * np.exp(spread * noise) if base else spread * noise
        out[name] = jnp.asarray(drawn.astype(out[name].dtype))
    for name, factor in factors.items():
        out[name] = (out[name] * factor).astype(out[name].dtype)
    return out
```

```python
from contextlib import ExitStack

import concourse.bass as bass
from concourse import mybir

F32 = mybir.dt.float32
BF16 = mybir.dt.bfloat16
U32 = mybir.dt.uint32
ALU = mybir.AluOpType
ACT = mybir.ActivationFunctionType
AX = mybir.AxisListType

P = 128
BATCH, SEQ, D = 2, 1024, 256
TOKENS = BATCH * SEQ
TILES = TOKENS // P
TPB = SEQ // P
KC = D // P
HEADS, HD = 16, 16
PAIRS = HEADS // 2
QUADS = HEADS // 4
SCALE = HD ** 0.5
REL = 256
TERMS = 3
Q_SLOTS = (0, 0, 1, 1, 0, 2)
K_SLOTS = (0, 1, 0, 1, 2, 0)
STACK = len(Q_SLOTS) * HD
BAND = 3 * P
ROW = 127 + BAND
XH, XD = 16, 64
INNER = XH * XD
NCTX, DCTX = 77, 192
CTXC = DCTX // 2
XBANKS = ((0, 6), (6, 12), (12, 16))
XK = XH * NCTX
XCH = (XK + P - 1) // P
XTAIL = XK - (XCH - 1) * P
RSTEPS = 10
EXPERTS = 8
CAP = TOKENS // EXPERTS
EPS = 1e-5
BIG = 1e30
GROUPS = 4
GT = TOKENS // GROUPS // P
BANK = 512


def decoder_layer(nc, x, ctxT, wqT, wkT, wvT, woT, pekT, pek0, pev, xwqT, xwk, xwv, xwo, xbo, wg, weT, be,
                  ident, ones, diag, fold, earlier, experts, out):
    nc.disable_value_cache = True
    qparts = nc.dram_tensor("qparts", (TERMS, D, TOKENS), BF16)
    kparts = nc.dram_tensor("kparts", (TERMS, D, TOKENS), BF16)
    pparts = nc.dram_tensor("pparts", (TERMS, HD, REL), BF16)
    pvrows = nc.dram_tensor("pvrows", (ROW + 1, HD), F32)
    rel = nc.dram_tensor("rel", (2 * HEADS, P, ROW), F32)
    gmat = nc.dram_tensor("gmat", (P, KC, BATCH, XK), F32)
    umat = nc.dram_tensor("umat", (BATCH, XK, D), F32)

    ctx = ExitStack()
    with ctx:
        def sb(name, shape, dt, where=ctx):
            return where.enter_context(nc.sbuf_tensor(name, shape, dt))

        def sem(name):
            return ctx.enter_context(nc.semaphore(name))

        ps = ctx.enter_context(nc.psum_tensor("ps", [P, 8, BANK], F32))
        S_BANK, T_BANK, R_BANK, O_BANK = 0, 4, 6, 7

        idf = sb("idf", [P, P], F32)
        x1 = sb("x1", [P, TILES, D], F32)
        half = sb("half", [P, 1], F32)

        proj = ExitStack()
        v_sb = sb("v_sb", [P, TILES, D], F32)
        pk0 = sb("pk0", [P, 1], F32)
        pev0 = sb("pev0", [P, HD], F32)
        xg = sb("xg", [P, 2, GT, D], F32, proj)
        hg = sb("hg", [P, GT, D], F32, proj)
        hT = sb("hT", [P, 2, KC, BANK], F32, proj)
        wq_sb = sb("wq_sb", [P, KC, D], F32, proj)
        wk_sb = sb("wk_sb", [P, KC, D], F32, proj)
        wv_sb = sb("wv_sb", [P, KC, D], F32, proj)
        st1 = sb("st1", [P, GT, 6], F32, proj)
        mv1 = sb("mv1", [P, GT, 2], F32, proj)
        rstd1 = sb("rstd1", [P, GT], F32, proj)
        full = sb("full", [P, 2, BANK], F32, proj)
        rest = sb("rest", [P, 2, BANK], F32, proj)
        parts = sb("parts", [P, 2, TERMS, BANK], BF16, proj)
        pk_in = sb("pk_in", [HD, REL + 1], F32, proj)
        pk_d = sb("pk_d", [HD, REL], F32, proj)
        pk_r = sb("pk_r", [HD, REL], F32, proj)
        pk_parts = sb("pk_parts", [HD, TERMS, REL], BF16, proj)
        pv_in = sb("pv_in", [P, 2, HD], F32, proj)
        zrow = sb("zrow", [P, P], F32, proj)
        brow = sb("brow", [P, P - 1], F32, proj)
        xq_w = sb("xq_w", [P, INNER // P, D], F32, proj)
        xo_w = sb("xo_w", [P, INNER // P, D], F32, proj)
        xk_w = sb("xk_w", [CTXC, 2, INNER], F32, proj)
        xv_w = sb("xv_w", [CTXC, 2, INNER], F32, proj)
        ctx_sb = sb("ctx_sb", [CTXC, 2, BATCH * NCTX], F32, proj)
        xkT = sb("xkT", [P, INNER // P, BATCH * NCTX], F32, proj)
        xvT = sb("xvT", [P, INNER // P, BATCH * NCTX], F32, proj)
        g_out = sb("g_out", [P, KC, BATCH, XK], F32, proj)
        u_out = sb("u_out", [NCTX, BATCH, XH, D], F32, proj)
        proj.close()

        att = ExitStack()
        q6 = sb("q6", [STACK, HEADS, SEQ], BF16, att)
        k6 = sb("k6", [STACK, HEADS, SEQ], BF16, att)
        p6 = sb("p6", [STACK, REL], BF16, att)
        rel_out = sb("rel_out", [P, 4, REL], F32, att)
        bias = sb("bias", [P, HEADS, BAND], F32, att)
        prob = sb("prob", [P, 2, SEQ], F32, att)
        pT = sb("pT", [P, 2, TPB, P], F32, att)
        bandT = sb("bandT", [P, 3, HEADS, P], F32, att)
        pvt = sb("pvt", [P, 3, P * HD], F32, att)
        far = sb("far", [P, 2], F32, att)
        low = sb("low", [P, 2], F32, att)
        rsum = sb("rsum", [P, 2, HEADS], F32, att)
        rrec = sb("rrec", [P, HEADS], F32, att)
        picked = sb("picked", [P, HEADS, P], F32, att)
        diag_sb = sb("diag_sb", [P, P], F32, att)
        fold_sb = sb("fold_sb", [P, HD], F32, att)
        zb = sb("zb", [P, D], BF16, att)
        att.close()

        late = ExitStack()
        wo_sb = sb("wo_sb", [P, KC, D], F32, late)
        xr = sb("xr", [P, 2, GT, D], F32, late)
        oT = sb("oT", [P, 2, KC, BANK], F32, late)
        bo = sb("bo", [P, D], F32, late)
        h2 = sb("h2", [P, 2, GT, D], F32, late)
        h2T = sb("h2T", [P, KC, TOKENS], F32, late)
        st2 = sb("st2", [P, GT, 6], F32, late)
        mv2 = sb("mv2", [P, 2, GT, 2], F32, late)
        rstd2 = sb("rstd2", [P, 2, GT], F32, late)
        g_sb = sb("g_sb", [P, KC, BATCH, XK], F32, late)
        u_sb = sb("u_sb", [P, BATCH, XCH, D], F32, late)
        h2s = sb("h2s", [P, 2, KC, P], F32, late)
        xlow = sb("xlow", [P, 2, XH], F32, late)
        xsum = sb("xsum", [P, 2, XH], F32, late)
        xrec = sb("xrec", [P, XH], F32, late)
        xp = sb("xp", [P, 2, XK], F32, late)
        xpT = sb("xpT", [P, 2, XCH, P], F32, late)
        st3 = sb("st3", [P, 6], F32, late)
        mvs = sb("mvs", [P, 2], F32, late)
        mv3 = sb("mv3", [P, TILES, 2], F32, late)
        rstd3 = sb("rstd3", [P, TILES], F32, late)
        we_sb = sb("we_sb", [P, KC, EXPERTS * D], F32, late)
        be_sb = sb("be_sb", [EXPERTS, D], F32, late)
        wg_sb = sb("wg_sb", [P, KC, EXPERTS], F32, late)
        earlier_sb = sb("earlier_sb", [P, P], F32, late)
        ones_sb = sb("ones_sb", [P, P], F32, late)
        e8 = sb("e8", [P, EXPERTS], F32, late)
        h3 = sb("h3", [P, 2, 2, D], F32, late)
        h3T = sb("h3T", [P, 2, KC * 2 * P], F32, late)
        top = sb("top", [P, 2], F32, late)
        below = sb("below", [P, 2, EXPERTS], F32, late)
        expb = sb("expb", [P, 2, EXPERTS], F32, late)
        den = sb("den", [P, 2], F32, late)
        gate = sb("gate", [P, 2], F32, late)
        cand = sb("cand", [P, 2, EXPERTS], F32, late)
        first_e = sb("first_e", [P, 2], F32, late)
        chosen = sb("chosen", [P, 2, 2, EXPERTS], F32, late)
        place = sb("place", [P, 2, EXPERTS], F32, late)
        count = sb("count", [P, EXPERTS], F32, late)
        kept = sb("kept", [P, 2, EXPERTS], F32, late)
        expw = sb("expw", [P, 2, EXPERTS], F32, late)
        wgt = sb("wgt", [P, 2, 2, EXPERTS], F32, late)
        wgtT = sb("wgtT", [EXPERTS, 2, 2 * P], F32, late)
        late.close()

        s_cst, s_w, s_set = sem("s_cst"), sem("s_w"), sem("s_set")
        s_x = [sem("s_x_0"), sem("s_x_1")]
        s_stat, s_agg, s_var, s_rstd, s_h = sem("s_stat"), sem("s_agg"), sem("s_var"), sem("s_rstd"), sem("s_h")
        s_proj, s_full, s_hi = sem("s_proj"), sem("s_full"), sem("s_hi")
        s_rest, s_mid, s_lo = sem("s_rest"), sem("s_mid"), sem("s_lo")
        s_parts = [sem("s_parts0"), sem("s_parts1")]
        s_v, s_vc = sem("s_v"), sem("s_vc")
        s_pk, s_pkp, s_pkd, s_pv, s_pvd, s_pad = (sem("s_pk"), sem("s_pkp"), sem("s_pkd"), sem("s_pv"),
                                                  sem("s_pvd"), sem("s_pad"))
        s_tab, s_qk, s_b = sem("s_tab"), sem("s_qk"), sem("s_b")
        s_r, s_s, s_far = sem("s_r"), sem("s_s"), sem("s_far")
        s_rc = sem("s_rc")
        s_rw = sem("s_rw")
        s_min = sem("s_min")
        s_exp = sem("s_exp")
        s_av = sem("s_av")
        s_cp = sem("s_cp")
        s_o = sem("s_o")
        s_on = sem("s_on")
        s_rr = sem("s_rr")
        s_t = [sem("s_t0"), sem("s_t1")]
        s_tc = [sem("s_tc0"), sem("s_tc1")]
        s_z = sem("s_z")
        s_go = {e: sem(f"s_go_{e}") for e in ("sp", "pool", "dve", "pe")}
        s_done = sem("s_done")
        s_xw, s_xwc = sem("s_xw"), [sem("s_xwc0"), sem("s_xwc1")]
        s_xin, s_gu = sem("s_xin"), sem("s_gu")
        s_wo, s_xr = sem("s_wo"), [sem("s_xr0"), sem("s_xr1")]
        s_att, s_add1, s_stat2, s_agg2 = sem("s_att"), sem("s_add1"), sem("s_stat2"), sem("s_agg2")
        s_var2, s_rstd2, s_h2, s_x1b = sem("s_var2"), sem("s_rstd2"), sem("s_h2"), sem("s_x1b")
        s_h2t, s_h2tc = [sem("s_h2t0"), sem("s_h2t1")], [sem("s_h2tc0"), sem("s_h2tc1")]
        s_g, s_u, s_h2s = sem("s_g"), sem("s_u"), sem("s_h2s")
        s_s2 = sem("s_s2")
        s_xl = sem("s_xl")
        s_xe = sem("s_xe")
        s_xs, s_xn = sem("s_xs"), sem("s_xn")
        s_xt = sem("s_xt")
        s_xc = [sem(f"s_xc{n}") for n in range(3)]
        s_xu = sem("s_xu")
        s_x2 = sem("s_x2")
        s_agg3 = sem("s_agg3")
        s_stat3, s_mv3, s_var3, s_rstd3 = sem("s_stat3"), sem("s_mv3"), sem("s_var3"), sem("s_rstd3")
        s_we, s_cnt0 = sem("s_we"), sem("s_cnt0")
        s3_h, s3_l, s3_o, s3_c = sem("s3_h"), sem("s3_l"), sem("s3_o"), sem("s3_c")
        s3_t = sem("s3_t")
        s3_tc = sem("s3_tc")
        s3_r = sem("s3_r")
        s3_e = sem("s3_e")
        s3_w = sem("s3_w")
        s3_wt = sem("s3_wt")
        s3_wc = sem("s3_wc")
        s3_b = sem("s3_b")
        s3_y = sem("s3_y")
        s3_acc = sem("s3_acc")
        s3_out = sem("s3_out")

        block = ctx.enter_context(nc.Block())

        x_v = x.rearrange("(g s p) d -> g p s d", s=GT, p=P)

        def head_no(b, i, h):
            return b * (TPB * HEADS) + i * HEADS + h

        def head_uses(i):
            return PAIRS if i < 4 else HEADS

        def uses_before(i):
            return sum(head_uses(j) + 2 for j in range(i))

        def use(b, i, h, k):
            own = h // 2 if i < 4 else h
            return b * uses_before(TPB) + (GROUPS + uses_before(i) + own + 1)

        def use4(b, i, c, k):
            if i < 4:
                return b * uses_before(TPB) + c * 2 + (GROUPS + uses_before(i) + k // 2 + 1)
            return b * uses_before(TPB) + c * 4 + (GROUPS + uses_before(i) + k + 1)

        def use_values(b, i, g):
            return b * uses_before(TPB) + (GROUPS + uses_before(i) + head_uses(i) + g // 2 + 1)

        def banks_of(i, k):
            if i < 4:
                return [(k % 2, 0, i + 1)]
            return [(0, 0, 4), (1, 4, i + 1)]

        def score(k, K):
            at = S_BANK + 2 * (k % 2)
            return ps[:, at:at + 2, :].rearrange("p k n -> p (k n)")[:, 0:K]

        MCH = INNER // P
        units = []
        for what in "kv":
            units += [(what, m, min(m + 3, MCH)) for m in range(0, MCH, 3)]
        XKV = len(units)
        for kc in range(KC):
            units += [("g", kc, range(h, min(h + 6, XH), 2)) for h0 in range(0, XH, 6) for h in (h0, h0 + 1)]
        for b_ in range(BATCH):
            units += [("u", b_, range(h, min(h + 4, XH), 2)) for h0 in range(0, XH, 4) for h in (h0, h0 + 1)]
        XUNITS = len(units)
        CK = BATCH * NCTX

        def unit_copies(n):
            what = units[n]
            bank = ps[:, S_BANK + n % 4, :]
            if what[0] in "kv":
                _, m0, m1 = what
                dst = (xkT if what[0] == "k" else xvT)[:, m0:m1, :]
                return dst, bank[:, 0:(m1 - m0) * CK].rearrange("p (m k) -> p m k", k=CK), \
                    (-1.0 / XD ** 0.5 if what[0] == "k" else 1.0)
            if what[0] == "g":
                _, kc, hs = what
                dst = g_out[:, kc, :, :].rearrange("p b (h k) -> p h b k", k=NCTX)[:, hs[0]:hs[-1] + 1:2]
                return dst, bank[:, 0:len(hs) * CK].rearrange("p (h b k) -> p h b k", b=BATCH, k=NCTX), 1.0
            _, b_, hs = what
            return u_out[:, b_, hs[0]:hs[-1] + 1:2, :], ps[0:NCTX, S_BANK + n % 4, :].rearrange("p (h f) -> p h f", f=D), 1.0

        @block.sync
        def _(sp):
            sp.sem_inc(s_rw, 16)
            later = []
            for dst, src in ((idf[:, :], ident), (pk0[:, :], pek0),
                             (pev0[:, :], pev[0:1, :].broadcast_to([P, HD])),
                             (pk_in[:, :], pekT[:, 0:REL + 1]),
                             (pv_in[:, :, :], pev[1:REL + 1, :].rearrange("(c p) d -> p c d", p=P))):
                sp.dma_start(dst, src).then_inc(s_cst, 16)
            for dst, src, rows in ((xq_w, xwqT, P), (xo_w, xwo, P), (xk_w, xwk, CTXC), (xv_w, xwv, CTXC),
                                   (ctx_sb, ctxT, CTXC)):
                later.append((dst, src, rows))
            for g in range(2):
                sp.dma_start(xg[:, g], x_v[g]).then_inc(s_x[g], 16)
                if g == 0:
                    for dst, src in ((wq_sb, wqT), (wk_sb, wkT), (wv_sb, wvT)):
                        sp.dma_start(dst[:, :, :], src.rearrange("(c p) n -> p c n", p=P)).then_inc(s_w, 16)
            for dst, src, rows in later:
                sp.dma_start(dst[:, :, :], src.rearrange("(c p) n -> p c n", p=rows)).then_inc(s_xin, 16)
            sp.wait_ge(s_set, 2)
            rel_v = rel.ap().rearrange("s r u -> r s u")
            for sl in range(2 * HEADS):
                sp.dma_start(rel_v[:, sl, 0:P], zrow[:, :]).then_inc(s_pad, 16)
                sp.dma_start(rel_v[:, sl, P + REL:ROW], brow[:, :]).then_inc(s_pad, 16)
            sp.dma_start(pvrows[0:P, :], zrow[:, 0:HD]).then_inc(s_pvd, 16)
            sp.dma_start(pvrows[P + REL:ROW + 1, :], zrow[:, 0:HD]).then_inc(s_pvd, 16)
            sp.wait_ge(s_pv, 1)
            sp.dma_start(pvrows[P:P + REL, :].rearrange("(c p) d -> p c d", p=P), pv_in[:, :, :]).then_inc(s_pvd, 16)
            sp.wait_ge(s_pkp, 4)
            sp.dma_start(pparts.ap().rearrange("t d j -> d t j"), pk_parts[:, :, :]).then_inc(s_pkd, 16)
            for g in range(GROUPS):
                if g + 2 < GROUPS:
                    sp.wait_ge(s_h, g + 1)
                    sp.dma_start(xg[:, g % 2], x_v[g + 2]).then_inc(s_x[g % 2], 16)
                for j in range(4):
                    u = 4 * g + j
                    sp.wait_ge(s_lo, u + 1)
                    to = (qparts, kparts)[j // 2].ap()[:, (j % 2) * P:(j % 2 + 1) * P, g * BANK:(g + 1) * BANK]
                    sp.dma_start(to.rearrange("t p n -> p t n"), parts[:, u % 2]).then_inc(s_parts[u % 2], 16)
            for n in range(2):
                sp.wait_ge(s_xwc[n], (XUNITS + 1 - n) // 2)
            sp.dma_start(gmat.ap(), g_out[:, :, :, :]).then_inc(s_gu, 16)
            for b in range(BATCH):
                sp.dma_start(umat.ap()[b].rearrange("(h k) f -> k h f", k=NCTX), u_out[:, b, :, :]).then_inc(s_gu, 16)
            sp.wait_ge(s_gu, 48)
            for k in range(2):
                sp.wait_ge(s_parts[k], 16 * 8)
            sp.wait_ge(s_vc, TILES // 2)
            sp.wait_ge(s_pad, 16 * 4 * HEADS)
            sp.wait_ge(s_pvd, 48)
            sp.wait_ge(s_pkd, 16)
            for n, t in enumerate(K_SLOTS):
                sp.dma_start(p6[n * HD:(n + 1) * HD, :], pparts[t]).then_inc(s_tab, 16)
            for blk in range(3):
                sp.dma_start(pvt[:, blk, :], bass.AP(tensor=pvrows, offset=blk * P * HD, ap=[[HD, P], [1, P * HD]])
                             ).then_inc(s_tab, 16)
            sp.dma_start(diag_sb[:, :], diag).then_inc(s_tab, 16)
            sp.dma_start(fold_sb[:, :], fold).then_inc(s_tab, 16)

            def write_rel(b, i, c):
                quad = b * (TPB * QUADS) + (i * QUADS + c)
                sp.wait_ge(s_rc, 2 * quad + 3)
                sl = (i % 2) * HEADS + 4 * c
                sp.dma_start(rel.ap()[sl:sl + 4, :, P:P + REL].rearrange("s r u -> r s u"), rel_out[:, :, :]
                             ).then_inc(s_rw, 16)

            def read_bias(b, i, c):
                if i > 0:
                    sp.wait_ge(s_min, head_no(b, i - 1, 4 * c + 3) + 2)
                sl = (i % 2) * HEADS + 4 * c
                src = bass.AP(tensor=rel, offset=sl * (P * ROW) + 127, ap=[[ROW - 1, P], [P * ROW, 4], [1, BAND]])
                sp.dma_start(bias[:, 4 * c:4 * c + 4, :], src).then_inc(s_b, 16)

            def written(b, i, c):
                sp.wait_ge(s_rw, 16 * (b * (TPB * QUADS) + (i * QUADS + c)) + 32)

            def biased(b, i, c):
                sp.wait_ge(s_b, 16 * (b * (TPB * QUADS) + (i * QUADS + c)) + 16)

            with sp.Fori(0, BATCH) as b:
                sp.wait_ge(s_min, b * (TPB * HEADS) + 1)
                for n in range(len(Q_SLOTS)):
                    for dst, src, t in ((q6, qparts, Q_SLOTS[n]), (k6, kparts, K_SLOTS[n])):
                        src_v = src.ap()[t].rearrange("(h d) n -> d h n", d=HD)
                        sp.dma_start(dst[n * HD:(n + 1) * HD, :, :], src_v[:, :, bass.ds(b * SEQ, SEQ)]
                                     ).then_inc(s_qk, 16)
                for c in range(QUADS):
                    write_rel(b, 0, c)
                    written(b, 0, c)
                for c in range(2):
                    read_bias(b, 0, c)
                    biased(b, 0, c)
                for i in range(TPB):
                    for c in range(QUADS):
                        ahead = (i, c + 2) if c < 2 else (i + 1, c - 2)
                        if i + 1 < TPB:
                            write_rel(b, i + 1, c)
                        if ahead[0] < TPB:
                            read_bias(b, *ahead)
                            biased(b, *ahead)
                        if i + 1 < TPB:
                            written(b, i + 1, c)
                sp.sem_inc(s_go["sp"], 1)
            sp.wait_ge(s_on, TILES + 1)
            sp.dma_start(wo_sb[:, :, :], woT.rearrange("(c p) n -> p c n", p=P)).then_inc(s_wo, 16)
            sp.dma_start(bo[:, :], xbo.broadcast_to([P, D])).then_inc(s_wo, 16)
            for g in range(2):
                sp.dma_start(xr[:, g], x_v[g]).then_inc(s_xr[g], 16)
            sp.dma_start(g_sb[:, :, :, :], gmat.ap()).then_inc(s_g, 16)
            whole = XK // P
            for b in range(BATCH):
                sp.dma_start(u_sb[:, b, 0:whole, :], umat.ap()[b, 0:whole * P].rearrange("(c p) f -> p c f", p=P)
                             ).then_inc(s_u, 16)
                sp.dma_start(u_sb[0:XK - whole * P, b, whole, :], umat.ap()[b, whole * P:XK]).then_inc(s_u, 16)
            for g in range(2, GROUPS):
                sp.wait_ge(s_add1, g - 1)
                sp.dma_start(xr[:, g % 2], x_v[g]).then_inc(s_xr[g % 2], 16)
            sp.dma_start(we_sb[:, :, :].rearrange("p c (e f) -> p c e f", e=EXPERTS),
                         weT.rearrange("(c p) e f -> p c e f", p=P)).then_inc(s_we, 16)
            sp.dma_start(be_sb[:, :], be).then_inc(s_we, 16)
            sp.dma_start(wg_sb[:, :, :], wg.rearrange("(c p) e -> p c e", p=P)).then_inc(s_we, 16)
            sp.dma_start(earlier_sb[:, :], earlier).then_inc(s_we, 16)
            sp.dma_start(ones_sb[:, :], ones).then_inc(s_we, 16)
            sp.dma_start(e8[:, :], experts).then_inc(s_we, 16)
            out_v = out.rearrange("(t p) d -> p t d", p=P)
            with sp.Fori(0, TILES // 2) as j:
                sp.wait_ge(s3_acc, j * 18 + 27)
                sp.dma_start(out_v[:, bass.ds(2 * j, 2), :], x1[:, bass.ds(2 * j, 2), :]).then_inc(s_done, 16)
                sp.sem_inc(s_go["sp"], 1)
            sp.wait_ge(s_done, 16 * (TILES // 2))

        @block.gpsimd
        def _(pool):
            pool.sem_inc(s_cp, 2)
            pool.wait_ge(s_set, 1)
            for g in range(GROUPS):
                pool.wait_ge(s_agg, g + 1)
                nc.gpsimd.tensor_scalar(rstd1[:, :], mv1[:, :, 1], EPS, None, ALU.add).then_inc(s_var, 1)
                pool.wait_ge(s_var, g + 1)
                nc.gpsimd.tensor_tensor(rstd1[:, :], rstd1[:, :], half[:, 0:1].broadcast_to([P, GT]), ALU.pow
                                        ).then_inc(s_rstd, 1)
                for j in range(4):
                    u = 4 * g + j
                    pool.wait_ge(s_rest, u + 1)
                    nc.gpsimd.tensor_copy(parts[:, u % 2, 1, :], rest[:, u % 2, :]).then_inc(s_mid, 1)

            with pool.Fori(0, BATCH) as b:
                for i in range(TPB):
                    lo = max(0, i - 2)
                    pool.wait_ge(s_o, b * TPB + (i + 1))
                    pool.sem_inc(s_go["pool"], 1)
                    with pool.Fori(0, QUADS) as c:
                        for k in range(4):
                            for bank, _, _ in banks_of(i, k):
                                pool.wait_ge(s_tc[bank], use4(b, i, c, k))
                            nc.gpsimd.tensor_copy(bandT[:, lo + 2 - i:3, bass.ds(4 * c + k, 1), :],
                                                  pT[:, k % 2, lo:i + 1, :].unsqueeze(2)).then_inc(s_cp, 1)

            pool.wait_ge(s_wo, 32)
            for g in range(GROUPS):
                pool.wait_ge(s_agg2, g + 1)
                nc.gpsimd.tensor_scalar(rstd2[:, g % 2, :], mv2[:, g % 2, :, 1], EPS, None, ALU.add).then_inc(s_var2, 1)
                pool.wait_ge(s_var2, g + 1)
                nc.gpsimd.tensor_tensor(rstd2[:, g % 2, :], rstd2[:, g % 2, :], half[:, 0:1].broadcast_to([P, GT]),
                                        ALU.pow).then_inc(s_rstd2, 1)
                pool.wait_ge(s_h2, g + 1)
                nc.gpsimd.tensor_tensor(x1[:, GT * g:GT * (g + 1), :], x1[:, GT * g:GT * (g + 1), :],
                                        bo[:, :].unsqueeze(1).broadcast_to([P, GT, D]), ALU.add).then_inc(s_x1b, 1)
            for kc in range(KC):
                pool.wait_ge(s_h2tc[kc], GROUPS)
            with pool.Fori(0, TPB) as j:
                for u in range(2):
                    pool.wait_ge(s_s2, j * 6 + (3 * u + 3))
                    nc.gpsimd.tensor_copy(h2s[:, u, :, :], h2T[:, :, bass.ds(j * P + u * SEQ, P)]).then_inc(s_h2s, 1)
            pool.wait_ge(s_mv3, TILES)
            nc.gpsimd.tensor_scalar(rstd3[:, :], mv3[:, :, 1], EPS, None, ALU.add).then_inc(s_var3, 1)
            pool.wait_ge(s_var3, 1)
            nc.gpsimd.tensor_tensor(rstd3[:, :], rstd3[:, :], half[:, 0:1].broadcast_to([P, TILES]), ALU.pow
                                    ).then_inc(s_rstd3, 1)

        LAST_USE = GROUPS + BATCH * uses_before(TPB)

        @block.scalar
        def _(act):
            act.sem_inc(s_rc, 1)
            act.sem_inc(s_exp, 2)
            act.wait_ge(s_cst, 80)
            act.wait_ge(s_pk, 1)
            nc.scalar.copy(pk_parts[:, 0, :], pk_d[:, :]).then_inc(s_pkp, 1)
            act.wait_ge(s_pkp, 2)
            nc.scalar.copy(pk_parts[:, 1, :], pk_r[:, :]).then_inc(s_pkp, 1)
            for g in range(GROUPS):
                act.wait_ge(s_t[1], g + 1)
                if g >= 2:
                    act.wait_ge(s_v, 2 * (g - 1))
                nc.scalar.copy(hT[:, g % 2, 1, :], ps[:, T_BANK + 1, :]).then_inc(s_tc[1], 1)
                for j in range(4):
                    u = 4 * g + j
                    act.wait_ge(s_proj, u + 1)
                    if u >= 2:
                        act.wait_ge(s_lo, u - 1)
                        act.wait_ge(s_parts[u % 2], 16 * (u // 2))
                    if j < 2:
                        nc.scalar.activation(full[:, u % 2, :], ps[:, S_BANK + j, :], ACT.Copy, scale=-1.0 / SCALE
                                             ).then_inc(s_full, 1)
                    else:
                        nc.scalar.activation(full[:, u % 2, :], ps[:, S_BANK + j, :], ACT.Identity, bias=pk0[:, 0:1]
                                             ).then_inc(s_full, 1)
                    act.wait_ge(s_full, u + 1)
                    nc.scalar.copy(parts[:, u % 2, 0, :], full[:, u % 2, :]).then_inc(s_hi, 1)

            for n in range(0, XUNITS, 2):
                act.wait_ge(s_xw, n + 1)
                dst, src, scale = unit_copies(n)
                nc.scalar.activation(dst, src, ACT.Copy, scale=scale).then_inc(s_xwc[0], 1)

            def rel_copy(b, i, pair, pos):
                q = b * (TPB * PAIRS) + i * PAIRS + pair
                act.wait_ge(s_r, q + 1)
                if pos == 0:
                    act.wait_ge(s_rw, 8 * q + 16)
                nc.scalar.copy(rel_out[:, 2 * pos:2 * pos + 2, :].rearrange("p s j -> p (s j)"), ps[:, R_BANK, :]
                               ).then_inc(s_rc, 1)

            def softmax(b, i, c, k):
                act.wait_ge(s_min, head_no(b, i, 4 * c + k) + 2)
                if i < 4:
                    act.wait_ge(s_t[k % 2], use4(b, i, c, k) - 1)
                else:
                    act.wait_ge(s_t[1], use4(b, i, c, k) - 2)
                K = (i + 1) * P
                nc.scalar.activation(prob[:, k % 2, 0:K], score(k, K), ACT.Exp, bias=low[:, k % 2:k % 2 + 1],
                                     scale=-1.0, accum_out=rsum[:, i % 2, bass.ds(4 * c + k, 1)]).then_inc(s_exp, 1)

            def copy_t(b, i, c, k):
                for bank, k0, k1 in banks_of(i, k):
                    if bank == 1:
                        act.wait_ge(s_t[1], use4(b, i, c, k))
                        act.wait_ge(s_av, head_no(b, i, 4 * c + k) + 1)
                        act.wait_ge(s_cp, head_no(b, i, 4 * c + k) + 1)
                        nc.scalar.copy(pT[:, k % 2, k0:k1, :].rearrange("p k n -> p (k n)"),
                                       ps[:, T_BANK + 1, 0:(k1 - k0) * P]).then_inc(s_tc[1], 1)

            def quad(b, i, c, last):
                for k in range(4):
                    if k < 3:
                        softmax(b, i, c, k + 1)
                    elif not last:
                        softmax(b, i, c + 1, 0)
                    copy_t(b, i, c, k)
                    if k % 2 == 1 and i + 1 < TPB:
                        rel_copy(b, i + 1, 2 * c + k // 2, k // 2)

            with act.Fori(0, BATCH) as b:
                with act.Fori(0, QUADS) as c:
                    for pos in range(2):
                        rel_copy(b, 0, 2 * c + pos, pos)
                for i in range(TPB):
                    softmax(b, i, 0, 0)
                    with act.Fori(0, QUADS - 1) as c:
                        quad(b, i, c, False)
                    quad(b, i, QUADS - 1, True)

            act.wait_ge(s_on, TILES + 1)
            for g in range(GROUPS + 1):
                if g < GROUPS:
                    act.wait_ge(s_t[1], LAST_USE + g + 1)
                    if g >= 2:
                        act.wait_ge(s_att, g - 1)
                    nc.scalar.copy(oT[:, g % 2, 1, :], ps[:, T_BANK + 1, :]).then_inc(s_tc[1], 1)
                if g >= 1:
                    act.wait_ge(s_h2t[1], g)
                    nc.scalar.copy(h2T[:, 1, (g - 1) * BANK:g * BANK], ps[:, 1, :]).then_inc(s_h2tc[1], 1)

            act.sem_inc(s_xe, 3)
            act.sem_inc(s_xc[2], 1)

            def cross_exp(j, u):
                for n, (h0, h1) in enumerate(XBANKS):
                    act.wait_ge(s_xl, j * 6 + (3 * u + n + 1))
                    if n == 0:
                        act.wait_ge(s_xt, j * 6 + (3 * u + 3))
                    for h in range(h0, h1):
                        at = (h - h0) * NCTX
                        ins = nc.scalar.activation(xp[:, u, h * NCTX:(h + 1) * NCTX], ps[:, n, at:at + NCTX], ACT.Exp,
                                                   bias=xlow[:, u, h:h + 1], scale=-1.0, accum_out=xsum[:, u, h:h + 1])
                    ins.then_inc(s_xe, 1)

            def cross_step(j, u, following):
                act.wait_ge(s_xt, j * 6 + (3 * u + 9))
                act.wait_ge(s_xu, j * 2 + (u + 1))
                nc.scalar.copy(xpT[:, u, XCH - 2, :], ps[:, 5, 0:P])
                nc.scalar.copy(xpT[0:XTAIL, u, XCH - 1, :], ps[0:XTAIL, 5, P:2 * P]).then_inc(s_xc[2], 1)
                if following is not None:
                    cross_exp(*following)

            cross_exp(0, 0)
            with act.Fori(0, TPB - 1) as j:
                cross_step(j, 0, (j, 1))
                cross_step(j, 1, (j + 1, 0))
            cross_step(TPB - 1, 0, (TPB - 1, 1))
            cross_step(TPB - 1, 1, None)

            act.sem_inc(s3_tc, 1)
            act.sem_inc(s3_wc, 1)

            def route(j, v):
                act.wait_ge(s3_t, j + 2)
                act.wait_ge(s3_y, j * 8 + 8)
                nc.scalar.copy(h3T[:, v, :], ps[:, 4, :]).then_inc(s3_tc, 1)
                act.wait_ge(s3_r, j * RSTEPS + 2)
                nc.scalar.activation(expb[:, :, :], below[:, :, :], ACT.Exp).then_inc(s3_e, 1)
                act.wait_ge(s3_wt, j + 1)
                nc.scalar.copy(wgtT[:, v, :], ps[0:EXPERTS, 6, 0:2 * P]).then_inc(s3_wc, 1)

            route(0, 0)
            with act.Fori(0, TILES // 4 - 1) as jj:
                route(2 * jj + 1, 1)
                route(2 * jj + 2, 0)
            route(TILES // 2 - 1, 1)

        @block.vector
        def _(dve):
            dve.sem_inc(s_min, 1)
            dve.sem_inc(s_on, 1)
            nc.vector.memset(half[:, :], -0.5).then_inc(s_set, 1)
            nc.vector.memset(zrow[:, :], 0.0)
            nc.vector.memset(brow[:, :], BIG).then_inc(s_set, 1)
            dve.wait_ge(s_cst, 80)
            nc.vector.tensor_scalar(pk_d[:, :], pk_in[:, 1:REL + 1], pk_in[:, 0:1], None, ALU.subtract
                                    ).then_inc(s_pk, 1)
            nc.vector.tensor_tensor(pv_in[:, :, :], pv_in[:, :, :], pev0[:, :].unsqueeze(1).broadcast_to([P, 2, HD]),
                                    ALU.subtract).then_inc(s_pv, 1)
            dve.wait_ge(s_pkp, 1)
            nc.vector.tensor_tensor(pk_r[:, :], pk_d[:, :], pk_parts[:, 0, :], ALU.subtract).then_inc(s_pkp, 1)
            dve.wait_ge(s_pkp, 3)
            nc.vector.tensor_tensor(pk_parts[:, 2, :], pk_r[:, :], pk_parts[:, 1, :], ALU.subtract).then_inc(s_pkp, 1)
            for g in range(GROUPS):
                dve.wait_ge(s_x[g % 2], 16 * (g // 2 + 1))
                for s in range(GT):
                    nc.vector.bn_stats(st1[:, s, :], xg[:, g % 2, s, :]).then_inc(s_stat, 1)
                dve.wait_ge(s_stat, GT * (g + 1))
                for s in range(GT):
                    ins = nc.vector.bn_aggr(mv1[:, s, :], st1[:, s, :])
                ins.then_inc(s_agg, 1)
                dve.wait_ge(s_rstd, g + 1)
                if g >= 1:
                    dve.wait_ge(s_t[1], g)
                for s in range(GT):
                    ins = nc.vector.tensor_scalar(hg[:, s, :], xg[:, g % 2, s, :], mv1[:, s, 0:1], rstd1[:, s:s + 1],
                                                  ALU.subtract, ALU.mult)
                ins.then_inc(s_h, 1)
                dve.wait_ge(s_t[0], g + 1)
                if g >= 2:
                    dve.wait_ge(s_v, 2 * (g - 1))
                nc.vector.tensor_copy(hT[:, g % 2, 0, :], ps[:, T_BANK, :]).then_inc(s_tc[0], 1)
                for j in range(4):
                    u = 4 * g + j
                    dve.wait_ge(s_hi, u + 1)
                    nc.vector.tensor_tensor(rest[:, u % 2, :], full[:, u % 2, :], parts[:, u % 2, 0, :], ALU.subtract
                                            ).then_inc(s_rest, 1)
                    dve.wait_ge(s_mid, u + 1)
                    nc.vector.tensor_tensor(parts[:, u % 2, 2, :], rest[:, u % 2, :], parts[:, u % 2, 1, :],
                                            ALU.subtract).then_inc(s_lo, 1)
                for half_g in range(2):
                    dve.wait_ge(s_v, 2 * g + half_g + 1)
                    t = GT * g + 2 * half_g
                    nc.vector.tensor_tensor(v_sb[:, t:t + 2, :].rearrange("p t (h d) -> p (t h) d", d=HD),
                                            ps[:, R_BANK + half_g, :].rearrange("p (a d) -> p a d", d=HD),
                                            pev0[:, :].unsqueeze(1).broadcast_to([P, 2 * HEADS, HD]), ALU.add
                                            ).then_inc(s_vc, 1)
            for n in range(1, XUNITS, 2):
                dve.wait_ge(s_xw, n + 1)
                dst, src, scale = unit_copies(n)
                nc.vector.tensor_scalar(dst, src, scale, None, ALU.mult).then_inc(s_xwc[1], 1)
            dve.wait_ge(s_gu, 48)
            for k in range(2):
                dve.wait_ge(s_parts[k], 16 * 8)
            dve.wait_ge(s_pvd, 48)
            dve.wait_ge(s_pad, 16 * 4 * HEADS)
            dve.wait_ge(s_pkd, 16)
            nc.vector.memset(zb[:, :], 0.0).then_inc(s_z, 1)
            dve.wait_ge(s_tab, 16 * 11)

            def minimum(b, i, c, k, last):
                n = head_no(b, i, 4 * c + k)
                w0 = max(0, i - 2) * P
                K = (i + 1) * P
                dve.wait_ge(s_s, n + 1)
                dve.wait_ge(s_b, b * (16 * TPB * QUADS) + (c * 16 + (16 * i * QUADS + 16)))
                dve.wait_ge(s_exp, n + 1)
                first = BIG
                if i > 2:
                    nc.vector.tensor_reduce(far[:, k % 2:k % 2 + 1], score(k, K)[:, 0:w0], AX.X, ALU.min
                                            ).then_inc(s_far, 1)
                    dve.wait_ge(s_far, b * ((TPB - 3) * HEADS) + (4 * c + ((i - 3) * HEADS + k + 1)))
                    first = far[:, k % 2:k % 2 + 1]
                dve.sem_inc(s_go["dve"], 1)
                s = score(k, K)[:, w0:K]
                nc.vector.tensor_tensor_reduce(s, s, bias[:, 4 * c + k, BAND - (K - w0):BAND], 1.0, first,
                                               ALU.add, ALU.min, low[:, k % 2:k % 2 + 1]).then_inc(s_min, 1)

            def copy_t(b, i, c, k):
                for bank, k0, k1 in banks_of(i, k):
                    if bank == 0:
                        dve.wait_ge(s_t[0], use4(b, i, c, k))
                        dve.wait_ge(s_av, head_no(b, i, 4 * c + k) + 1)
                        dve.wait_ge(s_cp, head_no(b, i, 4 * c + k) + 1)
                        nc.vector.tensor_copy(pT[:, k % 2, k0:k1, :].rearrange("p k n -> p (k n)"),
                                              ps[:, T_BANK, 0:(k1 - k0) * P]).then_inc(s_tc[0], 1)

            def quad(b, i, c, last):
                for k in range(4):
                    if k < 3:
                        minimum(b, i, c, k + 1, last)
                    elif not last:
                        minimum(b, i, c + 1, 0, last)
                    copy_t(b, i, c, k)

            def finish(b, i):
                for g in range(4):
                    dve.wait_ge(s_t[g % 2], use_values(b, i, g))
                    dve.wait_ge(s_o, b * TPB + (i + 1))
                    nc.vector.tensor_tensor(
                        picked[:, :, 32 * g:32 * g + 32].rearrange("p h (a q) -> p a h q", q=8),
                        ps[:, T_BANK + g % 2, :].rearrange("p (a h q) -> p a h q", a=4, q=8),
                        diag_sb[:, :].rearrange("p (h q) -> p h q", q=8).unsqueeze(1).broadcast_to([P, 4, HEADS, 8]),
                        ALU.mult).then_inc(s_tc[g % 2], 1)
                nc.vector.reciprocal(rrec[:, :], rsum[:, i % 2, :]).then_inc(s_rr, 1)
                dve.wait_ge(s_rr, b * TPB + (i + 1))
                dve.wait_ge(s_o, b * TPB + (i + 2))
                nc.vector.tensor_tensor(
                    x1[:, bass.ds(b * TPB + i, 1), :].rearrange("p o (h d) -> p (o h) d", d=HD),
                    ps[:, O_BANK, 0:D].rearrange("p (h d) -> p h d", d=HD),
                    rrec[:, :].unsqueeze(2).broadcast_to([P, HEADS, HD]), ALU.mult).then_inc(s_on, 1)

            with dve.Fori(0, BATCH) as b:
                minimum(b, 0, 0, 0, False)
                for i in range(TPB):
                    for c in range(QUADS):
                        quad(b, i, c, c == QUADS - 1)
                    if i + 1 < TPB:
                        minimum(b, i + 1, 0, 0, False)
                    finish(b, i)

            dve.wait_ge(s_on, TILES + 1)
            for g in range(GROUPS + 1):
                if g < GROUPS:
                    dve.wait_ge(s_t[0], LAST_USE + g + 1)
                    if g >= 2:
                        dve.wait_ge(s_att, g - 1)
                    nc.vector.tensor_copy(oT[:, g % 2, 0, :], ps[:, T_BANK, :]).then_inc(s_tc[0], 1)
                if g >= 1:
                    dve.wait_ge(s_h2t[0], g)
                    nc.vector.tensor_copy(h2T[:, 0, (g - 1) * BANK:g * BANK], ps[:, 0, :]).then_inc(s_h2tc[0], 1)
                if g == GROUPS:
                    break
                dve.wait_ge(s_att, g + 1)
                dve.wait_ge(s_xr[g % 2], 16 * (g // 2 + 1))
                for k in range(2):
                    t = GT * g + 2 * k
                    ins = nc.vector.tensor_tensor(x1[:, t:t + 2, :].rearrange("p t d -> p (t d)"), ps[:, 6 + k, :],
                                                  xr[:, g % 2, 2 * k:2 * k + 2, :].rearrange("p t d -> p (t d)"),
                                                  ALU.add)
                ins.then_inc(s_add1, 1)
                dve.wait_ge(s_add1, g + 1)
                for s in range(GT):
                    nc.vector.bn_stats(st2[:, s, :], x1[:, GT * g + s, :]).then_inc(s_stat2, 1)
                dve.wait_ge(s_stat2, GT * (g + 1))
                for s in range(GT):
                    ins = nc.vector.bn_aggr(mv2[:, g % 2, s, :], st2[:, s, :])
                ins.then_inc(s_agg2, 1)
                dve.wait_ge(s_rstd2, g + 1)
                if g >= 2:
                    dve.wait_ge(s_h2t[1], g - 1)
                for s in range(GT):
                    ins = nc.vector.tensor_scalar(h2[:, g % 2, s, :], x1[:, GT * g + s, :], mv2[:, g % 2, s, 0:1],
                                                  rstd2[:, g % 2, s:s + 1], ALU.subtract, ALU.mult)
                ins.then_inc(s_h2, 1)

            dve.sem_inc(s_xc[0], 1)
            dve.sem_inc(s_xc[1], 1)
            dve.sem_inc(s_x2, 2)

            def cross_low(j, u):
                for n, (h0, h1) in enumerate(XBANKS):
                    dve.wait_ge(s_s2, j * 6 + (3 * u + n + 7))
                    nc.vector.tensor_reduce(xlow[:, u, h0:h1],
                                            ps[:, n, 0:(h1 - h0) * NCTX].rearrange("p (h k) -> p h k", k=NCTX),
                                            AX.X, ALU.min).then_inc(s_xl, 1)

            def cross_step(j, u, following):
                dve.wait_ge(s_xe, j * 6 + (3 * u + 6))
                nc.vector.reciprocal(xrec[:, :], xsum[:, u, :]).then_inc(s_xs, 1)
                dve.wait_ge(s_xs, j * 2 + (u + 1))
                p3 = xp[:, u, :].rearrange("p (h k) -> p h k", k=NCTX)
                nc.vector.tensor_tensor(p3, p3, xrec[:, :].unsqueeze(2).broadcast_to([P, XH, NCTX]), ALU.mult
                                        ).then_inc(s_xn, 1)
                for n in range(2):
                    dve.wait_ge(s_xt, j * 6 + (3 * u + n + 7))
                    dve.wait_ge(s_xu, j * 2 + (u + 1))
                    nc.vector.tensor_copy(xpT[:, u, 4 * n:4 * n + 4, :].rearrange("p c n -> p (c n)"), ps[:, 3 + n, :]
                                          ).then_inc(s_xc[n], 1)
                if following is not None:
                    cross_low(*following)
                dve.wait_ge(s_xu, j * 2 + (u + 3))
                xt = x1[:, bass.ds(j + TPB * u, 1), :].rearrange("p o d -> p (o d)")
                nc.vector.tensor_tensor(xt, ps[:, 6 + u, 0:D], xt, ALU.add).then_inc(s_x2, 1)
                dve.wait_ge(s_x2, j * 2 + (u + 3))
                nc.vector.bn_stats(st3[:, :], xt).then_inc(s_stat3, 1)
                dve.wait_ge(s_stat3, j * 2 + (u + 1))
                dve.sem_inc(s_go["dve"], 1)
                nc.vector.bn_aggr(mvs[:, :], st3[:, :]).then_inc(s_agg3, 1)
                dve.wait_ge(s_agg3, j * 2 + (u + 1))
                nc.vector.tensor_copy(mv3[:, bass.ds(j + TPB * u, 1), :].rearrange("p o d -> p (o d)"), mvs[:, :]
                                      ).then_inc(s_mv3, 1)

            dve.wait_ge(s_x1b, GROUPS)
            cross_low(0, 0)
            with dve.Fori(0, TPB - 1) as j:
                cross_step(j, 0, (j, 1))
                cross_step(j, 1, (j + 1, 0))
            cross_step(TPB - 1, 0, (TPB - 1, 1))
            cross_step(TPB - 1, 1, None)

            dve.sem_inc(s3_w, 1)
            dve.sem_inc(s3_acc, 9)
            nc.vector.memset(count[:, :], 0.0).then_inc(s_cnt0, 1)
            dve.wait_ge(s_cnt0, 1)
            dve.wait_ge(s_we, 16 * 6)
            dve.wait_ge(s_rstd3, 1)

            def rows(j, v):
                dve.wait_ge(s3_t, j + 1)
                for u in range(2):
                    t = 2 * j + u
                    ins = nc.vector.tensor_scalar(h3[:, v, u, :],
                                                  x1[:, bass.ds(t, 1), :].rearrange("p o d -> p (o d)"),
                                                  mv3[:, bass.ds(t, 1), 0:1].rearrange("p o d -> p (o d)"),
                                                  rstd3[:, bass.ds(t, 1)], ALU.subtract, ALU.mult)
                ins.then_inc(s3_h, 1)

            def choose(j, v):
                step = [0]

                def link(ins):
                    step[0] += 1
                    ins.then_inc(s3_r, 1)
                    dve.wait_ge(s3_r, j * RSTEPS + step[0])

                lg = ps[:, 5, 0:2 * EXPERTS].rearrange("p (u e) -> p u e", e=EXPERTS)
                e_row = e8[:, :].unsqueeze(1).broadcast_to([P, 2, EXPERTS])
                dve.wait_ge(s3_l, j + 1)
                link(nc.vector.tensor_reduce(top[:, :], lg, AX.X, ALU.max))
                link(nc.vector.tensor_tensor(below[:, :, :], lg, top[:, :].unsqueeze(2).broadcast_to([P, 2, EXPERTS]),
                                             ALU.subtract))
                link(nc.vector.scalar_tensor_tensor(out=cand[:, :, :], in0=below[:, :, :], scalar=0.0, in1=e_row,
                                                    op0=ALU.is_ge, op1=ALU.mult))
                link(nc.vector.tensor_reduce(first_e[:, :], cand[:, :, :], AX.X, ALU.min))
                nc.vector.tensor_tensor(chosen[:, v, :, :], e_row,
                                        first_e[:, :].unsqueeze(2).broadcast_to([P, 2, EXPERTS]), ALU.is_equal
                                        ).then_inc(s3_o, 1)
                dve.wait_ge(s3_e, j + 1)
                link(nc.vector.tensor_reduce(den[:, :], expb[:, :, :], AX.X, ALU.add))
                link(nc.vector.reciprocal(gate[:, :], den[:, :]))
                dve.wait_ge(s3_o, j + 1)

            def weigh(j, v):
                step = [6]

                def link(ins):
                    step[0] += 1
                    ins.then_inc(s3_r, 1)
                    dve.wait_ge(s3_r, j * RSTEPS + step[0])

                dve.wait_ge(s3_c, j + 1)
                at = ps[:, 5, 16:16 + 2 * EXPERTS].rearrange("p (u e) -> p u e", e=EXPERTS)
                link(nc.vector.tensor_tensor(place[:, :, :], at, count[:, :].unsqueeze(1).broadcast_to([P, 2, EXPERTS]),
                                             ALU.add))
                link(nc.vector.tensor_tensor(count[:, :], ps[:, 5, 32:32 + EXPERTS], count[:, :], ALU.add))
                link(nc.vector.scalar_tensor_tensor(out=kept[:, :, :], in0=place[:, :, :], scalar=float(CAP),
                                                    in1=chosen[:, v, :, :], op0=ALU.is_lt, op1=ALU.mult))
                link(nc.vector.tensor_tensor(expw[:, :, :], kept[:, :, :],
                                             gate[:, :].unsqueeze(2).broadcast_to([P, 2, EXPERTS]), ALU.mult))
                nc.vector.tensor_copy(wgt[:, v, :, :], expw[:, :, :]).then_inc(s3_w, 1)
                dve.wait_ge(s3_w, j + 2)

            def add_bias(j, u):
                dve.wait_ge(s3_b, j + 1)
                xt = x1[:, bass.ds(2 * j + u, 1), :].rearrange("p o d -> p (o d)")
                nc.vector.tensor_tensor(xt, ps[:, 7, u * D:(u + 1) * D], xt, ALU.add).then_inc(s3_acc, 1)
                dve.wait_ge(s3_acc, j * 18 + (9 * u + 10))

            def add_experts(j, v, u, q):
                dve.wait_ge(s3_y, j * 8 + (4 * u + q + 17))
                xt = x1[:, bass.ds(2 * j + u, 1), :].rearrange("p o d -> p (o d)")
                for e in range(2):
                    nc.vector.scalar_tensor_tensor(out=xt, in0=ps[:, q, e * D:(e + 1) * D],
                                                   scalar=wgt[:, v, u, 2 * q + e:2 * q + e + 1], in1=xt,
                                                   op0=ALU.mult, op1=ALU.add).then_inc(s3_acc, 1)
                    dve.wait_ge(s3_acc, j * 18 + (9 * u + 2 * q + e + 11))

            def experts_step(j, v, last):
                if not last:
                    rows(j + 1, 1 - v)
                add_bias(j, 0)
                for q in range(4):
                    add_experts(j, v, 0, q)
                add_bias(j, 1)
                add_experts(j, v, 1, 0)
                if not last:
                    choose(j + 1, 1 - v)
                add_experts(j, v, 1, 1)
                add_experts(j, v, 1, 2)
                if not last:
                    weigh(j + 1, 1 - v)
                add_experts(j, v, 1, 3)

            rows(0, 0)
            choose(0, 0)
            weigh(0, 0)
            with dve.Fori(0, TILES // 4 - 1) as jj:
                experts_step(2 * jj, 0, False)
                experts_step(2 * jj + 1, 1, False)
            experts_step(TILES // 2 - 2, 0, False)
            experts_step(TILES // 2 - 1, 1, True)

        @block.tensor
        def _(pe):
            pe.sem_inc(s_av, 2)
            pe.sem_inc(s_o, 1)
            pe.wait_ge(s_cst, 80)
            pe.wait_ge(s_w, 48)
            for g in range(GROUPS):
                pe.wait_ge(s_h, g + 1)
                for kc in range(KC):
                    if g >= 1:
                        pe.wait_ge(s_tc[kc], g)
                    for s in range(GT):
                        mm = pe.transpose(ps[:, T_BANK + kc, s * P:(s + 1) * P], hg[:, s, kc * P:(kc + 1) * P],
                                          idf[:, :])
                    mm.then_inc(s_t[kc], 1)
                for kc in range(KC):
                    pe.wait_ge(s_tc[kc], g + 1)
                for j in range(4):
                    if g >= 1:
                        pe.wait_ge(s_full, 4 * (g - 1) + j + 1)
                    w = (wq_sb, wk_sb)[j // 2]
                    for kc in range(KC):
                        mm = pe.matmul(ps[:, S_BANK + j, :], w[:, kc, (j % 2) * P:(j % 2 + 1) * P],
                                       hT[:, g % 2, kc, :], start=(kc == 0), stop=(kc == KC - 1))
                    mm.then_inc(s_proj, 1)
                for half_g in range(2):
                    if g >= 1:
                        pe.wait_ge(s_vc, 2 * (g - 1) + half_g + 1)
                    for s in range(2):
                        for kc in range(KC):
                            mm = pe.matmul(ps[:, R_BANK + half_g, s * D:(s + 1) * D],
                                           hT[:, g % 2, kc, (2 * half_g + s) * P:(2 * half_g + s + 1) * P],
                                           wv_sb[:, kc, :], start=(kc == 0), stop=(kc == KC - 1))
                    mm.then_inc(s_v, 1)
            pe.wait_ge(s_full, 4 * GROUPS)
            pe.wait_ge(s_vc, 2 * GROUPS)
            pe.wait_ge(s_xin, 16 * 5)
            for n, what in enumerate(units):
                if n >= 4:
                    pe.wait_ge(s_xwc[n % 2], (n - 4) // 2 + 1)
                if n == XKV:
                    for k in range(2):
                        pe.wait_ge(s_xwc[k], (XKV + 1 - k) // 2)
                bank = S_BANK + n % 4
                if what[0] in "kv":
                    w = xk_w if what[0] == "k" else xv_w
                    for m in range(what[1], what[2]):
                        at = (m - what[1]) * CK
                        for kc in range(2):
                            mm = pe.matmul(ps[:, bank, at:at + CK], w[:, kc, m * P:(m + 1) * P], ctx_sb[:, kc, :],
                                           start=(kc == 0), stop=(kc == 1))
                elif what[0] == "g":
                    _, kc, hs = what
                    for at, h in enumerate(hs):
                        rows = slice(XD * (h % 2), XD * (h % 2) + XD)
                        mm = pe.matmul(ps[:, bank, at * CK:(at + 1) * CK],
                                       xq_w[rows, h // 2, kc * P:(kc + 1) * P], xkT[rows, h // 2, :],
                                       start=True, stop=True)
                else:
                    _, b_, hs = what
                    for at, h in enumerate(hs):
                        rows = slice(XD * (h % 2), XD * (h % 2) + XD)
                        mm = pe.matmul(ps[0:NCTX, bank, at * D:(at + 1) * D],
                                       xvT[rows, h // 2, b_ * NCTX:(b_ + 1) * NCTX], xo_w[rows, h // 2, :],
                                       start=True, stop=True)
                mm.then_inc(s_xw, 1)
            for k in range(2):
                pe.wait_ge(s_xwc[k], (XUNITS + 1 - k) // 2)
            pe.wait_ge(s_z, 1)
            pe.wait_ge(s_tab, 16 * 11)

            def rel_scores(b, i, pair):
                pe.wait_ge(s_rc, b * (TPB * PAIRS) + i * PAIRS + pair + 1)
                for s in range(2):
                    mm = pe.matmul(ps[:, R_BANK, s * REL:(s + 1) * REL],
                                   q6[:, bass.ds(2 * pair + s, 1), i * P:(i + 1) * P].rearrange("p o n -> p (o n)"),
                                   p6[:, :], start=True, stop=True)
                mm.then_inc(s_r, 1)

            def scores(b, i, c, k):
                pe.wait_ge(s_exp, head_no(b, i, 4 * c + k) + 1)
                K = (i + 1) * P
                for n0 in range(0, K, BANK):
                    n1 = min(K, n0 + BANK)
                    mm = pe.matmul(score(k, K)[:, n0:n1],
                                   q6[:, bass.ds(4 * c + k, 1), i * P:(i + 1) * P].rearrange("p o n -> p (o n)"),
                                   k6[:, bass.ds(4 * c + k, 1), n0:n1].rearrange("p o n -> p (o n)"), start=True, stop=True)
                mm.then_inc(s_s, 1)

            def transposes(b, i, c, k):
                pe.wait_ge(s_exp, head_no(b, i, 4 * c + k) + 3)
                for bank, k0, k1 in banks_of(i, k):
                    pe.wait_ge(s_tc[bank], use4(b, i, c, k) - 1)
                    for kb in range(k0, k1):
                        mm = pe.transpose(ps[:, T_BANK + bank, (kb - k0) * P:(kb - k0 + 1) * P],
                                          prob[:, k % 2, kb * P:(kb + 1) * P], idf[:, :])
                    mm.then_inc(s_t[bank], 1)

            def zero_out(b, i):
                pe.wait_ge(s_on, b * TPB + (i + 1))
                pe.matmul(ps[:, O_BANK, 0:D], zb[:, 0:P], zb[:, :], start=True, stop=False, skip_group_check=True)

            def values(b, i, c, k):
                for bank, _, _ in banks_of(i, k):
                    pe.wait_ge(s_tc[bank], use4(b, i, c, k))
                for kb in range(i + 1):
                    mm = pe.matmul(ps[:, O_BANK, bass.ds((4 * c + k) * HD, HD)], pT[:, k % 2, kb, :],
                                   v_sb[:, bass.ds(b * TPB + kb, 1), bass.ds((4 * c + k) * HD, HD)].rearrange("p o n -> p (o n)"),
                                   start=False, stop=False, skip_group_check=True)
                mm.then_inc(s_av, 1)

            def rel_values(b, i):
                pe.wait_ge(s_cp, head_no(b, i, HEADS - 1) + 3)
                first = max(0, 2 - i)
                for g in range(4):
                    pe.wait_ge(s_tc[g % 2], use_values(b, i, g) - 1)
                    for a in range(4):
                        q = 8 * (4 * g + a)
                        for blk in range(first, 3):
                            mm = pe.matmul(ps[:, T_BANK + g % 2, a * P:(a + 1) * P].rearrange("p (h q) -> p h q", q=8),
                                           pvt[:, blk, (P - 8 - q) * HD:(P - q) * HD], bandT[:, blk, :, q:q + 8],
                                           start=(blk == first), stop=(blk == 2))
                    mm.then_inc(s_t[g % 2], 1)

            def fold_values(b, i):
                for g in range(2, 4):
                    pe.wait_ge(s_tc[g % 2], use_values(b, i, g))
                for h in range(HEADS):
                    mm = pe.matmul(ps[:, O_BANK, h * HD:(h + 1) * HD], picked[:, h, :], fold_sb[:, :],
                                   start=False, stop=(h == HEADS - 1), skip_group_check=True)
                mm.then_inc(s_o, 1)

            def quad(b, i, c, first, last):
                for k in range(4):
                    if k < 3:
                        scores(b, i, c, k + 1)
                    elif not last:
                        scores(b, i, c + 1, 0)
                    transposes(b, i, c, k)
                    if k % 2 == 1 and i + 1 < TPB:
                        rel_scores(b, i + 1, 2 * c + k // 2)
                    if k > 0:
                        values(b, i, c, k - 1)
                    elif not first:
                        values(b, i, c - 1, 3)
                    else:
                        zero_out(b, i)

            with pe.Fori(0, BATCH) as b:
                pe.wait_ge(s_qk, b * (16 * 2 * len(Q_SLOTS)) + 16 * 2 * len(Q_SLOTS))
                pe.sem_inc(s_go["pe"], 1)
                with pe.Fori(0, PAIRS) as pair:
                    rel_scores(b, 0, pair)
                scores(b, 0, 0, 0)
                for i in range(TPB):
                    quad(b, i, 0, True, False)
                    with pe.Fori(1, QUADS - 1) as c:
                        quad(b, i, c, False, False)
                    quad(b, i, QUADS - 1, False, True)
                    values(b, i, QUADS - 1, 3)
                    if i + 1 < TPB:
                        scores(b, i + 1, 0, 0)
                    rel_values(b, i)
                    fold_values(b, i)

            pe.wait_ge(s_on, TILES + 1)
            pe.wait_ge(s_wo, 32)
            for g in range(GROUPS + 1):
                if g < GROUPS:
                    for kc in range(KC):
                        pe.wait_ge(s_tc[kc], LAST_USE + g)
                        for s in range(GT):
                            mm = pe.transpose(ps[:, T_BANK + kc, s * P:(s + 1) * P],
                                              x1[:, GT * g + s, kc * P:(kc + 1) * P], idf[:, :])
                        mm.then_inc(s_t[kc], 1)
                    for kc in range(KC):
                        pe.wait_ge(s_tc[kc], LAST_USE + g + 1)
                    if g >= 1:
                        pe.wait_ge(s_add1, g)
                    for s in range(GT):
                        for kc in range(KC):
                            mm = pe.matmul(ps[:, 6 + s // 2, (s % 2) * D:(s % 2 + 1) * D],
                                           oT[:, g % 2, kc, s * P:(s + 1) * P], wo_sb[:, kc, :],
                                           start=(kc == 0), stop=(kc == KC - 1))
                    mm.then_inc(s_att, 1)
                if g >= 1:
                    pe.wait_ge(s_h2, g)
                    for kc in range(KC):
                        if g >= 2:
                            pe.wait_ge(s_h2tc[kc], g - 1)
                        for s in range(GT):
                            mm = pe.transpose(ps[:, kc, s * P:(s + 1) * P], h2[:, (g - 1) % 2, s, kc * P:(kc + 1) * P],
                                              idf[:, :])
                        mm.then_inc(s_h2t[kc], 1)
            for kc in range(KC):
                pe.wait_ge(s_h2tc[kc], GROUPS)

            pe.sem_inc(s_s2, 6)
            pe.sem_inc(s_xt, 6)
            pe.sem_inc(s_xu, 2)
            pe.wait_ge(s_g, 16)
            pe.wait_ge(s_u, 64)

            def cross_scores(j, u):
                pe.wait_ge(s_h2s, j * 2 + (u + 1))
                for n, (h0, h1) in enumerate(XBANKS):
                    pe.wait_ge(s_xe, j * 6 + (3 * u + n + 1))
                    for kc in range(KC):
                        mm = pe.matmul(ps[:, n, 0:(h1 - h0) * NCTX], h2s[:, u, kc, :],
                                       g_sb[:, kc, u, h0 * NCTX:h1 * NCTX], start=(kc == 0), stop=(kc == KC - 1))
                    mm.then_inc(s_s2, 1)

            def cross_step(j, u, following):
                pe.wait_ge(s_xn, j * 2 + (u + 1))
                for n in range(3):
                    pe.wait_ge(s_xc[n], j * 2 + (u + 1))
                    for c in range(4 * n, min(4 * n + 4, XCH)):
                        w = P if c < XCH - 1 else XTAIL
                        mm = pe.transpose(ps[0:w, 3 + n, (c - 4 * n) * P:(c - 4 * n + 1) * P],
                                          xp[:, u, c * P:c * P + w], idf[:, :])
                    mm.then_inc(s_xt, 1)
                if following is not None:
                    cross_scores(*following)
                for n in range(3):
                    pe.wait_ge(s_xc[n], j * 2 + (u + 2))
                pe.wait_ge(s_x2, j * 2 + (u + 1))
                for c in range(XCH):
                    w = P if c < XCH - 1 else XTAIL
                    mm = pe.matmul(ps[:, 6 + u, 0:D], xpT[0:w, u, c, :], u_sb[0:w, u, c, :],
                                   start=(c == 0), stop=(c == XCH - 1))
                mm.then_inc(s_xu, 1)

            cross_scores(0, 0)
            with pe.Fori(0, TPB - 1) as j:
                cross_step(j, 0, (j, 1))
                cross_step(j, 1, (j + 1, 0))
            cross_step(TPB - 1, 0, (TPB - 1, 1))
            cross_step(TPB - 1, 1, None)

            pe.sem_inc(s3_t, 1)
            pe.sem_inc(s3_y, 16)
            pe.wait_ge(s_we, 16 * 6)
            pe.wait_ge(s_x2, TILES + 2)

            def turn_rows(j, v):
                pe.wait_ge(s3_h, j + 1)
                pe.wait_ge(s3_tc, j + 1)
                for kc in range(KC):
                    for u in range(2):
                        at = (2 * kc + u) * P
                        mm = pe.transpose(ps[:, 4, at:at + P], h3[:, v, u, kc * P:(kc + 1) * P], idf[:, :])
                mm.then_inc(s3_t, 1)

            def logits(j, v):
                pe.wait_ge(s3_tc, j + 2)
                pe.wait_ge(s3_w, j + 1)
                for u in range(2):
                    for kc in range(KC):
                        at = (2 * kc + u) * P
                        mm = pe.matmul(ps[:, 5, u * EXPERTS:(u + 1) * EXPERTS], h3T[:, v, at:at + P], wg_sb[:, kc, :],
                                       start=(kc == 0), stop=(kc == KC - 1))
                mm.then_inc(s3_l, 1)

            def counts(j, v):
                pe.wait_ge(s3_o, j + 1)
                pe.matmul(ps[:, 5, 16:24], earlier_sb[:, :], chosen[:, v, 0, :], start=True, stop=True)
                pe.matmul(ps[:, 5, 24:32], earlier_sb[:, :], chosen[:, v, 1, :], start=True, stop=False)
                pe.matmul(ps[:, 5, 24:32], ones_sb[:, :], chosen[:, v, 0, :], start=False, stop=True)
                pe.matmul(ps[:, 5, 32:40], ones_sb[:, :], chosen[:, v, 0, :], start=True, stop=False)
                pe.matmul(ps[:, 5, 32:40], ones_sb[:, :], chosen[:, v, 1, :], start=False, stop=True
                          ).then_inc(s3_c, 1)

            def turn_weights(j, v):
                pe.wait_ge(s3_w, j + 2)
                pe.wait_ge(s3_wc, j + 1)
                for u in range(2):
                    mm = pe.transpose(ps[0:EXPERTS, 6, u * P:(u + 1) * P], wgt[:, v, u, :], idf[:, :])
                mm.then_inc(s3_wt, 1)

            def biases(j, v):
                pe.wait_ge(s3_wc, j + 2)
                pe.wait_ge(s3_acc, j * 18 + 1)
                for u in range(2):
                    mm = pe.matmul(ps[:, 7, u * D:(u + 1) * D], wgtT[:, v, u * P:(u + 1) * P], be_sb[:, :],
                                   start=True, stop=True)
                mm.then_inc(s3_b, 1)

            def experts_out(j, v, u, q):
                pe.wait_ge(s3_acc, j * 18 + (9 * u + 2 * q + 3))
                for kc in range(KC):
                    at = (2 * kc + u) * P
                    mm = pe.matmul(ps[:, q, :], h3T[:, v, at:at + P], we_sb[:, kc, q * BANK:(q + 1) * BANK],
                                   start=(kc == 0), stop=(kc == KC - 1))
                mm.then_inc(s3_y, 1)

            def experts_step(j, v, last):
                experts_out(j, v, 0, 0)
                biases(j, v)
                for q in range(1, 4):
                    experts_out(j, v, 0, q)
                if not last:
                    turn_rows(j + 1, 1 - v)
                experts_out(j, v, 1, 0)
                if not last:
                    logits(j + 1, 1 - v)
                experts_out(j, v, 1, 1)
                experts_out(j, v, 1, 2)
                if not last:
                    counts(j + 1, 1 - v)
                experts_out(j, v, 1, 3)
                if not last:
                    turn_weights(j + 1, 1 - v)

            turn_rows(0, 0)
            logits(0, 0)
            counts(0, 0)
            turn_weights(0, 0)
            with pe.Fori(0, TILES // 4 - 1) as jj:
                experts_step(2 * jj, 0, False)
                experts_step(2 * jj + 1, 1, False)
            experts_step(TILES // 2 - 2, 0, False)
            experts_step(TILES // 2 - 1, 1, True)


def kernel(**inputs):
    import numpy as _np
    import concourse.bacc as _bacc
    from concourse import mybir as _mybir
    from concourse.bass_utils import run_bass_kernel_spmd as _run

    a = {k: _np.asarray(v) for k, v in inputs.items()}
    arange = _np.arange
    arrays = {
        "x": a["x"].reshape(TOKENS, D),
        "ctxT": a["ctx_768"].reshape(BATCH * NCTX, DCTX).T,
        "wqT": a["L0_attn_Wq"].T,
        "wkT": a["L0_attn_Wk"].T,
        "wvT": a["L0_attn_Wv"].T,
        "woT": a["L0_attn_Wo"].T,
        "pekT": a["L0_attn_pek"].T,
        "pek0": _np.tile(a["L0_attn_pek"][0], P // HD).reshape(P, 1),
        "pev": a["L0_attn_pev"],
        "xwqT": a["L0_xattn_Wq"].T,
        "xwk": a["L0_xattn_Wk"],
        "xwv": a["L0_xattn_Wv"],
        "xwo": a["L0_xattn_Wo"],
        "xbo": a["L0_xattn_bo"].reshape(1, D),
        "wg": a["L0_ffn_wg"],
        "weT": a["L0_ffn_W"].transpose(2, 0, 1),
        "be": a["L0_ffn_b"],
        "ident": _np.eye(P, dtype=_np.float32),
        "ones": _np.ones((P, P), _np.float32),
        "diag": (7 - arange(P)[:, None] // HD == arange(P)[None, :] % 8).astype(_np.float32),
        "fold": (arange(P)[:, None] % HD == arange(HD)[None, :]).astype(_np.float32),
        "earlier": (arange(P)[:, None] < arange(P)[None, :]).astype(_np.float32),
        "experts": _np.broadcast_to(arange(EXPERTS, dtype=_np.float32) - EXPERTS, (P, EXPERTS)),
    }
    nc = _bacc.Bacc("TRN2", target_bir_lowering=False, num_devices=1)
    ins, args = {}, []
    for name, v in arrays.items():
        v = _np.ascontiguousarray(v)
        ins[f"in_{name}"] = v
        args.append(nc.dram_tensor(f"in_{name}", v.shape, _mybir.dt.from_np(v.dtype), kind="ExternalInput").ap())
    out = nc.dram_tensor("out_0", (TOKENS, D), _mybir.dt.float32, kind="ExternalOutput").ap()
    decoder_layer(nc, *args, out)
    r = _run(nc, [ins], core_ids=[0])
    return r.results[0]["out_0"].reshape(BATCH, SEQ, D)
```

```python
from contextlib import ExitStack

import concourse.bass as bass
from concourse import mybir

F32 = mybir.dt.float32
BF16 = mybir.dt.bfloat16
U32 = mybir.dt.uint32
ALU = mybir.AluOpType
ACT = mybir.ActivationFunctionType
AX = mybir.AxisListType

P = 128
BATCH, SEQ, D = 2, 1024, 256
TOKENS = BATCH * SEQ
TILES = TOKENS // P
TPB = SEQ // P
KC = D // P
HEADS, HD = 16, 16
PAIRS = HEADS // 2
QUADS = HEADS // 4
SCALE = HD ** 0.5
REL = 256
TERMS = 3
Q_SLOTS = (0, 0, 1, 1, 0, 2)
K_SLOTS = (0, 1, 0, 1, 2, 0)
STACK = len(Q_SLOTS) * HD
BAND = 3 * P
ROW = 127 + BAND
XH, XD = 16, 64
INNER = XH * XD
NCTX, DCTX = 77, 192
CTXC = DCTX // 2
XBANKS = ((0, 6), (6, 12), (12, 16))
XK = XH * NCTX
XCH = (XK + P - 1) // P
XTAIL = XK - (XCH - 1) * P
RSTEPS = 10
EXPERTS = 8
CAP = TOKENS // EXPERTS
EPS = 1e-5
BIG = 1e30
GROUPS = 4
GT = TOKENS // GROUPS // P
BANK = 512


def decoder_layer(nc, x, ctxT, wqT, wkT, wvT, woT, pekT, pek0, pev, xwqT, xwk, xwv, xwo, xbo, wg, weT, be,
                  ident, ones, diag, fold, earlier, experts, out):
    nc.disable_value_cache = True
    qparts = nc.dram_tensor("qparts", (TERMS, D, TOKENS), BF16)
    kparts = nc.dram_tensor("kparts", (TERMS, D, TOKENS), BF16)
    pparts = nc.dram_tensor("pparts", (TERMS, HD, REL), BF16)
    pvrows = nc.dram_tensor("pvrows", (ROW + 1, HD), F32)
    rel = nc.dram_tensor("rel", (2 * HEADS, P, ROW), F32)
    gmat = nc.dram_tensor("gmat", (P, KC, BATCH, XK), F32)
    umat = nc.dram_tensor("umat", (BATCH, XK, D), F32)

    ctx = ExitStack()
    with ctx:
        def sb(name, shape, dt, where=ctx):
            return where.enter_context(nc.sbuf_tensor(name, shape, dt))

        def sem(name):
            return ctx.enter_context(nc.semaphore(name))

        ps = ctx.enter_context(nc.psum_tensor("ps", [P, 8, BANK], F32))
        S_BANK, T_BANK, R_BANK, O_BANK = 0, 4, 6, 7

        idf = sb("idf", [P, P], F32)
        x1 = sb("x1", [P, TILES, D], F32)
        half = sb("half", [P, 1], F32)

        v_b = sb("v_b", [P, TPB, D], F32)

        proj = ExitStack()
        pk0 = sb("pk0", [P, 1], F32, proj)
        pev0 = sb("pev0", [P, HD], F32, proj)
        xg = sb("xg", [P, 2, GT, D], F32, proj)
        hg = sb("hg", [P, GT, D], F32, proj)
        hT = sb("hT", [P, 2, KC, BANK], F32, proj)
        wq_sb = sb("wq_sb", [P, KC, D], F32, proj)
        wk_sb = sb("wk_sb", [P, KC, D], F32, proj)
        wv_sb = sb("wv_sb", [P, KC, D], F32, proj)
        st1 = sb("st1", [P, GT, 6], F32, proj)
        mv1 = sb("mv1", [P, GT, 2], F32, proj)
        rstd1 = sb("rstd1", [P, GT], F32, proj)
        full = sb("full", [P, 4, BANK], F32, proj)
        rest = sb("rest", [P, 4, BANK], F32, proj)
        parts = sb("parts", [P, 4, TERMS, BANK], BF16, proj)
        pk_in = sb("pk_in", [HD, REL + 1], F32, proj)
        pk_d = sb("pk_d", [HD, REL], F32, proj)
        pk_r = sb("pk_r", [HD, REL], F32, proj)
        pk_parts = sb("pk_parts", [HD, TERMS, REL], BF16, proj)
        pv_in = sb("pv_in", [P, 2, HD], F32, proj)
        zrow = sb("zrow", [P, P], F32, proj)
        brow = sb("brow", [P, P - 1], F32, proj)
        proj.close()

        att = ExitStack()
        q6 = sb("q6", [STACK, HEADS, SEQ], BF16, att)
        k6 = sb("k6", [STACK, HEADS, SEQ], BF16, att)
        p6 = sb("p6", [STACK, REL], BF16, att)
        pvt = sb("pvt", [P, 3, P * HD], F32, att)
        diag_sb = sb("diag_sb", [P, HEADS * 4], F32, att)
        fold_sb = sb("fold_sb", [P, 2, HD], F32, att)

        fw = ExitStack()
        xk_w = sb("xk_w", [CTXC, 2, INNER], F32, fw)
        xv_w = sb("xv_w", [CTXC, 2, INNER], F32, fw)
        ctx_sb = sb("ctx_sb", [CTXC, 2, BATCH * NCTX], F32, fw)
        xq_w = sb("xq_w", [P, INNER // P, D], F32, fw)
        xkT = sb("xkT", [P, INNER // P, BATCH * NCTX], F32, fw)
        g_out = sb("g_out", [P, KC, BATCH, XK], F32, fw)
        xvT = sb("xvT", [P, INNER // P, BATCH * NCTX], F32, fw)
        xo_w = sb("xo_w", [P, INNER // P, D], F32, fw)
        u_out = sb("u_out", [NCTX, BATCH, XH, D], F32, fw)
        fw.close()

        rel_out = sb("rel_out", [P, 2, 4, REL], F32, att)
        prob = sb("prob", [P, 2, SEQ], F32, att)
        bias = sb("bias", [P, HEADS, BAND], F32, att)
        pT = sb("pT", [P, 2, 4, TPB - 3, P], F32, att)
        bandT = sb("bandT", [P, 3, HEADS, P], F32, att)
        far = sb("far", [P, 2], F32, att)
        low = sb("low", [P, 2], F32, att)
        rsum = sb("rsum", [P, 2, HEADS], F32, att)
        rrec = sb("rrec", [P, HEADS], F32, att)
        picked = sb("picked", [P, HEADS, P // 2], F32, att)
        oTs = sb("oTs", [P, BANK], F32, att)
        zb = sb("zb", [P, BANK], BF16, att)
        att.close()

        late = ExitStack()
        wo_sb = sb("wo_sb", [P, KC, D], F32, late)
        xr = sb("xr", [P, 2, GT, D], F32, late)
        oT = sb("oT", [P, 2, KC, BANK], F32, late)
        bo = sb("bo", [P, D], F32, late)
        h2 = sb("h2", [P, 2, GT, D], F32, late)
        h2T = sb("h2T", [P, KC, TOKENS], F32, late)
        st2 = sb("st2", [P, GT, 6], F32, late)
        mv2 = sb("mv2", [P, 2, GT, 2], F32, late)
        rstd2 = sb("rstd2", [P, 2, GT], F32, late)
        g_sb = sb("g_sb", [P, KC, BATCH, XK], F32, late)
        u_sb = sb("u_sb", [P, BATCH, XCH, D], F32, late)
        h2s = sb("h2s", [P, 2, KC, P], F32, late)
        xlow = sb("xlow", [P, 2, XH], F32, late)
        xsum = sb("xsum", [P, 2, XH], F32, late)
        xrec = sb("xrec", [P, XH], F32, late)
        xp = sb("xp", [P, 2, XK], F32, late)
        xpT = sb("xpT", [P, 2, XCH, P], F32, late)
        st3 = sb("st3", [P, 6], F32, late)
        mvs = sb("mvs", [P, 2], F32, late)
        mv3 = sb("mv3", [P, TILES, 2], F32, late)
        rstd3 = sb("rstd3", [P, TILES], F32, late)
        we_sb = sb("we_sb", [P, KC, EXPERTS * D], F32, late)
        be_sb = sb("be_sb", [EXPERTS, D], F32, late)
        wg_sb = sb("wg_sb", [P, KC, EXPERTS], F32, late)
        earlier_sb = sb("earlier_sb", [P, P], F32, late)
        ones_sb = sb("ones_sb", [P, P], F32, late)
        e8 = sb("e8", [P, EXPERTS], F32, late)
        h3 = sb("h3", [P, 2, 2, D], F32, late)
        h3T = sb("h3T", [P, 2, KC * 2 * P], F32, late)
        top = sb("top", [P, 2], F32, late)
        below = sb("below", [P, 2, EXPERTS], F32, late)
        expb = sb("expb", [P, 2, EXPERTS], F32, late)
        den = sb("den", [P, 2], F32, late)
        gate = sb("gate", [P, 2], F32, late)
        cand = sb("cand", [P, 2, EXPERTS], F32, late)
        first_e = sb("first_e", [P, 2], F32, late)
        chosen = sb("chosen", [P, 2, 2, EXPERTS], F32, late)
        place = sb("place", [P, 2, EXPERTS], F32, late)
        count = sb("count", [P, EXPERTS], F32, late)
        kept = sb("kept", [P, 2, EXPERTS], F32, late)
        expw = sb("expw", [P, 2, EXPERTS], F32, late)
        wgt = sb("wgt", [P, 2, 2, EXPERTS], F32, late)
        wgtT = sb("wgtT", [EXPERTS, 2, 2 * P], F32, late)
        late.close()

        s_cst, s_w, s_set = sem("s_cst"), sem("s_w"), sem("s_set")
        s_x = [sem("s_x_0"), sem("s_x_1")]
        s_stat, s_agg, s_var, s_rstd, s_h = sem("s_stat"), sem("s_agg"), sem("s_var"), sem("s_rstd"), sem("s_h")
        s_proj, s_full, s_hi = sem("s_proj"), sem("s_full"), sem("s_hi")
        s_rest, s_mid, s_lo = sem("s_rest"), sem("s_mid"), sem("s_lo")
        s_parts = [sem(f"s_parts{j}") for j in range(4)]
        s_v, s_vc = sem("s_v"), sem("s_vc")
        s_pk, s_pkp, s_pkd, s_pv, s_pvd, s_pad = (sem("s_pk"), sem("s_pkp"), sem("s_pkd"), sem("s_pv"),
                                                  sem("s_pvd"), sem("s_pad"))
        s_tab, s_qk = sem("s_tab"), sem("s_qk")
        s_b = [sem(f"s_b{c}") for c in range(QUADS)]
        s_r, s_s, s_far = sem("s_r"), sem("s_s"), sem("s_far")
        s_rc = sem("s_rc")
        s_rw = [sem("s_rw0"), sem("s_rw1")]
        s_min = sem("s_min")
        s_exp = sem("s_exp")
        s_av = sem("s_av")
        s_vb = sem("s_vb")
        s_oc = sem("s_oc")
        s_of = sem("s_of")
        s_o = sem("s_o")
        s_on = sem("s_on")
        s_rr = sem("s_rr")
        s_t = [sem("s_t0"), sem("s_t1")]
        s_tc = [sem("s_tc0"), sem("s_tc1")]
        s_z = sem("s_z")
        s_go = {e: sem(f"s_go_{e}") for e in ("sp", "pool", "dve", "pe")}
        s_done = sem("s_done")
        s_xw, s_xwc = sem("s_xw"), [sem("s_xwc0"), sem("s_xwc1")]
        s_xin, s_gu = sem("s_xin"), sem("s_gu")
        s_wo, s_xr = sem("s_wo"), [sem("s_xr0"), sem("s_xr1")]
        s_att, s_add1, s_stat2, s_agg2 = sem("s_att"), sem("s_add1"), sem("s_stat2"), sem("s_agg2")
        s_var2, s_rstd2, s_h2, s_x1b = sem("s_var2"), sem("s_rstd2"), sem("s_h2"), sem("s_x1b")
        s_h2t, s_h2tc = [sem("s_h2t0"), sem("s_h2t1")], [sem("s_h2tc0"), sem("s_h2tc1")]
        s_g, s_u, s_h2s = sem("s_g"), sem("s_u"), sem("s_h2s")
        s_s2 = sem("s_s2")
        s_xl = sem("s_xl")
        s_xe = sem("s_xe")
        s_xs, s_xn = sem("s_xs"), sem("s_xn")
        s_xt = sem("s_xt")
        s_xc = [sem(f"s_xc{n}") for n in range(3)]
        s_xu = sem("s_xu")
        s_x2 = sem("s_x2")
        s_agg3 = sem("s_agg3")
        s_stat3, s_mv3, s_var3, s_rstd3 = sem("s_stat3"), sem("s_mv3"), sem("s_var3"), sem("s_rstd3")
        s_we, s_cnt0 = sem("s_we"), sem("s_cnt0")
        s3_h, s3_l, s3_o, s3_c = sem("s3_h"), sem("s3_l"), sem("s3_o"), sem("s3_c")
        s3_t = sem("s3_t")
        s3_tc = sem("s3_tc")
        s3_r = sem("s3_r")
        s3_e = sem("s3_e")
        s3_w = sem("s3_w")
        s3_wt = sem("s3_wt")
        s3_wc = sem("s3_wc")
        s3_b = sem("s3_b")
        s3_y = sem("s3_y")
        s3_acc = sem("s3_acc")
        s3_out = sem("s3_out")

        block = ctx.enter_context(nc.Block())

        x_v = x.rearrange("(g s p) d -> g p s d", s=GT, p=P)

        def head_no(b, i, h):
            return b * (TPB * HEADS) + i * HEADS + h

        def rel_writes(b, i, c):
            return b * (8 * TPB * QUADS) + (16 * (i * (QUADS // 2) + c // 2))

        def head_uses(i):
            return PAIRS if i < 4 else HEADS

        def uses_before(i):
            return sum(head_uses(j) + 1 for j in range(i))

        def use(b, i, h):
            own = h // 2 if i < 4 else h
            return b * uses_before(TPB) + (GROUPS + uses_before(i) + own + 1)

        def use_values(b, i):
            return b * uses_before(TPB) + (GROUPS + uses_before(i) + head_uses(i) + 1)

        def banks_of(i, h):
            if i < 4:
                return [(h % 2, 0, i + 1)]
            cut = min(i - 2, 4)
            return [(0, 0, cut), (1, cut, i + 1)]

        def transposed(i, h, k0, k1):
            lo = max(0, i - 2)
            places = []
            if k0 < lo:
                places.append((pT[:, (h // 4) % 2, h % 4, k0:min(k1, lo), :], k0, min(k1, lo)))
            if k1 > lo:
                a = max(k0, lo)
                places.append((bandT[:, a + 2 - i:k1 + 2 - i, h, :], a, k1))
            return places

        def ahead(i, h):
            n = i * HEADS + h + 2
            return (n // HEADS, n % HEADS) if n < TPB * HEADS else None

        def score(k, K):
            at = S_BANK + 2 * (k % 2)
            return ps[:, at:at + 2, :].rearrange("p k n -> p (k n)")[:, 0:K]

        MCH = INNER // P
        units = []
        for what in "kv":
            units += [(what, m, min(m + 3, MCH)) for m in range(0, MCH, 3)]
        XKV = len(units)
        for kc in range(KC):
            units += [("g", kc, range(h, min(h + 6, XH), 2)) for h0 in range(0, XH, 6) for h in (h0, h0 + 1)]
        for b_ in range(BATCH):
            units += [("u", b_, range(h, min(h + 4, XH), 2)) for h0 in range(0, XH, 4) for h in (h0, h0 + 1)]
        XUNITS = len(units)
        CK = BATCH * NCTX

        def unit_copies(n):
            what = units[n]
            bank = ps[:, S_BANK + n % 4, :]
            if what[0] in "kv":
                _, m0, m1 = what
                dst = (xkT if what[0] == "k" else xvT)[:, m0:m1, :]
                return dst, bank[:, 0:(m1 - m0) * CK].rearrange("p (m k) -> p m k", k=CK), \
                    (-1.0 / XD ** 0.5 if what[0] == "k" else 1.0)
            if what[0] == "g":
                _, kc, hs = what
                dst = g_out[:, kc, :, :].rearrange("p b (h k) -> p h b k", k=NCTX)[:, hs[0]:hs[-1] + 1:2]
                return dst, bank[:, 0:len(hs) * CK].rearrange("p (h b k) -> p h b k", b=BATCH, k=NCTX), 1.0
            _, b_, hs = what
            return u_out[:, b_, hs[0]:hs[-1] + 1:2, :], ps[0:NCTX, S_BANK + n % 4, :].rearrange("p (h f) -> p h f", f=D), 1.0

        @block.sync
        def _(sp):
            for k in range(2):
                sp.sem_inc(s_rw[k], 16)
            sp.dma_start(xg[:, 0], x_v[0]).then_inc(s_x[0], 16)
            for dst, src in ((idf[:, :], ident), (pk0[:, :], pek0),
                             (pev0[:, :], pev[0:1, :].broadcast_to([P, HD])),
                             (pk_in[:, :], pekT[:, 0:REL + 1]),
                             (pv_in[:, :, :], pev[1:REL + 1, :].rearrange("(c p) d -> p c d", p=P))):
                sp.dma_start(dst, src).then_inc(s_cst, 16)
            for dst, src in ((wq_sb, wqT), (wk_sb, wkT), (wv_sb, wvT)):
                sp.dma_start(dst[:, :, :], src.rearrange("(c p) n -> p c n", p=P)).then_inc(s_w, 16)
            sp.dma_start(xg[:, 1], x_v[1]).then_inc(s_x[1], 16)
            sp.wait_ge(s_set, 2)
            rel_v = rel.ap().rearrange("s r u -> r s u")
            sp.dma_start(rel_v[:, :, 0:P], zrow[:, :].unsqueeze(1).broadcast_to([P, 2 * HEADS, P])).then_inc(s_pad, 16)
            sp.dma_start(rel_v[:, :, P + REL:ROW], brow[:, :].unsqueeze(1).broadcast_to([P, 2 * HEADS, P - 1])
                         ).then_inc(s_pad, 16)
            sp.dma_start(pvrows[0:P, :], zrow[:, 0:HD]).then_inc(s_pvd, 16)
            sp.dma_start(pvrows[P + REL:ROW + 1, :], zrow[:, 0:HD]).then_inc(s_pvd, 16)
            sp.wait_ge(s_pv, 1)
            sp.dma_start(pvrows[P:P + REL, :].rearrange("(c p) d -> p c d", p=P), pv_in[:, :, :]).then_inc(s_pvd, 16)
            sp.wait_ge(s_pkp, 4)
            sp.dma_start(pparts.ap().rearrange("t d j -> d t j"), pk_parts[:, :, :]).then_inc(s_pkd, 16)
            for g in range(GROUPS):
                if g + 2 < GROUPS:
                    sp.wait_ge(s_h, g + 1)
                    sp.dma_start(xg[:, g % 2], x_v[g + 2]).then_inc(s_x[g % 2], 16)
                if g == 2:
                    for dst, src, rows in ((xk_w, xwk, CTXC), (xv_w, xwv, CTXC), (ctx_sb, ctxT, CTXC), (xq_w, xwqT, P),
                                           (xo_w, xwo, P)):
                        sp.dma_start(dst[:, :, :], src.rearrange("(c p) n -> p c n", p=rows)).then_inc(s_xin, 16)
                for j in range(4):
                    u = 4 * g + j
                    sp.wait_ge(s_lo, u + 1)
                    to = (qparts, kparts)[j // 2].ap()[:, (j % 2) * P:(j % 2 + 1) * P, g * BANK:(g + 1) * BANK]
                    sp.dma_start(to.rearrange("t p n -> p t n"), parts[:, u % 4]).then_inc(s_parts[u % 4], 16)
            for k in range(4):
                sp.wait_ge(s_parts[k], 16 * 4)
            sp.wait_ge(s_vc, TILES // 2)
            sp.wait_ge(s_pad, 32)
            sp.wait_ge(s_pvd, 48)
            sp.wait_ge(s_pkd, 16)
            for n, t in enumerate(K_SLOTS):
                sp.dma_start(p6[n * HD:(n + 1) * HD, :], pparts[t]).then_inc(s_tab, 16)
            for blk in range(3):
                sp.dma_start(pvt[:, blk, :], bass.AP(tensor=pvrows, offset=blk * P * HD, ap=[[HD, P], [1, P * HD]])
                             ).then_inc(s_tab, 16)
            sp.dma_start(diag_sb[:, :], diag).then_inc(s_tab, 16)
            sp.dma_start(fold_sb[:, :, :], fold).then_inc(s_tab, 16)

            def write_rel(b, i, c):
                sp.wait_ge(s_rc, b * (TPB * PAIRS) + (2 * (i * QUADS + c) + 3))
                sl = (i % 2) * HEADS + 4 * c
                sp.dma_start(rel.ap()[sl:sl + 4, :, P:P + REL].rearrange("s r u -> r s u"), rel_out[:, c % 2]
                             ).then_inc(s_rw[c % 2], 16)

            def read_bias(b, i, c):
                if i > 0:
                    sp.wait_ge(s_min, head_no(b, i - 1, 4 * c + 3) + 2)
                sp.wait_ge(s_rw[c % 2], rel_writes(b, i, c) + 32)
                sl = (i % 2) * HEADS + 4 * c
                src = bass.AP(tensor=rel, offset=sl * (P * ROW) + 127, ap=[[ROW - 1, P], [P * ROW, 4], [1, BAND]])
                sp.dma_start(bias[:, 4 * c:4 * c + 4, :], src).then_inc(s_b[c], 16)

            with sp.Fori(0, BATCH) as b:
                sp.wait_ge(s_min, b * (TPB * HEADS) + 1)
                for n in range(len(Q_SLOTS)):
                    for dst, src, t in ((q6, qparts, Q_SLOTS[n]), (k6, kparts, K_SLOTS[n])):
                        src_v = src.ap()[t].rearrange("(h d) n -> d h n", d=HD)
                        sp.dma_start(dst[n * HD:(n + 1) * HD, :, :], src_v[:, :, bass.ds(b * SEQ, SEQ)]
                                     ).then_inc(s_qk, 16)
                for i in range(TPB):
                    for c in range(QUADS):
                        write_rel(b, i, c)
                        if i == 0 and c == 1:
                            sp.wait_ge(s_gu, 48)
                        if c > 0:
                            read_bias(b, i, c - 1)
                    read_bias(b, i, QUADS - 1)
                sp.sem_inc(s_go["sp"], 1)
            sp.wait_ge(s_on, TILES + 1)
            sp.dma_start(wo_sb[:, :, :], woT.rearrange("(c p) n -> p c n", p=P)).then_inc(s_wo, 16)
            sp.dma_start(bo[:, :], xbo.broadcast_to([P, D])).then_inc(s_wo, 16)
            for g in range(2):
                sp.dma_start(xr[:, g], x_v[g]).then_inc(s_xr[g], 16)
            sp.dma_start(g_sb[:, :, :, :], gmat.ap()).then_inc(s_g, 16)
            whole = XK // P
            for b in range(BATCH):
                sp.dma_start(u_sb[:, b, 0:whole, :], umat.ap()[b, 0:whole * P].rearrange("(c p) f -> p c f", p=P)
                             ).then_inc(s_u, 16)
                sp.dma_start(u_sb[0:XK - whole * P, b, whole, :], umat.ap()[b, whole * P:XK]).then_inc(s_u, 16)
            for g in range(2, GROUPS):
                sp.wait_ge(s_add1, g - 1)
                sp.dma_start(xr[:, g % 2], x_v[g]).then_inc(s_xr[g % 2], 16)
            sp.dma_start(we_sb[:, :, :].rearrange("p c (e f) -> p c e f", e=EXPERTS),
                         weT.rearrange("(c p) e f -> p c e f", p=P)).then_inc(s_we, 16)
            sp.dma_start(be_sb[:, :], be).then_inc(s_we, 16)
            sp.dma_start(wg_sb[:, :, :], wg.rearrange("(c p) e -> p c e", p=P)).then_inc(s_we, 16)
            sp.dma_start(earlier_sb[:, :], earlier).then_inc(s_we, 16)
            sp.dma_start(ones_sb[:, :], ones).then_inc(s_we, 16)
            sp.dma_start(e8[:, :], experts).then_inc(s_we, 16)
            out_v = out.rearrange("(t p) d -> p t d", p=P)
            with sp.Fori(0, TILES // 2) as j:
                sp.wait_ge(s3_acc, j * 18 + 27)
                sp.dma_start(out_v[:, bass.ds(2 * j, 2), :], x1[:, bass.ds(2 * j, 2), :]).then_inc(s_done, 16)
                sp.sem_inc(s_go["sp"], 1)
            sp.wait_ge(s_done, 16 * (TILES // 2))

        @block.gpsimd
        def _(pool):
            pool.wait_ge(s_set, 1)

            def deviation(g):
                pool.wait_ge(s_agg, g + 1)
                nc.gpsimd.tensor_scalar(rstd1[:, :], mv1[:, :, 1], EPS, None, ALU.add).then_inc(s_var, 1)
                pool.wait_ge(s_var, g + 1)
                nc.gpsimd.tensor_tensor(rstd1[:, :], rstd1[:, :], half[:, 0:1].broadcast_to([P, GT]), ALU.pow
                                        ).then_inc(s_rstd, 1)

            deviation(0)
            for g in range(GROUPS):
                if g + 1 < GROUPS:
                    deviation(g + 1)
                for j in range(4):
                    u = 4 * g + j
                    pool.wait_ge(s_rest, u + 1)
                    nc.gpsimd.tensor_copy(parts[:, j, 1, :], rest[:, j, :]).then_inc(s_mid, 1)

            pool.wait_ge(s_vc, TILES // 2)
            pool.sem_inc(s_vb, 1)
            pool.wait_ge(s_av, TPB * QUADS + 2)
            nc.gpsimd.tensor_copy(v_b[:, :, :], x1[:, TPB:TILES, :]).then_inc(s_vb, 1)

            pool.wait_ge(s_wo, 32)
            for g in range(GROUPS):
                pool.wait_ge(s_agg2, g + 1)
                nc.gpsimd.tensor_scalar(rstd2[:, g % 2, :], mv2[:, g % 2, :, 1], EPS, None, ALU.add).then_inc(s_var2, 1)
                pool.wait_ge(s_var2, g + 1)
                nc.gpsimd.tensor_tensor(rstd2[:, g % 2, :], rstd2[:, g % 2, :], half[:, 0:1].broadcast_to([P, GT]),
                                        ALU.pow).then_inc(s_rstd2, 1)
                pool.wait_ge(s_h2, g + 1)
                nc.gpsimd.tensor_tensor(x1[:, GT * g:GT * (g + 1), :], x1[:, GT * g:GT * (g + 1), :],
                                        bo[:, :].unsqueeze(1).broadcast_to([P, GT, D]), ALU.add).then_inc(s_x1b, 1)
            for kc in range(KC):
                pool.wait_ge(s_h2tc[kc], GROUPS)
            with pool.Fori(0, TPB) as j:
                for u in range(2):
                    pool.wait_ge(s_s2, j * 6 + (3 * u + 3))
                    nc.gpsimd.tensor_copy(h2s[:, u, :, :], h2T[:, :, bass.ds(j * P + u * SEQ, P)]).then_inc(s_h2s, 1)
            pool.wait_ge(s_mv3, TILES)
            nc.gpsimd.tensor_scalar(rstd3[:, :], mv3[:, :, 1], EPS, None, ALU.add).then_inc(s_var3, 1)
            pool.wait_ge(s_var3, 1)
            nc.gpsimd.tensor_tensor(rstd3[:, :], rstd3[:, :], half[:, 0:1].broadcast_to([P, TILES]), ALU.pow
                                    ).then_inc(s_rstd3, 1)

        LAST_USE = GROUPS + BATCH * uses_before(TPB)

        @block.scalar
        def _(act):
            act.sem_inc(s_rc, 1)
            act.sem_inc(s_exp, 2)
            act.wait_ge(s_cst, 80)
            act.wait_ge(s_pk, 1)
            nc.scalar.copy(pk_parts[:, 0, :], pk_d[:, :]).then_inc(s_pkp, 1)
            act.wait_ge(s_pkp, 2)
            nc.scalar.copy(pk_parts[:, 1, :], pk_r[:, :]).then_inc(s_pkp, 1)
            for g in range(GROUPS):
                act.wait_ge(s_t[1], g + 1)
                if g >= 2:
                    act.wait_ge(s_v, 2 * (g - 1))
                nc.scalar.copy(hT[:, g % 2, 1, :], ps[:, T_BANK + 1, :]).then_inc(s_tc[1], 1)
                for j in range(4):
                    u = 4 * g + j
                    act.wait_ge(s_proj, u + 1)
                    if u >= 4:
                        act.wait_ge(s_lo, u - 3)
                        act.wait_ge(s_parts[j], 16 * (u // 4))
                    if j < 2:
                        nc.scalar.activation(full[:, j, :], ps[:, S_BANK + j, :], ACT.Copy, scale=-1.0 / SCALE
                                             ).then_inc(s_full, 1)
                    else:
                        nc.scalar.activation(full[:, j, :], ps[:, S_BANK + j, :], ACT.Identity, bias=pk0[:, 0:1]
                                             ).then_inc(s_full, 1)
                    act.wait_ge(s_full, u + 1)
                    nc.scalar.copy(parts[:, j, 0, :], full[:, j, :]).then_inc(s_hi, 1)

            def keep_folded(n, dst, src):
                for k in range(2):
                    act.wait_ge(s_xwc[k], (n + 1 - k) // 2)
                act.dma_start(dst, src).then_inc(s_gu, 16)

            first_u = [min(n for n, what in enumerate(units) if what[:2] == ("u", b)) for b in range(BATCH)]
            first_u.append(XUNITS)
            umat_v = umat.ap().rearrange("b (h k) f -> b k h f", k=NCTX)
            for n in range(0, XUNITS, 2):
                act.wait_ge(s_xw, n + 1)
                dst, src, scale = unit_copies(n)
                nc.scalar.activation(dst, src, ACT.Copy, scale=scale).then_inc(s_xwc[0], 1)
                if n in (first_u[0], first_u[0] + 1):
                    keep_folded(first_u[0], gmat.ap(), g_out[:, :, :, :])
                if n in (first_u[1], first_u[1] + 1):
                    keep_folded(first_u[1], umat_v[0], u_out[:, 0, :, :])
            keep_folded(XUNITS, umat_v[1], u_out[:, 1, :, :])

            def rel_copy(b, i, pair):
                c, pos = pair // 2, pair % 2
                act.wait_ge(s_r, b * (TPB * PAIRS) + (i * PAIRS + pair + 1))
                if pos == 0:
                    act.wait_ge(s_rw[c % 2], rel_writes(b, i, c) + 16)
                nc.scalar.copy(rel_out[:, c % 2, 2 * pos:2 * pos + 2, :].rearrange("p s j -> p (s j)"),
                               ps[:, R_BANK, :]).then_inc(s_rc, 1)

            def softmax(b, i, h):
                act.wait_ge(s_min, head_no(b, i, h) + 2)
                K = (i + 1) * P
                nc.scalar.activation(prob[:, h % 2, 0:K], score(h, K), ACT.Exp, bias=low[:, h % 2:h % 2 + 1],
                                     scale=-1.0, accum_out=rsum[:, i % 2, h:h + 1]).then_inc(s_exp, 1)

            def copy_t(b, i, h):
                for bank, k0, k1 in banks_of(i, h):
                    act.wait_ge(s_t[bank], use(b, i, h))
                    if bank == 1:
                        act.wait_ge(s_av, b * (TPB * QUADS) + (i * QUADS + h // 4 + 1))
                        act.wait_ge(s_t[1], b * uses_before(TPB) + (GROUPS + uses_before(i)))
                        places = transposed(i, h, k0, k1)
                        for to, a, z in places:
                            ins = nc.scalar.copy(to, ps[:, T_BANK + 1, (a - k0) * P:(z - k0) * P].rearrange(
                                "p (k n) -> p k n", n=P))
                        ins.then_inc(s_tc[1], 1)

            def copy_out(b, i):
                act.wait_ge(s_o, b * TPB + (i + 2))
                nc.scalar.copy(oTs[:, :], ps[:, O_BANK, :]).then_inc(s_oc, 1)

            with act.Fori(0, BATCH) as b:
                for pair in range(PAIRS):
                    rel_copy(b, 0, pair)
                softmax(b, 0, 0)
                softmax(b, 0, 1)
                act.wait_ge(s_gu, 48)
                for i in range(TPB):
                    for h in range(HEADS):
                        copy_t(b, i, h)
                        if ahead(i, h):
                            softmax(b, *ahead(i, h))
                        if h % 2 == 1 and i + 1 < TPB:
                            rel_copy(b, i + 1, h // 2)
                        if h == 1 and i > 0:
                            copy_out(b, i - 1)
                copy_out(b, TPB - 1)

            act.wait_ge(s_on, TILES + 1)
            for g in range(GROUPS + 1):
                if g < GROUPS:
                    act.wait_ge(s_t[1], LAST_USE + g + 1)
                    if g >= 2:
                        act.wait_ge(s_att, g - 1)
                    nc.scalar.copy(oT[:, g % 2, 1, :], ps[:, T_BANK + 1, :]).then_inc(s_tc[1], 1)
                if g >= 1:
                    act.wait_ge(s_h2t[1], g)
                    nc.scalar.copy(h2T[:, 1, (g - 1) * BANK:g * BANK], ps[:, 1, :]).then_inc(s_h2tc[1], 1)

            act.sem_inc(s_xe, 3)
            act.sem_inc(s_xc[2], 1)

            def cross_exp(j, u):
                for n, (h0, h1) in enumerate(XBANKS):
                    act.wait_ge(s_xl, j * 6 + (3 * u + n + 1))
                    if n == 0:
                        act.wait_ge(s_xt, j * 6 + (3 * u + 3))
                    for h in range(h0, h1):
                        at = (h - h0) * NCTX
                        ins = nc.scalar.activation(xp[:, u, h * NCTX:(h + 1) * NCTX], ps[:, n, at:at + NCTX], ACT.Exp,
                                                   bias=xlow[:, u, h:h + 1], scale=-1.0, accum_out=xsum[:, u, h:h + 1])
                    ins.then_inc(s_xe, 1)

            def cross_step(j, u, following):
                act.wait_ge(s_xt, j * 6 + (3 * u + 9))
                act.wait_ge(s_xu, j * 2 + (u + 1))
                nc.scalar.copy(xpT[:, u, XCH - 2, :], ps[:, 5, 0:P])
                nc.scalar.copy(xpT[0:XTAIL, u, XCH - 1, :], ps[0:XTAIL, 5, P:2 * P]).then_inc(s_xc[2], 1)
                if following is not None:
                    cross_exp(*following)

            cross_exp(0, 0)
            with act.Fori(0, TPB - 1) as j:
                cross_step(j, 0, (j, 1))
                cross_step(j, 1, (j + 1, 0))
            cross_step(TPB - 1, 0, (TPB - 1, 1))
            cross_step(TPB - 1, 1, None)

            act.sem_inc(s3_tc, 1)
            act.sem_inc(s3_wc, 1)

            def route(j, v):
                act.wait_ge(s3_t, j + 2)
                act.wait_ge(s3_y, j * 8 + 8)
                nc.scalar.copy(h3T[:, v, :], ps[:, 4, :]).then_inc(s3_tc, 1)
                act.wait_ge(s3_r, j * RSTEPS + 2)
                nc.scalar.activation(expb[:, :, :], below[:, :, :], ACT.Exp).then_inc(s3_e, 1)
                act.wait_ge(s3_wt, j + 1)
                nc.scalar.copy(wgtT[:, v, :], ps[0:EXPERTS, 6, 0:2 * P]).then_inc(s3_wc, 1)

            route(0, 0)
            with act.Fori(0, TILES // 4 - 1) as jj:
                route(2 * jj + 1, 1)
                route(2 * jj + 2, 0)
            route(TILES // 2 - 1, 1)

        @block.vector
        def _(dve):
            dve.sem_inc(s_min, 1)
            dve.sem_inc(s_on, 1)
            nc.vector.memset(half[:, :], -0.5).then_inc(s_set, 1)
            nc.vector.memset(zrow[:, :], 0.0)
            nc.vector.memset(brow[:, :], BIG).then_inc(s_set, 1)

            def normalise(g):
                dve.wait_ge(s_x[g % 2], 16 * (g // 2 + 1))
                for s in range(GT):
                    nc.vector.bn_stats(st1[:, s, :], xg[:, g % 2, s, :]).then_inc(s_stat, 1)
                dve.wait_ge(s_stat, GT * (g + 1))
                for s in range(GT):
                    ins = nc.vector.bn_aggr(mv1[:, s, :], st1[:, s, :])
                ins.then_inc(s_agg, 1)
                dve.wait_ge(s_rstd, g + 1)
                if g >= 1:
                    dve.wait_ge(s_t[1], g)
                for s in range(GT):
                    ins = nc.vector.tensor_scalar(hg[:, s, :], xg[:, g % 2, s, :], mv1[:, s, 0:1], rstd1[:, s:s + 1],
                                                  ALU.subtract, ALU.mult)
                ins.then_inc(s_h, 1)

            normalise(0)
            dve.wait_ge(s_cst, 80)
            nc.vector.tensor_scalar(pk_d[:, :], pk_in[:, 1:REL + 1], pk_in[:, 0:1], None, ALU.subtract
                                    ).then_inc(s_pk, 1)
            nc.vector.tensor_tensor(pv_in[:, :, :], pv_in[:, :, :], pev0[:, :].unsqueeze(1).broadcast_to([P, 2, HD]),
                                    ALU.subtract).then_inc(s_pv, 1)
            dve.wait_ge(s_pkp, 1)
            nc.vector.tensor_tensor(pk_r[:, :], pk_d[:, :], pk_parts[:, 0, :], ALU.subtract).then_inc(s_pkp, 1)
            dve.wait_ge(s_pkp, 3)
            nc.vector.tensor_tensor(pk_parts[:, 2, :], pk_r[:, :], pk_parts[:, 1, :], ALU.subtract).then_inc(s_pkp, 1)
            for g in range(GROUPS):
                dve.wait_ge(s_t[0], g + 1)
                if g >= 2:
                    dve.wait_ge(s_v, 2 * (g - 1))
                nc.vector.tensor_copy(hT[:, g % 2, 0, :], ps[:, T_BANK, :]).then_inc(s_tc[0], 1)
                if g + 1 < GROUPS:
                    normalise(g + 1)
                for j in range(5):
                    u = 4 * g + j
                    if j < 4:
                        dve.wait_ge(s_hi, u + 1)
                        nc.vector.tensor_tensor(rest[:, j, :], full[:, j, :], parts[:, j, 0, :], ALU.subtract
                                                ).then_inc(s_rest, 1)
                    if j > 0:
                        dve.wait_ge(s_mid, u)
                        nc.vector.tensor_tensor(parts[:, j - 1, 2, :], rest[:, j - 1, :], parts[:, j - 1, 1, :],
                                                ALU.subtract).then_inc(s_lo, 1)
                for half_g in range(2):
                    dve.wait_ge(s_v, 2 * g + half_g + 1)
                    t = GT * g + 2 * half_g
                    v_to = v_b[:, t:t + 2, :] if t < TPB else x1[:, t:t + 2, :]
                    nc.vector.tensor_tensor(v_to.rearrange("p t (h d) -> p (t h) d", d=HD),
                                            ps[:, R_BANK + half_g, :].rearrange("p (a d) -> p a d", d=HD),
                                            pev0[:, :].unsqueeze(1).broadcast_to([P, 2 * HEADS, HD]), ALU.add
                                            ).then_inc(s_vc, 1)
            for n in range(1, XUNITS, 2):
                dve.wait_ge(s_xw, n + 1)
                dst, src, scale = unit_copies(n)
                nc.vector.tensor_scalar(dst, src, scale, None, ALU.mult).then_inc(s_xwc[1], 1)
            dve.wait_ge(s_gu, 48)
            nc.vector.memset(zb[:, :], 0.0).then_inc(s_z, 1)
            dve.wait_ge(s_tab, 16 * 11)

            def minimum(b, i, h):
                n = head_no(b, i, h)
                w0 = max(0, i - 2) * P
                K = (i + 1) * P
                dve.wait_ge(s_s, n + 1)
                if h % 4 == 0:
                    dve.wait_ge(s_b[h // 4], b * (16 * TPB) + (16 * i + 16))
                dve.wait_ge(s_exp, n + 1)
                first = BIG
                if i > 2:
                    nc.vector.tensor_reduce(far[:, h % 2:h % 2 + 1], score(h, K)[:, 0:w0], AX.X, ALU.min
                                            ).then_inc(s_far, 1)
                    dve.wait_ge(s_far, b * ((TPB - 3) * HEADS) + ((i - 3) * HEADS + h + 1))
                    first = far[:, h % 2:h % 2 + 1]
                dve.sem_inc(s_go["dve"], 1)
                s = score(h, K)[:, w0:K]
                nc.vector.tensor_tensor_reduce(s, s, bias[:, h, BAND - (K - w0):BAND], 1.0, first,
                                               ALU.add, ALU.min, low[:, h % 2:h % 2 + 1]).then_inc(s_min, 1)

            def copy_t(b, i, h):
                for bank, k0, k1 in banks_of(i, h):
                    if bank == 0:
                        dve.wait_ge(s_t[0], use(b, i, h))
                        dve.wait_ge(s_av, b * (TPB * QUADS) + (i * QUADS + h // 4 + 1))
                        dve.wait_ge(s_t[1], b * uses_before(TPB) + (GROUPS + uses_before(i)))
                        for to, a, z in transposed(i, h, k0, k1):
                            ins = nc.vector.tensor_copy(to, ps[:, T_BANK, (a - k0) * P:(z - k0) * P].rearrange(
                                "p (k n) -> p k n", n=P))
                        ins.then_inc(s_tc[0], 1)

            def pick(b, i):
                for bank in range(2):
                    dve.wait_ge(s_t[bank], use_values(b, i))
                    dve.wait_ge(s_o, b * TPB + (i + 1))
                    nc.vector.tensor_tensor(
                        picked[:, :, 32 * bank:32 * bank + 32].rearrange("p h (g q) -> p g h q", q=4),
                        ps[:, T_BANK + bank, :].rearrange("p (g h q) -> p g h q", g=8, q=4),
                        diag_sb[:, :].rearrange("p (h q) -> p h q", q=4).unsqueeze(1).broadcast_to([P, 8, HEADS, 4]),
                        ALU.mult).then_inc(s_tc[bank], 1)

            def finish(b, i):
                nc.vector.reciprocal(rrec[:, :], rsum[:, i % 2, :]).then_inc(s_rr, 1)
                dve.wait_ge(s_rr, b * TPB + (i + 1))
                dve.wait_ge(s_of, b * TPB + (i + 1))
                nc.vector.tensor_tensor(
                    x1[:, bass.ds(b * TPB + i, 1), :].rearrange("p o (h d) -> p (o h) d", d=HD),
                    ps[:, O_BANK, :].rearrange("p (h r) -> p h r", r=32)[:, :, 0:HD],
                    rrec[:, :].unsqueeze(2).broadcast_to([P, HEADS, HD]), ALU.mult).then_inc(s_on, 1)

            with dve.Fori(0, BATCH) as b:
                minimum(b, 0, 0)
                minimum(b, 0, 1)
                for i in range(TPB):
                    for h in range(HEADS):
                        if ahead(i, h):
                            minimum(b, *ahead(i, h))
                        copy_t(b, i, h)
                        if h == 3 and i > 0:
                            finish(b, i - 1)
                    pick(b, i)
                finish(b, TPB - 1)

            dve.wait_ge(s_on, TILES + 1)

            def copy_o(g):
                dve.wait_ge(s_t[0], LAST_USE + g + 1)
                if g >= 2:
                    dve.wait_ge(s_att, g - 1)
                nc.vector.tensor_copy(oT[:, g % 2, 0, :], ps[:, T_BANK, :]).then_inc(s_tc[0], 1)

            def copy_h2(g):
                dve.wait_ge(s_h2t[0], g + 1)
                nc.vector.tensor_copy(h2T[:, 0, g * BANK:(g + 1) * BANK], ps[:, 0, :]).then_inc(s_h2tc[0], 1)

            copy_o(0)
            for g in range(GROUPS):
                dve.wait_ge(s_att, g + 1)
                dve.wait_ge(s_xr[g % 2], 16 * (g // 2 + 1))
                for k in range(2):
                    t = GT * g + 2 * k
                    ins = nc.vector.tensor_tensor(x1[:, t:t + 2, :].rearrange("p t d -> p (t d)"), ps[:, 6 + k, :],
                                                  xr[:, g % 2, 2 * k:2 * k + 2, :].rearrange("p t d -> p (t d)"),
                                                  ALU.add)
                ins.then_inc(s_add1, 1)
                if g + 1 < GROUPS:
                    copy_o(g + 1)
                dve.wait_ge(s_add1, g + 1)
                for s in range(GT):
                    nc.vector.bn_stats(st2[:, s, :], x1[:, GT * g + s, :]).then_inc(s_stat2, 1)
                dve.wait_ge(s_stat2, GT * (g + 1))
                for s in range(GT):
                    ins = nc.vector.bn_aggr(mv2[:, g % 2, s, :], st2[:, s, :])
                ins.then_inc(s_agg2, 1)
                if g >= 1:
                    copy_h2(g - 1)
                dve.wait_ge(s_rstd2, g + 1)
                for s in range(GT):
                    ins = nc.vector.tensor_scalar(h2[:, g % 2, s, :], x1[:, GT * g + s, :], mv2[:, g % 2, s, 0:1],
                                                  rstd2[:, g % 2, s:s + 1], ALU.subtract, ALU.mult)
                ins.then_inc(s_h2, 1)
            copy_h2(GROUPS - 1)

            dve.sem_inc(s_xc[0], 1)
            dve.sem_inc(s_xc[1], 1)
            dve.sem_inc(s_x2, 2)

            def cross_low(j, u):
                for n, (h0, h1) in enumerate(XBANKS):
                    dve.wait_ge(s_s2, j * 6 + (3 * u + n + 7))
                    nc.vector.tensor_reduce(xlow[:, u, h0:h1],
                                            ps[:, n, 0:(h1 - h0) * NCTX].rearrange("p (h k) -> p h k", k=NCTX),
                                            AX.X, ALU.min).then_inc(s_xl, 1)

            def cross_normalise(j, u):
                for n, (h0, h1) in enumerate(XBANKS):
                    dve.wait_ge(s_xe, j * 6 + (3 * u + n + 4))
                    nc.vector.reciprocal(xrec[:, h0:h1], xsum[:, u, h0:h1]).then_inc(s_xs, 1)
                    dve.wait_ge(s_xs, j * 6 + (3 * u + n + 1))
                    p3 = xp[:, u, h0 * NCTX:h1 * NCTX].rearrange("p (h k) -> p h k", k=NCTX)
                    nc.vector.tensor_tensor(p3, p3, xrec[:, h0:h1].unsqueeze(2).broadcast_to([P, h1 - h0, NCTX]),
                                            ALU.mult).then_inc(s_xn, 1)

            def cross_step(j, u, following):
                for n in range(2):
                    dve.wait_ge(s_xt, j * 6 + (3 * u + n + 7))
                    dve.wait_ge(s_xu, j * 2 + (u + 1))
                    nc.vector.tensor_copy(xpT[:, u, 4 * n:4 * n + 4, :].rearrange("p c n -> p (c n)"), ps[:, 3 + n, :]
                                          ).then_inc(s_xc[n], 1)
                if following is not None:
                    cross_low(*following)
                    cross_normalise(*following)
                dve.wait_ge(s_xu, j * 2 + (u + 3))
                xt = x1[:, bass.ds(j + TPB * u, 1), :].rearrange("p o d -> p (o d)")
                nc.vector.tensor_tensor(xt, ps[:, 6 + u, 0:D], xt, ALU.add).then_inc(s_x2, 1)
                dve.wait_ge(s_x2, j * 2 + (u + 3))
                nc.vector.bn_stats(st3[:, :], xt).then_inc(s_stat3, 1)
                dve.wait_ge(s_stat3, j * 2 + (u + 1))
                dve.sem_inc(s_go["dve"], 1)
                nc.vector.bn_aggr(mvs[:, :], st3[:, :]).then_inc(s_agg3, 1)
                dve.wait_ge(s_agg3, j * 2 + (u + 1))
                nc.vector.tensor_copy(mv3[:, bass.ds(j + TPB * u, 1), :].rearrange("p o d -> p (o d)"), mvs[:, :]
                                      ).then_inc(s_mv3, 1)

            dve.wait_ge(s_x1b, GROUPS)
            cross_low(0, 0)
            cross_normalise(0, 0)
            with dve.Fori(0, TPB - 1) as j:
                cross_step(j, 0, (j, 1))
                cross_step(j, 1, (j + 1, 0))
            cross_step(TPB - 1, 0, (TPB - 1, 1))
            cross_step(TPB - 1, 1, None)

            dve.sem_inc(s3_w, 1)
            dve.sem_inc(s3_acc, 9)
            nc.vector.memset(count[:, :], 0.0).then_inc(s_cnt0, 1)
            dve.wait_ge(s_cnt0, 1)
            dve.wait_ge(s_we, 16 * 6)
            dve.wait_ge(s_rstd3, 1)

            def rows(j, v):
                dve.wait_ge(s3_t, j + 1)
                for u in range(2):
                    t = 2 * j + u
                    ins = nc.vector.tensor_scalar(h3[:, v, u, :],
                                                  x1[:, bass.ds(t, 1), :].rearrange("p o d -> p (o d)"),
                                                  mv3[:, bass.ds(t, 1), 0:1].rearrange("p o d -> p (o d)"),
                                                  rstd3[:, bass.ds(t, 1)], ALU.subtract, ALU.mult)
                ins.then_inc(s3_h, 1)

            def choose(j, v):
                step = [0]

                def link(ins):
                    step[0] += 1
                    ins.then_inc(s3_r, 1)
                    dve.wait_ge(s3_r, j * RSTEPS + step[0])

                lg = ps[:, 5, 0:2 * EXPERTS].rearrange("p (u e) -> p u e", e=EXPERTS)
                e_row = e8[:, :].unsqueeze(1).broadcast_to([P, 2, EXPERTS])
                dve.wait_ge(s3_l, j + 1)
                link(nc.vector.tensor_reduce(top[:, :], lg, AX.X, ALU.max))
                link(nc.vector.tensor_tensor(below[:, :, :], lg, top[:, :].unsqueeze(2).broadcast_to([P, 2, EXPERTS]),
                                             ALU.subtract))
                link(nc.vector.scalar_tensor_tensor(out=cand[:, :, :], in0=below[:, :, :], scalar=0.0, in1=e_row,
                                                    op0=ALU.is_ge, op1=ALU.mult))
                link(nc.vector.tensor_reduce(first_e[:, :], cand[:, :, :], AX.X, ALU.min))
                nc.vector.tensor_tensor(chosen[:, v, :, :], e_row,
                                        first_e[:, :].unsqueeze(2).broadcast_to([P, 2, EXPERTS]), ALU.is_equal
                                        ).then_inc(s3_o, 1)
                dve.wait_ge(s3_e, j + 1)
                link(nc.vector.tensor_reduce(den[:, :], expb[:, :, :], AX.X, ALU.add))
                link(nc.vector.reciprocal(gate[:, :], den[:, :]))
                dve.wait_ge(s3_o, j + 1)

            def weigh(j, v):
                step = [6]

                def link(ins):
                    step[0] += 1
                    ins.then_inc(s3_r, 1)
                    dve.wait_ge(s3_r, j * RSTEPS + step[0])

                dve.wait_ge(s3_c, j + 1)
                at = ps[:, 5, 16:16 + 2 * EXPERTS].rearrange("p (u e) -> p u e", e=EXPERTS)
                link(nc.vector.tensor_tensor(place[:, :, :], at, count[:, :].unsqueeze(1).broadcast_to([P, 2, EXPERTS]),
                                             ALU.add))
                link(nc.vector.tensor_tensor(count[:, :], ps[:, 5, 32:32 + EXPERTS], count[:, :], ALU.add))
                link(nc.vector.scalar_tensor_tensor(out=kept[:, :, :], in0=place[:, :, :], scalar=float(CAP),
                                                    in1=chosen[:, v, :, :], op0=ALU.is_lt, op1=ALU.mult))
                link(nc.vector.tensor_tensor(expw[:, :, :], kept[:, :, :],
                                             gate[:, :].unsqueeze(2).broadcast_to([P, 2, EXPERTS]), ALU.mult))
                nc.vector.tensor_copy(wgt[:, v, :, :], expw[:, :, :]).then_inc(s3_w, 1)
                dve.wait_ge(s3_w, j + 2)

            def add_bias(j, u):
                dve.wait_ge(s3_b, j + 1)
                xt = x1[:, bass.ds(2 * j + u, 1), :].rearrange("p o d -> p (o d)")
                nc.vector.tensor_tensor(xt, ps[:, 7, u * D:(u + 1) * D], xt, ALU.add).then_inc(s3_acc, 1)
                dve.wait_ge(s3_acc, j * 18 + (9 * u + 10))

            def add_experts(j, v, u, q):
                dve.wait_ge(s3_y, j * 8 + (4 * u + q + 17))
                xt = x1[:, bass.ds(2 * j + u, 1), :].rearrange("p o d -> p (o d)")
                for e in range(2):
                    nc.vector.scalar_tensor_tensor(out=xt, in0=ps[:, q, e * D:(e + 1) * D],
                                                   scalar=wgt[:, v, u, 2 * q + e:2 * q + e + 1], in1=xt,
                                                   op0=ALU.mult, op1=ALU.add).then_inc(s3_acc, 1)
                    dve.wait_ge(s3_acc, j * 18 + (9 * u + 2 * q + e + 11))

            def experts_step(j, v, last):
                if not last:
                    rows(j + 1, 1 - v)
                add_bias(j, 0)
                for q in range(4):
                    add_experts(j, v, 0, q)
                add_bias(j, 1)
                add_experts(j, v, 1, 0)
                if not last:
                    choose(j + 1, 1 - v)
                add_experts(j, v, 1, 1)
                add_experts(j, v, 1, 2)
                if not last:
                    weigh(j + 1, 1 - v)
                add_experts(j, v, 1, 3)

            rows(0, 0)
            choose(0, 0)
            weigh(0, 0)
            with dve.Fori(0, TILES // 4 - 1) as jj:
                experts_step(2 * jj, 0, False)
                experts_step(2 * jj + 1, 1, False)
            experts_step(TILES // 2 - 2, 0, False)
            experts_step(TILES // 2 - 1, 1, True)

        @block.tensor
        def _(pe):
            pe.sem_inc(s_av, 2)
            pe.sem_inc(s_o, 1)
            pe.wait_ge(s_cst, 80)
            pe.wait_ge(s_w, 48)

            def turn_normalised(g):
                pe.wait_ge(s_h, g + 1)
                for kc in range(KC):
                    if g >= 1:
                        pe.wait_ge(s_tc[kc], g)
                    for s in range(GT):
                        mm = pe.transpose(ps[:, T_BANK + kc, s * P:(s + 1) * P], hg[:, s, kc * P:(kc + 1) * P],
                                          idf[:, :])
                    mm.then_inc(s_t[kc], 1)

            turn_normalised(0)
            for g in range(GROUPS):
                for kc in range(KC):
                    pe.wait_ge(s_tc[kc], g + 1)
                for j in range(4):
                    if g >= 1:
                        pe.wait_ge(s_full, 4 * (g - 1) + j + 1)
                    w = (wq_sb, wk_sb)[j // 2]
                    for kc in range(KC):
                        mm = pe.matmul(ps[:, S_BANK + j, :], w[:, kc, (j % 2) * P:(j % 2 + 1) * P],
                                       hT[:, g % 2, kc, :], start=(kc == 0), stop=(kc == KC - 1))
                    mm.then_inc(s_proj, 1)
                if g + 1 < GROUPS:
                    turn_normalised(g + 1)
                for half_g in range(2):
                    if g >= 1:
                        pe.wait_ge(s_vc, 2 * (g - 1) + half_g + 1)
                    for s in range(2):
                        for kc in range(KC):
                            mm = pe.matmul(ps[:, R_BANK + half_g, s * D:(s + 1) * D],
                                           hT[:, g % 2, kc, (2 * half_g + s) * P:(2 * half_g + s + 1) * P],
                                           wv_sb[:, kc, :], start=(kc == 0), stop=(kc == KC - 1))
                    mm.then_inc(s_v, 1)
            pe.wait_ge(s_full, 4 * GROUPS)
            pe.wait_ge(s_vc, 2 * GROUPS)
            pe.wait_ge(s_xin, 16 * 5)
            for n, what in enumerate(units):
                if n >= 4:
                    pe.wait_ge(s_xwc[n % 2], (n - 4) // 2 + 1)
                if n == XKV:
                    for k in range(2):
                        pe.wait_ge(s_xwc[k], (XKV + 1 - k) // 2)
                bank = S_BANK + n % 4
                if what[0] in "kv":
                    w = xk_w if what[0] == "k" else xv_w
                    for m in range(what[1], what[2]):
                        at = (m - what[1]) * CK
                        for kc in range(2):
                            mm = pe.matmul(ps[:, bank, at:at + CK], w[:, kc, m * P:(m + 1) * P], ctx_sb[:, kc, :],
                                           start=(kc == 0), stop=(kc == 1))
                elif what[0] == "g":
                    _, kc, hs = what
                    for at, h in enumerate(hs):
                        rows = slice(XD * (h % 2), XD * (h % 2) + XD)
                        mm = pe.matmul(ps[:, bank, at * CK:(at + 1) * CK],
                                       xq_w[rows, h // 2, kc * P:(kc + 1) * P], xkT[rows, h // 2, :],
                                       start=True, stop=True)
                else:
                    _, b_, hs = what
                    for at, h in enumerate(hs):
                        rows = slice(XD * (h % 2), XD * (h % 2) + XD)
                        mm = pe.matmul(ps[0:NCTX, bank, at * D:(at + 1) * D],
                                       xvT[rows, h // 2, b_ * NCTX:(b_ + 1) * NCTX], xo_w[rows, h // 2, :],
                                       start=True, stop=True)
                mm.then_inc(s_xw, 1)
            for k in range(2):
                pe.wait_ge(s_xwc[k], (XUNITS + 1 - k) // 2)
            pe.wait_ge(s_tab, 16 * 11)

            def rel_scores(b, i, pair):
                pe.wait_ge(s_rc, b * (TPB * PAIRS) + i * PAIRS + pair + 1)
                for s in range(2):
                    mm = pe.matmul(ps[:, R_BANK, s * REL:(s + 1) * REL],
                                   q6[:, bass.ds(2 * pair + s, 1), i * P:(i + 1) * P].rearrange("p o n -> p (o n)"),
                                   p6[:, :], start=True, stop=True)
                mm.then_inc(s_r, 1)

            def scores(b, i, h):
                pe.wait_ge(s_exp, head_no(b, i, h) + 1)
                K = (i + 1) * P
                for n0 in range(0, K, BANK):
                    n1 = min(K, n0 + BANK)
                    mm = pe.matmul(score(h, K)[:, n0:n1], q6[:, h, i * P:(i + 1) * P], k6[:, h, n0:n1],
                                   start=True, stop=True)
                mm.then_inc(s_s, 1)

            def transposes(b, i, h):
                pe.wait_ge(s_exp, head_no(b, i, h) + 3)
                for bank, k0, k1 in banks_of(i, h):
                    pe.wait_ge(s_tc[bank], use(b, i, h) - 1)
                    for kb in range(k0, k1):
                        mm = pe.transpose(ps[:, T_BANK + bank, (kb - k0) * P:(kb - k0 + 1) * P],
                                          prob[:, h % 2, kb * P:(kb + 1) * P], idf[:, :])
                    mm.then_inc(s_t[bank], 1)

            def zero_out(b, i):
                pe.wait_ge(s_on, b * TPB + (i + 1))
                pe.matmul(ps[:, O_BANK, :], zb[:, 0:P], zb[:, :], start=True, stop=False, skip_group_check=True)

            def values(b, i, c, k0, k1):
                for bank in range(2):
                    pe.wait_ge(s_tc[bank], use(b, i, 4 * c + 3))
                for kb in range(k0, k1):
                    for k in range(4):
                        h = 4 * c + k
                        probs = pT[:, c % 2, k, kb, :] if kb < i - 2 else bandT[:, kb + 2 - i, h, :]
                        mm = pe.matmul(ps[32 * k:32 * k + HD, O_BANK, c * P:(c + 1) * P],
                                       v_b[:, kb, h * HD:(h + 1) * HD], probs,
                                       start=False, stop=False, skip_group_check=True)
                if k1 == i + 1:
                    mm.then_inc(s_av, 1)

            def rel_values(b, i):
                first = max(0, 2 - i)
                for bank in range(2):
                    pe.wait_ge(s_tc[bank], use_values(b, i) - 1)
                    for g in range(8):
                        for blk in range(first, 3):
                            for e in range(2):
                                q = 8 * (8 * bank + g) + 4 * e
                                mm = pe.matmul(ps[64 * e:64 * e + 64, T_BANK + bank, g * 64:(g + 1) * 64].rearrange(
                                                   "p (h q) -> p h q", q=4),
                                               pvt[:, blk, (P - 4 - q) * HD:(P - q) * HD], bandT[:, blk, :, q:q + 4],
                                               start=(blk == first), stop=(blk == 2))
                    mm.then_inc(s_t[bank], 1)

            def fold_values(b, i):
                for bank in range(2):
                    pe.wait_ge(s_tc[bank], use_values(b, i))
                for k in range(4):
                    for e in range(2):
                        to = ps[32 * k:32 * k + HD, O_BANK, :].rearrange("p (c g e q) -> p c g e q", c=QUADS, e=2, q=4)
                        mm = pe.matmul(to[:, :, :, e, :], fold_sb[:, e, :],
                                       picked[:, k:HEADS:4, :].rearrange("p c (g q) -> p c g q", q=4),
                                       start=False, stop=True, skip_group_check=True)
                mm.then_inc(s_o, 1)

            def turn_back(b, i):
                pe.wait_ge(s_oc, b * TPB + (i + 1))
                for c in range(QUADS):
                    mm = pe.transpose(ps[:, O_BANK, c * P:(c + 1) * P], oTs[:, c * P:(c + 1) * P], idf[:, :])
                mm.then_inc(s_of, 1)

            with pe.Fori(0, BATCH) as b:
                pe.wait_ge(s_qk, b * (16 * 2 * len(Q_SLOTS)) + 16 * 2 * len(Q_SLOTS))
                pe.wait_ge(s_vb, b + 1)
                pe.sem_inc(s_go["pe"], 1)
                with pe.Fori(0, PAIRS) as pair:
                    rel_scores(b, 0, pair)
                scores(b, 0, 0)
                scores(b, 0, 1)
                pe.wait_ge(s_z, 1)
                for i in range(TPB):
                    for h in range(HEADS):
                        if ahead(i, h):
                            scores(b, *ahead(i, h))
                        transposes(b, i, h)
                        if h % 2 == 1 and i + 1 < TPB:
                            rel_scores(b, i + 1, h // 2)
                        c, k = h // 4, h % 4
                        if c > 0:
                            if h == 4:
                                zero_out(b, i)
                            k0, k1 = (i + 1) * k // 4, (i + 1) * (k + 1) // 4
                            if k1 > k0:
                                values(b, i, c - 1, k0, k1)
                        elif i > 0 and h == 0:
                            fold_values(b, i - 1)
                        elif i > 0 and h == 2:
                            turn_back(b, i - 1)
                    values(b, i, QUADS - 1, 0, i + 1)
                    rel_values(b, i)
                fold_values(b, TPB - 1)
                turn_back(b, TPB - 1)

            pe.wait_ge(s_on, TILES + 1)
            pe.wait_ge(s_wo, 32)

            def turn_o(g):
                for kc in range(KC):
                    pe.wait_ge(s_tc[kc], LAST_USE + g)
                    for s in range(GT):
                        mm = pe.transpose(ps[:, T_BANK + kc, s * P:(s + 1) * P],
                                          x1[:, GT * g + s, kc * P:(kc + 1) * P], idf[:, :])
                    mm.then_inc(s_t[kc], 1)

            def turn_h2(g):
                pe.wait_ge(s_h2, g + 1)
                for kc in range(KC):
                    if g >= 1:
                        pe.wait_ge(s_h2tc[kc], g)
                    for s in range(GT):
                        mm = pe.transpose(ps[:, kc, s * P:(s + 1) * P], h2[:, g % 2, s, kc * P:(kc + 1) * P],
                                          idf[:, :])
                    mm.then_inc(s_h2t[kc], 1)

            turn_o(0)
            for g in range(GROUPS):
                for kc in range(KC):
                    pe.wait_ge(s_tc[kc], LAST_USE + g + 1)
                if g >= 1:
                    pe.wait_ge(s_add1, g)
                for s in range(GT):
                    for kc in range(KC):
                        mm = pe.matmul(ps[:, 6 + s // 2, (s % 2) * D:(s % 2 + 1) * D],
                                       oT[:, g % 2, kc, s * P:(s + 1) * P], wo_sb[:, kc, :],
                                       start=(kc == 0), stop=(kc == KC - 1))
                mm.then_inc(s_att, 1)
                if g + 1 < GROUPS:
                    turn_o(g + 1)
                if g >= 1:
                    turn_h2(g - 1)
            turn_h2(GROUPS - 1)
            for kc in range(KC):
                pe.wait_ge(s_h2tc[kc], GROUPS)

            pe.sem_inc(s_s2, 6)
            pe.sem_inc(s_xt, 6)
            pe.sem_inc(s_xu, 2)
            pe.wait_ge(s_g, 16)
            pe.wait_ge(s_u, 64)

            def cross_scores(j, u):
                pe.wait_ge(s_h2s, j * 2 + (u + 1))
                for n, (h0, h1) in enumerate(XBANKS):
                    pe.wait_ge(s_xe, j * 6 + (3 * u + n + 1))
                    for kc in range(KC):
                        mm = pe.matmul(ps[:, n, 0:(h1 - h0) * NCTX], h2s[:, u, kc, :],
                                       g_sb[:, kc, u, h0 * NCTX:h1 * NCTX], start=(kc == 0), stop=(kc == KC - 1))
                    mm.then_inc(s_s2, 1)

            def cross_step(j, u, following):
                normalised = 0
                for n in range(3):
                    pe.wait_ge(s_xc[n], j * 2 + (u + 1))
                    for c in range(4 * n, min(4 * n + 4, XCH)):
                        w = P if c < XCH - 1 else XTAIL
                        need = max(m for m, (h0, h1) in enumerate(XBANKS) if h0 * NCTX < c * P + w) + 1
                        if need > normalised:
                            pe.wait_ge(s_xn, j * 6 + (3 * u + need))
                            normalised = need
                        mm = pe.transpose(ps[0:w, 3 + n, (c - 4 * n) * P:(c - 4 * n + 1) * P],
                                          xp[:, u, c * P:c * P + w], idf[:, :])
                    mm.then_inc(s_xt, 1)
                if following is not None:
                    cross_scores(*following)
                for n in range(3):
                    pe.wait_ge(s_xc[n], j * 2 + (u + 2))
                pe.wait_ge(s_x2, j * 2 + (u + 1))
                for c in range(XCH):
                    w = P if c < XCH - 1 else XTAIL
                    mm = pe.matmul(ps[:, 6 + u, 0:D], xpT[0:w, u, c, :], u_sb[0:w, u, c, :],
                                   start=(c == 0), stop=(c == XCH - 1))
                mm.then_inc(s_xu, 1)

            cross_scores(0, 0)
            with pe.Fori(0, TPB - 1) as j:
                cross_step(j, 0, (j, 1))
                cross_step(j, 1, (j + 1, 0))
            cross_step(TPB - 1, 0, (TPB - 1, 1))
            cross_step(TPB - 1, 1, None)

            pe.sem_inc(s3_t, 1)
            pe.sem_inc(s3_y, 16)
            pe.wait_ge(s_we, 16 * 6)
            pe.wait_ge(s_x2, TILES + 2)

            def turn_rows(j, v):
                pe.wait_ge(s3_h, j + 1)
                pe.wait_ge(s3_tc, j + 1)
                for kc in range(KC):
                    for u in range(2):
                        at = (2 * kc + u) * P
                        mm = pe.transpose(ps[:, 4, at:at + P], h3[:, v, u, kc * P:(kc + 1) * P], idf[:, :])
                mm.then_inc(s3_t, 1)

            def logits(j, v):
                pe.wait_ge(s3_tc, j + 2)
                pe.wait_ge(s3_w, j + 1)
                for u in range(2):
                    for kc in range(KC):
                        at = (2 * kc + u) * P
                        mm = pe.matmul(ps[:, 5, u * EXPERTS:(u + 1) * EXPERTS], h3T[:, v, at:at + P], wg_sb[:, kc, :],
                                       start=(kc == 0), stop=(kc == KC - 1))
                mm.then_inc(s3_l, 1)

            def counts(j, v):
                pe.wait_ge(s3_o, j + 1)
                pe.matmul(ps[:, 5, 16:24], earlier_sb[:, :], chosen[:, v, 0, :], start=True, stop=True)
                pe.matmul(ps[:, 5, 24:32], earlier_sb[:, :], chosen[:, v, 1, :], start=True, stop=False)
                pe.matmul(ps[:, 5, 24:32], ones_sb[:, :], chosen[:, v, 0, :], start=False, stop=True)
                pe.matmul(ps[:, 5, 32:40], ones_sb[:, :], chosen[:, v, 0, :], start=True, stop=False)
                pe.matmul(ps[:, 5, 32:40], ones_sb[:, :], chosen[:, v, 1, :], start=False, stop=True
                          ).then_inc(s3_c, 1)

            def turn_weights(j, v):
                pe.wait_ge(s3_w, j + 2)
                pe.wait_ge(s3_wc, j + 1)
                for u in range(2):
                    mm = pe.transpose(ps[0:EXPERTS, 6, u * P:(u + 1) * P], wgt[:, v, u, :], idf[:, :])
                mm.then_inc(s3_wt, 1)

            def biases(j, v):
                pe.wait_ge(s3_wc, j + 2)
                pe.wait_ge(s3_acc, j * 18 + 1)
                for u in range(2):
                    mm = pe.matmul(ps[:, 7, u * D:(u + 1) * D], wgtT[:, v, u * P:(u + 1) * P], be_sb[:, :],
                                   start=True, stop=True)
                mm.then_inc(s3_b, 1)

            def experts_out(j, v, u, q):
                pe.wait_ge(s3_acc, j * 18 + (9 * u + 2 * q + 3))
                for kc in range(KC):
                    at = (2 * kc + u) * P
                    mm = pe.matmul(ps[:, q, :], h3T[:, v, at:at + P], we_sb[:, kc, q * BANK:(q + 1) * BANK],
                                   start=(kc == 0), stop=(kc == KC - 1))
                mm.then_inc(s3_y, 1)

            def experts_step(j, v, last):
                experts_out(j, v, 0, 0)
                biases(j, v)
                for q in range(1, 4):
                    experts_out(j, v, 0, q)
                if not last:
                    turn_rows(j + 1, 1 - v)
                experts_out(j, v, 1, 0)
                if not last:
                    logits(j + 1, 1 - v)
                experts_out(j, v, 1, 1)
                experts_out(j, v, 1, 2)
                if not last:
                    counts(j + 1, 1 - v)
                experts_out(j, v, 1, 3)
                if not last:
                    turn_weights(j + 1, 1 - v)

            turn_rows(0, 0)
            logits(0, 0)
            counts(0, 0)
            turn_weights(0, 0)
            with pe.Fori(0, TILES // 4 - 1) as jj:
                experts_step(2 * jj, 0, False)
                experts_step(2 * jj + 1, 1, False)
            experts_step(TILES // 2 - 2, 0, False)
            experts_step(TILES // 2 - 1, 1, True)


def kernel(**inputs):
    import numpy as _np
    import concourse.bacc as _bacc
    from concourse import mybir as _mybir
    from concourse.bass_utils import run_bass_kernel_spmd as _run

    a = {k: _np.asarray(v) for k, v in inputs.items()}
    arange = _np.arange
    arrays = {
        "x": a["x"].reshape(TOKENS, D),
        "ctxT": a["ctx_768"].reshape(BATCH * NCTX, DCTX).T,
        "wqT": a["L0_attn_Wq"].T,
        "wkT": a["L0_attn_Wk"].T,
        "wvT": a["L0_attn_Wv"].T,
        "woT": a["L0_attn_Wo"].T,
        "pekT": a["L0_attn_pek"].T,
        "pek0": _np.tile(a["L0_attn_pek"][0], P // HD).reshape(P, 1),
        "pev": a["L0_attn_pev"],
        "xwqT": a["L0_xattn_Wq"].T,
        "xwk": a["L0_xattn_Wk"],
        "xwv": a["L0_xattn_Wv"],
        "xwo": a["L0_xattn_Wo"],
        "xbo": a["L0_xattn_bo"].reshape(1, D),
        "wg": a["L0_ffn_wg"],
        "weT": a["L0_ffn_W"].transpose(2, 0, 1),
        "be": a["L0_ffn_b"],
        "ident": _np.eye(P, dtype=_np.float32),
        "ones": _np.ones((P, P), _np.float32),
        "diag": (3 - arange(P)[:, None] // HD % 4 == arange(4 * HEADS)[None, :] % 4).astype(_np.float32),
        "fold": _np.stack([(arange(P)[:, None] % HD == arange(HD)[None, :]) & (arange(P)[:, None] // 64 == e)
                           for e in range(2)], axis=1).astype(_np.float32),
        "earlier": (arange(P)[:, None] < arange(P)[None, :]).astype(_np.float32),
        "experts": _np.broadcast_to(arange(EXPERTS, dtype=_np.float32) - EXPERTS, (P, EXPERTS)),
    }
    nc = _bacc.Bacc("TRN2", target_bir_lowering=False, num_devices=1)
    ins, args = {}, []
    for name, v in arrays.items():
        v = _np.ascontiguousarray(v)
        ins[f"in_{name}"] = v
        args.append(nc.dram_tensor(f"in_{name}", v.shape, _mybir.dt.from_np(v.dtype), kind="ExternalInput").ap())
    out = nc.dram_tensor("out_0", (TOKENS, D), _mybir.dt.float32, kind="ExternalOutput").ap()
    decoder_layer(nc, *args, out)
    r = _run(nc, [ins], core_ids=[0])
    return r.results[0]["out_0"].reshape(BATCH, SEQ, D)
```

```python
from contextlib import ExitStack

import concourse.bass as bass
from concourse import mybir

F32 = mybir.dt.float32
BF16 = mybir.dt.bfloat16
ALU = mybir.AluOpType
ACT = mybir.ActivationFunctionType
AX = mybir.AxisListType

P = 128
BATCH, SEQ, D = 2, 1024, 256
TOKENS = BATCH * SEQ
TILES = TOKENS // P
TPB = SEQ // P
KC = D // P
HEADS, HD = 16, 16
PAIRS = HEADS // 2
QUADS = HEADS // 4
SCALE = HD ** 0.5
REL = 256
TERMS = 3
Q_SLOTS = (0, 0, 1, 1, 0, 2)
K_SLOTS = (0, 1, 0, 1, 2, 0)
STACK = len(Q_SLOTS) * HD
BAND = 3 * P
ROW = 127 + BAND
XH, XD = 16, 64
INNER = XH * XD
NCTX, DCTX = 77, 192
CTXC = DCTX // 2
XBANKS = ((0, 6), (6, 12), (12, 16))
XK = XH * NCTX
XCH = (XK + P - 1) // P
XTAIL = XK - (XCH - 1) * P
RSTEPS = 10
EXPERTS = 8
CAP = TOKENS // EXPERTS
EPS = 1e-5
BIG = 1e30
GROUPS = 4
GT = TOKENS // GROUPS // P
BANK = 512


def decoder_layer(nc, x, ctxT, wqT, wkT, wvT, woT, pekT, pek0, pev, xwqT, xwk, xwv, xwo, xbo, wg, weT, be,
                  ident, ones, diag, fold, earlier, experts, out):
    nc.disable_value_cache = True
    qparts = nc.dram_tensor("qparts", (TERMS, D, TOKENS), BF16)
    kparts = nc.dram_tensor("kparts", (TERMS, D, TOKENS), BF16)
    pparts = nc.dram_tensor("pparts", (TERMS, HD, REL), BF16)
    pvrows = nc.dram_tensor("pvrows", (ROW + 1, HD), F32)
    rel = nc.dram_tensor("rel", (2 * HEADS, P, ROW), F32)
    gmat = nc.dram_tensor("gmat", (P, KC, BATCH, XK), F32)
    umat = nc.dram_tensor("umat", (BATCH, XK, D), F32)

    ctx = ExitStack()
    with ctx:
        def sb(name, shape, dt, where=ctx):
            return where.enter_context(nc.sbuf_tensor(name, shape, dt))

        def sem(name):
            return ctx.enter_context(nc.semaphore(name))

        ps = ctx.enter_context(nc.psum_tensor("ps", [P, 8, BANK], F32))
        S_BANK, T_BANK, R_BANK, O_BANK = 0, 4, 6, 7

        idf = sb("idf", [P, P], F32)
        x1 = sb("x1", [P, TILES, D], F32)
        half = sb("half", [P, 1], F32)

        v_b = sb("v_b", [P, TPB, D], F32)

        proj = ExitStack()
        pk0 = sb("pk0", [P, 1], F32, proj)
        pev0 = sb("pev0", [P, HD], F32, proj)
        xg = sb("xg", [P, 2, GT, D], F32, proj)
        hg = sb("hg", [P, GT, D], F32, proj)
        hT = sb("hT", [P, 2, KC, BANK], F32, proj)
        wq_sb = sb("wq_sb", [P, KC, D], F32, proj)
        wk_sb = sb("wk_sb", [P, KC, D], F32, proj)
        wv_sb = sb("wv_sb", [P, KC, D], F32, proj)
        st1 = sb("st1", [P, GT, 6], F32, proj)
        mv1 = sb("mv1", [P, GT, 2], F32, proj)
        rstd1 = sb("rstd1", [P, GT], F32, proj)
        full = sb("full", [P, 4, BANK], F32, proj)
        rest = sb("rest", [P, 4, BANK], F32, proj)
        parts = sb("parts", [P, 4, TERMS, BANK], BF16, proj)
        pk_in = sb("pk_in", [HD, REL + 1], F32, proj)
        pk_d = sb("pk_d", [HD, REL], F32, proj)
        pk_r = sb("pk_r", [HD, REL], F32, proj)
        pk_parts = sb("pk_parts", [HD, TERMS, REL], BF16, proj)
        pv_in = sb("pv_in", [P, 2, HD], F32, proj)
        zrow = sb("zrow", [P, P], F32, proj)
        brow = sb("brow", [P, P - 1], F32, proj)
        proj.close()

        att = ExitStack()
        q6 = sb("q6", [STACK, 2, HEADS, P], BF16, att)
        k6 = sb("k6", [STACK, HEADS, SEQ], BF16, att)
        p6 = sb("p6", [STACK, REL], BF16, att)
        pvt = sb("pvt", [P, 3, P * HD], F32, att)
        diag_sb = sb("diag_sb", [P, HEADS * 4], F32, att)
        fold_sb = sb("fold_sb", [P, 2, HD], F32, att)

        fw = ExitStack()
        xk_w = sb("xk_w", [CTXC, 2, INNER], F32, fw)
        xv_w = sb("xv_w", [CTXC, 2, INNER], F32, fw)
        ctx_sb = sb("ctx_sb", [CTXC, 2, BATCH * NCTX], F32, fw)
        xq_w = sb("xq_w", [P, INNER // P, D], F32, fw)
        xkT = sb("xkT", [P, INNER // P, BATCH * NCTX], F32, fw)
        g_out = sb("g_out", [P, KC, BATCH, XK], F32, fw)
        xvT = sb("xvT", [P, INNER // P, BATCH * NCTX], F32, fw)
        xo_w = sb("xo_w", [P, INNER // P, D], F32, fw)
        u_out = sb("u_out", [NCTX, BATCH, XH, D], F32, fw)
        fw.close()

        rel_out = sb("rel_out", [P, 2, 4, REL], F32, att)
        prob = sb("prob", [P, 2 * SEQ], F32, att)
        bias = sb("bias", [P, HEADS, BAND], F32, att)
        pT = sb("pT", [P, 2, 4, TPB - 3, P], F32, att)
        bandT = sb("bandT", [P, 2, 3, HEADS, P], F32, att)
        far = sb("far", [P, 2], F32, att)
        low = sb("low", [P, 4], F32, att)
        rsum = sb("rsum", [P, 2, HEADS], F32, att)
        rrec = sb("rrec", [P, 2, HEADS], F32, att)
        picked = sb("picked", [P, HEADS, P // 2], F32, att)
        oTs = sb("oTs", [P, 2, BANK], F32, att)
        zb = sb("zb", [P, BANK], BF16, att)
        att.close()

        late = ExitStack()
        wo_sb = sb("wo_sb", [P, KC, D], F32, late)
        xr = sb("xr", [P, 2, GT, D], F32, late)
        oT = sb("oT", [P, 2, KC, BANK], F32, late)
        bo = sb("bo", [P, D], F32, late)
        h2 = sb("h2", [P, 2, GT, D], F32, late)
        h2T = sb("h2T", [P, KC, TOKENS], F32, late)
        st2 = sb("st2", [P, GT, 6], F32, late)
        mv2 = sb("mv2", [P, 2, GT, 2], F32, late)
        rstd2 = sb("rstd2", [P, 2, GT], F32, late)
        g_sb = sb("g_sb", [P, KC, BATCH, XK], F32, late)
        u_sb = sb("u_sb", [P, BATCH, XCH, D], F32, late)
        h2s = sb("h2s", [P, 2, KC, P], F32, late)
        xlow = sb("xlow", [P, 2, XH], F32, late)
        xsum = sb("xsum", [P, 2, XH], F32, late)
        xrec = sb("xrec", [P, XH], F32, late)
        xp = sb("xp", [P, 2, XK], F32, late)
        xpT = sb("xpT", [P, 2, XCH, P], F32, late)
        st3 = sb("st3", [P, 6], F32, late)
        mvs = sb("mvs", [P, 2], F32, late)
        mv3 = sb("mv3", [P, TILES, 2], F32, late)
        rstd3 = sb("rstd3", [P, TILES], F32, late)
        we_sb = sb("we_sb", [P, KC, EXPERTS * D], F32, late)
        be_sb = sb("be_sb", [EXPERTS, D], F32, late)
        wg_sb = sb("wg_sb", [P, KC, EXPERTS], F32, late)
        earlier_sb = sb("earlier_sb", [P, P], F32, late)
        ones_sb = sb("ones_sb", [P, P], F32, late)
        earlier_b = sb("earlier_b", [P, P], BF16, late)
        ones_b = sb("ones_b", [P, P], BF16, late)
        e8 = sb("e8", [P, EXPERTS], F32, late)
        h3 = sb("h3", [P, 2, 2, D], F32, late)
        h3T = sb("h3T", [P, 2, KC * 2 * P], F32, late)
        top = sb("top", [P, 2], F32, late)
        below = sb("below", [P, 2, EXPERTS], F32, late)
        expb = sb("expb", [P, 2, EXPERTS], F32, late)
        den = sb("den", [P, 2], F32, late)
        gate = sb("gate", [P, 2], F32, late)
        cand = sb("cand", [P, 2, EXPERTS], F32, late)
        first_e = sb("first_e", [P, 2], F32, late)
        chosen = sb("chosen", [P, 2, 2, EXPERTS], BF16, late)
        place = sb("place", [P, 2, EXPERTS], F32, late)
        count = sb("count", [P, EXPERTS], F32, late)
        kept = sb("kept", [P, 2, EXPERTS], F32, late)
        expw = sb("expw", [P, 2, EXPERTS], F32, late)
        wgt = sb("wgt", [P, 2, 2, EXPERTS], F32, late)
        wgtT = sb("wgtT", [EXPERTS, 2, 2 * P], F32, late)
        late.close()

        s_cst, s_w, s_set = sem("s_cst"), sem("s_w"), sem("s_set")
        s_x = [sem("s_x_0"), sem("s_x_1")]
        s_stat, s_agg, s_var, s_rstd, s_h = sem("s_stat"), sem("s_agg"), sem("s_var"), sem("s_rstd"), sem("s_h")
        s_proj, s_full, s_hi = sem("s_proj"), sem("s_full"), sem("s_hi")
        s_rest, s_mid, s_lo = sem("s_rest"), sem("s_mid"), sem("s_lo")
        s_parts = [sem(f"s_parts{j}") for j in range(4)]
        s_v, s_vc = sem("s_v"), sem("s_vc")
        s_pk, s_pkp, s_pkd, s_pv, s_pvd, s_pad = (sem("s_pk"), sem("s_pkp"), sem("s_pkd"), sem("s_pv"),
                                                  sem("s_pvd"), sem("s_pad"))
        s_tab, s_k, s_q = sem("s_tab"), sem("s_k"), [sem("s_q0"), sem("s_q1")]
        s_b = [sem(f"s_b{c}") for c in range(QUADS)]
        s_r, s_s, s_far = sem("s_r"), sem("s_s"), sem("s_far")
        s_rc = sem("s_rc")
        s_rw = [sem("s_rw0"), sem("s_rw1")]
        s_min = sem("s_min")
        s_exp = sem("s_exp")
        s_av = sem("s_av")
        s_vb = sem("s_vb")
        s_of = sem("s_of")
        s_oc = sem("s_oc")
        s_rv = sem("s_rv")
        s_pick = sem("s_pick")
        s_fo = sem("s_fo")
        s_fa = sem("s_fa")
        s_on = sem("s_on")
        s_rr = sem("s_rr")
        s_t = [sem("s_t0"), sem("s_t1")]
        s_tc = [sem("s_tc0"), sem("s_tc1")]
        s_z = sem("s_z")
        s_go = {e: sem(f"s_go_{e}") for e in ("sp", "pool", "dve", "pe")}
        s_done = sem("s_done")
        s_xw, s_xwc = sem("s_xw"), [sem("s_xwc0"), sem("s_xwc1")]
        s_xin, s_gu = sem("s_xin"), sem("s_gu")
        s_wo, s_xr = sem("s_wo"), [sem("s_xr0"), sem("s_xr1")]
        s_att, s_add1, s_stat2, s_agg2 = sem("s_att"), sem("s_add1"), sem("s_stat2"), sem("s_agg2")
        s_var2, s_rstd2, s_h2, s_x1b = sem("s_var2"), sem("s_rstd2"), sem("s_h2"), sem("s_x1b")
        s_h2t, s_h2tc = [sem("s_h2t0"), sem("s_h2t1")], [sem("s_h2tc0"), sem("s_h2tc1")]
        s_g, s_u, s_h2s = sem("s_g"), sem("s_u"), sem("s_h2s")
        s_s2 = sem("s_s2")
        s_xl = sem("s_xl")
        s_xe = sem("s_xe")
        s_xs, s_xn = sem("s_xs"), sem("s_xn")
        s_xt = sem("s_xt")
        s_xc = [sem(f"s_xc{n}") for n in range(3)]
        s_xu = sem("s_xu")
        s_x2 = sem("s_x2")
        s_agg3 = sem("s_agg3")
        s_stat3, s_mv3, s_var3, s_rstd3 = sem("s_stat3"), sem("s_mv3"), sem("s_var3"), sem("s_rstd3")
        s_we, s_cnt0 = sem("s_we"), sem("s_cnt0")
        s3_h, s3_l, s3_o, s3_c = sem("s3_h"), sem("s3_l"), sem("s3_o"), sem("s3_c")
        s3_t = sem("s3_t")
        s3_tc = sem("s3_tc")
        s3_r = sem("s3_r")
        s3_e = sem("s3_e")
        s3_w = sem("s3_w")
        s3_wt = sem("s3_wt")
        s3_wc = sem("s3_wc")
        s3_b = sem("s3_b")
        s3_y = sem("s3_y")
        s3_acc = sem("s3_acc")

        block = ctx.enter_context(nc.Block())

        x_v = x.rearrange("(g s p) d -> g p s d", s=GT, p=P)

        def head_no(b, i, h):
            return b * (TPB * HEADS) + i * HEADS + h

        def rel_writes(b, i, c):
            return b * (8 * TPB * QUADS) + (16 * (i * (QUADS // 2) + c // 2))

        def head_uses(i):
            return PAIRS if i < 4 else HEADS

        def uses_before(i):
            return sum(head_uses(j) for j in range(i))

        def use(b, i, h):
            own = h // 2 if i < 4 else h
            return b * uses_before(TPB) + (GROUPS + uses_before(i) + own + 1)

        def banks_of(i, h):
            if i < 4:
                return [(h % 2, 0, i + 1)]
            cut = min(i - 2, 4)
            return [(0, 0, cut), (1, cut, i + 1)]

        def transposed(i, h, k0, k1):
            lo = max(0, i - 2)
            places = []
            if k0 < lo:
                places.append((pT[:, (h // 4) % 2, h % 4, k0:min(k1, lo), :], k0, min(k1, lo)))
            if k1 > lo:
                a = max(k0, lo)
                places.append((bandT[:, i % 2, a + 2 - i:k1 + 2 - i, h, :], a, k1))
            return places

        PAIR_AT = (4, 5, 7, 8, 10, 11, 13, 14)
        QUARTER_AT = (3, 6, 9, 12)

        def quarter_bank(i, g):
            return R_BANK if i + 1 < TPB else S_BANK + g

        def pair_bank(i, pair):
            return T_BANK if i == 0 and pair % 2 == 1 else R_BANK

        def depth(n):
            return 3 if n // HEADS < 4 else 2

        def ahead(i, h):
            for d in (2, 3):
                n = i * HEADS + h + d
                if n < TPB * HEADS and depth(n) == d:
                    return n // HEADS, n % HEADS
            return None

        def score(i, h):
            if i < 4:
                return ps[:, S_BANK + h % 4, 0:(i + 1) * P]
            at = S_BANK + 2 * (h % 2)
            return ps[:, at:at + 2, :].rearrange("p k n -> p (k n)")[:, 0:(i + 1) * P]

        def probs_of(i, h, k0, k1):
            at = h % 4 * BANK if i < 4 else h % 2 * SEQ
            return prob[:, at + k0:at + k1]

        MCH = INNER // P
        units = []
        for what in "kv":
            units += [(what, m, min(m + 3, MCH)) for m in range(0, MCH, 3)]
        XKV = len(units)
        for kc in range(KC):
            units += [("g", kc, range(h, min(h + 6, XH), 2)) for h0 in range(0, XH, 6) for h in (h0, h0 + 1)]
        for b_ in range(BATCH):
            units += [("u", b_, range(h, min(h + 4, XH), 2)) for h0 in range(0, XH, 4) for h in (h0, h0 + 1)]
        XUNITS = len(units)
        CK = BATCH * NCTX

        def unit_copies(n):
            what = units[n]
            bank = ps[:, S_BANK + n % 4, :]
            if what[0] in "kv":
                _, m0, m1 = what
                dst = (xkT if what[0] == "k" else xvT)[:, m0:m1, :]
                return dst, bank[:, 0:(m1 - m0) * CK].rearrange("p (m k) -> p m k", k=CK), \
                    (-1.0 / XD ** 0.5 if what[0] == "k" else 1.0)
            if what[0] == "g":
                _, kc, hs = what
                dst = g_out[:, kc, :, :].rearrange("p b (h k) -> p h b k", k=NCTX)[:, hs[0]:hs[-1] + 1:2]
                return dst, bank[:, 0:len(hs) * CK].rearrange("p (h b k) -> p h b k", b=BATCH, k=NCTX), 1.0
            _, b_, hs = what
            return u_out[:, b_, hs[0]:hs[-1] + 1:2, :], \
                ps[0:NCTX, S_BANK + n % 4, :].rearrange("p (h f) -> p h f", f=D), 1.0

        @block.sync
        def _(sp):
            for k in range(2):
                sp.sem_inc(s_rw[k], 16)
            sp.dma_start(xg[:, 0], x_v[0]).then_inc(s_x[0], 16)
            for dst, src in ((idf[:, :], ident), (pk0[:, :], pek0),
                             (pev0[:, :], pev[0:1, :].broadcast_to([P, HD])),
                             (pk_in[:, :], pekT[:, 0:REL + 1]),
                             (pv_in[:, :, :], pev[1:REL + 1, :].rearrange("(c p) d -> p c d", p=P))):
                sp.dma_start(dst, src).then_inc(s_cst, 16)
            for dst, src in ((wq_sb, wqT), (wk_sb, wkT), (wv_sb, wvT)):
                sp.dma_start(dst[:, :, :], src.rearrange("(c p) n -> p c n", p=P)).then_inc(s_w, 16)
            sp.dma_start(xg[:, 1], x_v[1]).then_inc(s_x[1], 16)
            sp.wait_ge(s_set, 2)
            rel_v = rel.ap().rearrange("s r u -> r s u")
            sp.dma_start(rel_v[:, :, 0:P], zrow[:, :].unsqueeze(1).broadcast_to([P, 2 * HEADS, P])).then_inc(s_pad, 16)
            sp.dma_start(rel_v[:, :, P + REL:ROW], brow[:, :].unsqueeze(1).broadcast_to([P, 2 * HEADS, P - 1])
                         ).then_inc(s_pad, 16)
            sp.dma_start(pvrows[0:P, :], zrow[:, 0:HD]).then_inc(s_pvd, 16)
            sp.dma_start(pvrows[P + REL:ROW + 1, :], zrow[:, 0:HD]).then_inc(s_pvd, 16)
            sp.wait_ge(s_pv, 1)
            sp.dma_start(pvrows[P:P + REL, :].rearrange("(c p) d -> p c d", p=P), pv_in[:, :, :]).then_inc(s_pvd, 16)
            sp.wait_ge(s_pkp, 4)
            sp.dma_start(pparts.ap().rearrange("t d j -> d t j"), pk_parts[:, :, :]).then_inc(s_pkd, 16)
            for g in range(GROUPS):
                if g + 2 < GROUPS:
                    sp.wait_ge(s_h, g + 1)
                    sp.dma_start(xg[:, g % 2], x_v[g + 2]).then_inc(s_x[g % 2], 16)
                if g == 2:
                    for dst, src, rows in ((xk_w, xwk, CTXC), (xv_w, xwv, CTXC), (ctx_sb, ctxT, CTXC), (xq_w, xwqT, P),
                                           (xo_w, xwo, P)):
                        sp.dma_start(dst[:, :, :], src.rearrange("(c p) n -> p c n", p=rows)).then_inc(s_xin, 16)
                for j in range(4):
                    u = 4 * g + j
                    sp.wait_ge(s_lo, u + 1)
                    to = (qparts, kparts)[j // 2].ap()[:, (j % 2) * P:(j % 2 + 1) * P, g * BANK:(g + 1) * BANK]
                    sp.dma_start(to.rearrange("t p n -> p t n"), parts[:, u % 4]).then_inc(s_parts[u % 4], 16)
            for k in range(4):
                sp.wait_ge(s_parts[k], 16 * 4)
            sp.wait_ge(s_vc, TILES // 2)
            sp.wait_ge(s_pad, 32)
            sp.wait_ge(s_pvd, 48)
            sp.wait_ge(s_pkd, 16)
            for n, t in enumerate(K_SLOTS):
                sp.dma_start(p6[n * HD:(n + 1) * HD, :], pparts[t]).then_inc(s_tab, 16)
            for blk in range(3):
                sp.dma_start(pvt[:, blk, :], bass.AP(tensor=pvrows, offset=blk * P * HD, ap=[[HD, P], [1, P * HD]])
                             ).then_inc(s_tab, 16)
            sp.dma_start(diag_sb[:, :], diag).then_inc(s_tab, 16)
            sp.dma_start(fold_sb[:, :, :], fold).then_inc(s_tab, 16)

            def load_q(b, i):
                if i > 1:
                    sp.wait_ge(s_s, head_no(b, i - 2, HEADS - 1) + 1)
                for n in range(len(Q_SLOTS)):
                    src_v = qparts.ap()[Q_SLOTS[n]].rearrange("(h d) n -> d h n", d=HD)
                    sp.dma_start(q6[n * HD:(n + 1) * HD, i % 2, :, :], src_v[:, :, bass.ds(b * SEQ + i * P, P)]
                                 ).then_inc(s_q[i % 2], 16)

            def write_rel(b, i, c):
                sp.wait_ge(s_rc, b * (TPB * PAIRS) + (2 * (i * QUADS + c) + 3))
                sl = (i % 2) * HEADS + 4 * c
                sp.dma_start(rel.ap()[sl:sl + 4, :, P:P + REL].rearrange("s r u -> r s u"), rel_out[:, c % 2]
                             ).then_inc(s_rw[c % 2], 16)

            def read_bias(b, i, c):
                if i > 0:
                    sp.wait_ge(s_min, head_no(b, i - 1, 4 * c + 3) + 2)
                sp.wait_ge(s_rw[c % 2], rel_writes(b, i, c) + 32)
                sl = (i % 2) * HEADS + 4 * c
                src = bass.AP(tensor=rel, offset=sl * (P * ROW) + 127, ap=[[ROW - 1, P], [P * ROW, 4], [1, BAND]])
                sp.dma_start(bias[:, 4 * c:4 * c + 4, :], src).then_inc(s_b[c], 16)

            with sp.Fori(0, BATCH) as b:
                sp.wait_ge(s_min, b * (TPB * HEADS) + 1)
                load_q(b, 0)
                load_q(b, 1)
                for n in range(len(K_SLOTS)):
                    src_v = kparts.ap()[K_SLOTS[n]].rearrange("(h d) n -> d h n", d=HD)
                    sp.dma_start(k6[n * HD:(n + 1) * HD, :, :], src_v[:, :, bass.ds(b * SEQ, SEQ)]).then_inc(s_k, 16)
                for i in range(TPB):
                    for c in range(QUADS):
                        write_rel(b, i, c)
                        if c == QUADS - 1 and 0 < i < TPB - 1:
                            load_q(b, i + 1)
                        if i == 0 and c == 1:
                            sp.wait_ge(s_gu, 48)
                        if c > 0:
                            read_bias(b, i, c - 1)
                    read_bias(b, i, QUADS - 1)
                sp.sem_inc(s_go["sp"], 1)
            sp.wait_ge(s_on, TILES + 1)
            sp.dma_start(wo_sb[:, :, :], woT.rearrange("(c p) n -> p c n", p=P)).then_inc(s_wo, 16)
            sp.dma_start(bo[:, :], xbo.broadcast_to([P, D])).then_inc(s_wo, 16)
            for g in range(2):
                sp.dma_start(xr[:, g], x_v[g]).then_inc(s_xr[g], 16)
            sp.dma_start(g_sb[:, :, :, :], gmat.ap()).then_inc(s_g, 16)
            whole = XK // P
            for b in range(BATCH):
                sp.dma_start(u_sb[:, b, 0:whole, :], umat.ap()[b, 0:whole * P].rearrange("(c p) f -> p c f", p=P)
                             ).then_inc(s_u, 16)
                sp.dma_start(u_sb[0:XK - whole * P, b, whole, :], umat.ap()[b, whole * P:XK]).then_inc(s_u, 16)
            for g in range(2, GROUPS):
                sp.wait_ge(s_add1, g - 1)
                sp.dma_start(xr[:, g % 2], x_v[g]).then_inc(s_xr[g % 2], 16)
            sp.dma_start(we_sb[:, :, :].rearrange("p c (e f) -> p c e f", e=EXPERTS),
                         weT.rearrange("(c p) e f -> p c e f", p=P)).then_inc(s_we, 16)
            sp.dma_start(be_sb[:, :], be).then_inc(s_we, 16)
            sp.dma_start(wg_sb[:, :, :], wg.rearrange("(c p) e -> p c e", p=P)).then_inc(s_we, 16)
            sp.dma_start(earlier_sb[:, :], earlier).then_inc(s_we, 16)
            sp.dma_start(ones_sb[:, :], ones).then_inc(s_we, 16)
            sp.dma_start(e8[:, :], experts).then_inc(s_we, 16)
            out_v = out.rearrange("(t p) d -> p t d", p=P)
            with sp.Fori(0, TILES // 2) as j:
                sp.wait_ge(s3_acc, j * 18 + 27)
                sp.dma_start(out_v[:, bass.ds(2 * j, 2), :], x1[:, bass.ds(2 * j, 2), :]).then_inc(s_done, 16)
                sp.sem_inc(s_go["sp"], 1)
            sp.wait_ge(s_done, 16 * (TILES // 2))

        @block.gpsimd
        def _(pool):
            pool.wait_ge(s_set, 1)

            def deviation(g):
                pool.wait_ge(s_agg, g + 1)
                nc.gpsimd.tensor_scalar(rstd1[:, :], mv1[:, :, 1], EPS, None, ALU.add).then_inc(s_var, 1)
                pool.wait_ge(s_var, g + 1)
                nc.gpsimd.tensor_tensor(rstd1[:, :], rstd1[:, :], half[:, 0:1].broadcast_to([P, GT]), ALU.pow
                                        ).then_inc(s_rstd, 1)

            deviation(0)
            for g in range(GROUPS):
                if g + 1 < GROUPS:
                    deviation(g + 1)
                for j in range(4):
                    u = 4 * g + j
                    pool.wait_ge(s_rest, u + 1)
                    nc.gpsimd.tensor_copy(parts[:, j, 1, :], rest[:, j, :]).then_inc(s_mid, 1)

            pool.wait_ge(s_vc, TILES // 2)
            pool.sem_inc(s_vb, 1)
            pool.wait_ge(s_av, TPB * QUADS + 2)
            nc.gpsimd.tensor_copy(v_b[:, :, :], x1[:, TPB:TILES, :]).then_inc(s_vb, 1)

            pool.wait_ge(s_wo, 32)
            for g in range(GROUPS):
                pool.wait_ge(s_agg2, g + 1)
                nc.gpsimd.tensor_scalar(rstd2[:, g % 2, :], mv2[:, g % 2, :, 1], EPS, None, ALU.add).then_inc(s_var2, 1)
                pool.wait_ge(s_var2, g + 1)
                nc.gpsimd.tensor_tensor(rstd2[:, g % 2, :], rstd2[:, g % 2, :], half[:, 0:1].broadcast_to([P, GT]),
                                        ALU.pow).then_inc(s_rstd2, 1)
                pool.wait_ge(s_h2, g + 1)
                nc.gpsimd.tensor_tensor(x1[:, GT * g:GT * (g + 1), :], x1[:, GT * g:GT * (g + 1), :],
                                        bo[:, :].unsqueeze(1).broadcast_to([P, GT, D]), ALU.add).then_inc(s_x1b, 1)
            for kc in range(KC):
                pool.wait_ge(s_h2tc[kc], GROUPS)
            with pool.Fori(0, TPB) as j:
                for u in range(2):
                    pool.wait_ge(s_s2, j * 6 + (3 * u + 3))
                    nc.gpsimd.tensor_copy(h2s[:, u, :, :], h2T[:, :, bass.ds(j * P + u * SEQ, P)]).then_inc(s_h2s, 1)
            pool.wait_ge(s_mv3, TILES)
            nc.gpsimd.tensor_scalar(rstd3[:, :], mv3[:, :, 1], EPS, None, ALU.add).then_inc(s_var3, 1)
            pool.wait_ge(s_var3, 1)
            nc.gpsimd.tensor_tensor(rstd3[:, :], rstd3[:, :], half[:, 0:1].broadcast_to([P, TILES]), ALU.pow
                                    ).then_inc(s_rstd3, 1)

        LAST_USE = GROUPS + BATCH * uses_before(TPB)

        @block.scalar
        def _(act):
            act.sem_inc(s_rc, 1)
            act.sem_inc(s_oc, 1)
            act.sem_inc(s_exp, 2)
            act.wait_ge(s_cst, 80)
            act.wait_ge(s_pk, 1)
            nc.scalar.copy(pk_parts[:, 0, :], pk_d[:, :]).then_inc(s_pkp, 1)
            act.wait_ge(s_pkp, 2)
            nc.scalar.copy(pk_parts[:, 1, :], pk_r[:, :]).then_inc(s_pkp, 1)
            for g in range(GROUPS):
                act.wait_ge(s_t[1], g + 1)
                if g >= 2:
                    act.wait_ge(s_v, 2 * (g - 1))
                nc.scalar.copy(hT[:, g % 2, 1, :], ps[:, T_BANK + 1, :]).then_inc(s_tc[1], 1)
                for j in range(4):
                    u = 4 * g + j
                    act.wait_ge(s_proj, u + 1)
                    if u >= 4:
                        act.wait_ge(s_lo, u - 3)
                        act.wait_ge(s_parts[j], 16 * (u // 4))
                    if j < 2:
                        nc.scalar.activation(full[:, j, :], ps[:, S_BANK + j, :], ACT.Copy, scale=-1.0 / SCALE
                                             ).then_inc(s_full, 1)
                    else:
                        nc.scalar.activation(full[:, j, :], ps[:, S_BANK + j, :], ACT.Identity, bias=pk0[:, 0:1]
                                             ).then_inc(s_full, 1)
                    act.wait_ge(s_full, u + 1)
                    nc.scalar.copy(parts[:, j, 0, :], full[:, j, :]).then_inc(s_hi, 1)

            def keep_folded(n, dst, src):
                for k in range(2):
                    act.wait_ge(s_xwc[k], (n + 1 - k) // 2)
                act.dma_start(dst, src).then_inc(s_gu, 16)

            first_u = [min(n for n, what in enumerate(units) if what[:2] == ("u", b)) for b in range(BATCH)]
            first_u.append(XUNITS)
            umat_v = umat.ap().rearrange("b (h k) f -> b k h f", k=NCTX)
            for n in range(0, XUNITS, 2):
                act.wait_ge(s_xw, n + 1)
                dst, src, scale = unit_copies(n)
                nc.scalar.activation(dst, src, ACT.Copy, scale=scale).then_inc(s_xwc[0], 1)
                if n in (first_u[0], first_u[0] + 1):
                    keep_folded(first_u[0], gmat.ap(), g_out[:, :, :, :])
                if n in (first_u[1], first_u[1] + 1):
                    keep_folded(first_u[1], umat_v[0], u_out[:, 0, :, :])
            keep_folded(XUNITS, umat_v[1], u_out[:, 1, :, :])

            def rel_copy(b, i, pair):
                c, pos = pair // 2, pair % 2
                act.wait_ge(s_r, b * (TPB * PAIRS) + (i * PAIRS + pair + 1))
                if pos == 0:
                    act.wait_ge(s_rw[c % 2], rel_writes(b, i, c) + 16)
                nc.scalar.copy(rel_out[:, c % 2, 2 * pos:2 * pos + 2, :].rearrange("p s j -> p (s j)"),
                               ps[:, pair_bank(i, pair), :]).then_inc(s_rc, 1)

            def softmax(b, i, h):
                act.wait_ge(s_min, head_no(b, i, h) + 2)
                nc.scalar.activation(probs_of(i, h, 0, (i + 1) * P), score(i, h), ACT.Exp, bias=low[:, h % 4:h % 4 + 1],
                                     scale=-1.0, accum_out=rsum[:, i % 2, h:h + 1]).then_inc(s_exp, 1)

            def copy_t(b, i, h):
                for bank, k0, k1 in banks_of(i, h):
                    act.wait_ge(s_t[bank], use(b, i, h))
                    if bank == 1:
                        act.wait_ge(s_av, b * (TPB * QUADS) + (i * QUADS + h // 4 + 1))
                        act.wait_ge(s_rv, b * (4 * TPB) + (4 * i + 4))
                        places = transposed(i, h, k0, k1)
                        for to, a, z in places:
                            ins = nc.scalar.copy(to, ps[:, T_BANK + 1, (a - k0) * P:(z - k0) * P].rearrange(
                                "p (k n) -> p k n", n=P))
                        ins.then_inc(s_tc[1], 1)

            def copy_out(b, i):
                act.wait_ge(s_av, b * (TPB * QUADS) + ((i + 1) * QUADS + 2))
                nc.scalar.copy(oTs[:, i % 2, :], ps[:, O_BANK, :]).then_inc(s_oc, 1)

            with act.Fori(0, BATCH) as b:
                for pair in range(PAIRS):
                    rel_copy(b, 0, pair)
                for h in range(depth(0)):
                    softmax(b, 0, h)
                act.wait_ge(s_gu, 48)
                for i in range(TPB):
                    for h in range(HEADS):
                        copy_t(b, i, h)
                        if h in PAIR_AT and i + 1 < TPB:
                            rel_copy(b, i + 1, PAIR_AT.index(h))
                        if ahead(i, h):
                            softmax(b, *ahead(i, h))
                        if h == 2 and i > 0:
                            copy_out(b, i - 1)
                copy_out(b, TPB - 1)

            act.wait_ge(s_on, TILES + 1)
            for g in range(GROUPS + 1):
                if g < GROUPS:
                    act.wait_ge(s_t[1], LAST_USE + g + 1)
                    if g >= 2:
                        act.wait_ge(s_att, g - 1)
                    nc.scalar.copy(oT[:, g % 2, 1, :], ps[:, T_BANK + 1, :]).then_inc(s_tc[1], 1)
                if g >= 1:
                    act.wait_ge(s_h2t[1], g)
                    nc.scalar.copy(h2T[:, 1, (g - 1) * BANK:g * BANK], ps[:, 1, :]).then_inc(s_h2tc[1], 1)

            act.sem_inc(s_xe, 3)
            act.sem_inc(s_xc[2], 1)

            def cross_exp(j, u):
                for n, (h0, h1) in enumerate(XBANKS):
                    act.wait_ge(s_xl, j * 6 + (3 * u + n + 1))
                    if n == 0:
                        act.wait_ge(s_xt, j * 6 + (3 * u + 3))
                    for h in range(h0, h1):
                        at = (h - h0) * NCTX
                        ins = nc.scalar.activation(xp[:, u, h * NCTX:(h + 1) * NCTX], ps[:, n, at:at + NCTX], ACT.Exp,
                                                   bias=xlow[:, u, h:h + 1], scale=-1.0, accum_out=xsum[:, u, h:h + 1])
                    ins.then_inc(s_xe, 1)

            def cross_step(j, u, following):
                act.wait_ge(s_xt, j * 6 + (3 * u + 9))
                act.wait_ge(s_xu, j * 2 + (u + 1))
                nc.scalar.copy(xpT[:, u, XCH - 2, :], ps[:, 5, 0:P])
                nc.scalar.copy(xpT[0:XTAIL, u, XCH - 1, :], ps[0:XTAIL, 5, P:2 * P]).then_inc(s_xc[2], 1)
                if following is not None:
                    cross_exp(*following)

            cross_exp(0, 0)
            with act.Fori(0, TPB - 1) as j:
                cross_step(j, 0, (j, 1))
                cross_step(j, 1, (j + 1, 0))
            cross_step(TPB - 1, 0, (TPB - 1, 1))
            cross_step(TPB - 1, 1, None)

            act.sem_inc(s3_tc, 1)
            act.sem_inc(s3_wc, 1)

            def route(j, v):
                act.wait_ge(s3_t, j + 2)
                act.wait_ge(s3_y, j * 8 + 8)
                nc.scalar.copy(h3T[:, v, :], ps[:, 4, :]).then_inc(s3_tc, 1)
                act.wait_ge(s3_r, j * RSTEPS + 2)
                nc.scalar.activation(expb[:, :, :], below[:, :, :], ACT.Exp).then_inc(s3_e, 1)
                act.wait_ge(s3_wt, j + 1)
                nc.scalar.copy(wgtT[:, v, :], ps[0:EXPERTS, 6, 0:2 * P]).then_inc(s3_wc, 1)

            route(0, 0)
            with act.Fori(0, TILES // 4 - 1) as jj:
                route(2 * jj + 1, 1)
                route(2 * jj + 2, 0)
            route(TILES // 2 - 1, 1)

        @block.vector
        def _(dve):
            dve.sem_inc(s_min, 1)
            dve.sem_inc(s_on, 1)
            dve.sem_inc(s_pick, 1)
            nc.vector.memset(half[:, :], -0.5).then_inc(s_set, 1)
            nc.vector.memset(zrow[:, :], 0.0)
            nc.vector.memset(brow[:, :], BIG).then_inc(s_set, 1)

            def normalise(g):
                dve.wait_ge(s_x[g % 2], 16 * (g // 2 + 1))
                for s in range(GT):
                    nc.vector.bn_stats(st1[:, s, :], xg[:, g % 2, s, :]).then_inc(s_stat, 1)
                dve.wait_ge(s_stat, GT * (g + 1))
                for s in range(GT):
                    ins = nc.vector.bn_aggr(mv1[:, s, :], st1[:, s, :])
                ins.then_inc(s_agg, 1)
                dve.wait_ge(s_rstd, g + 1)
                if g >= 1:
                    dve.wait_ge(s_t[1], g)
                for s in range(GT):
                    ins = nc.vector.tensor_scalar(hg[:, s, :], xg[:, g % 2, s, :], mv1[:, s, 0:1], rstd1[:, s:s + 1],
                                                  ALU.subtract, ALU.mult)
                ins.then_inc(s_h, 1)

            normalise(0)
            dve.wait_ge(s_cst, 80)
            nc.vector.tensor_scalar(pk_d[:, :], pk_in[:, 1:REL + 1], pk_in[:, 0:1], None, ALU.subtract
                                    ).then_inc(s_pk, 1)
            nc.vector.tensor_tensor(pv_in[:, :, :], pv_in[:, :, :], pev0[:, :].unsqueeze(1).broadcast_to([P, 2, HD]),
                                    ALU.subtract).then_inc(s_pv, 1)
            dve.wait_ge(s_pkp, 1)
            nc.vector.tensor_tensor(pk_r[:, :], pk_d[:, :], pk_parts[:, 0, :], ALU.subtract).then_inc(s_pkp, 1)
            dve.wait_ge(s_pkp, 3)
            nc.vector.tensor_tensor(pk_parts[:, 2, :], pk_r[:, :], pk_parts[:, 1, :], ALU.subtract).then_inc(s_pkp, 1)
            for g in range(GROUPS):
                dve.wait_ge(s_t[0], g + 1)
                if g >= 2:
                    dve.wait_ge(s_v, 2 * (g - 1))
                nc.vector.tensor_copy(hT[:, g % 2, 0, :], ps[:, T_BANK, :]).then_inc(s_tc[0], 1)
                if g + 1 < GROUPS:
                    normalise(g + 1)
                for j in range(5):
                    u = 4 * g + j
                    if j < 4:
                        dve.wait_ge(s_hi, u + 1)
                        nc.vector.tensor_tensor(rest[:, j, :], full[:, j, :], parts[:, j, 0, :], ALU.subtract
                                                ).then_inc(s_rest, 1)
                    if j > 0:
                        dve.wait_ge(s_mid, u)
                        nc.vector.tensor_tensor(parts[:, j - 1, 2, :], rest[:, j - 1, :], parts[:, j - 1, 1, :],
                                                ALU.subtract).then_inc(s_lo, 1)
                for half_g in range(2):
                    dve.wait_ge(s_v, 2 * g + half_g + 1)
                    t = GT * g + 2 * half_g
                    v_to = v_b[:, t:t + 2, :] if t < TPB else x1[:, t:t + 2, :]
                    nc.vector.tensor_tensor(v_to.rearrange("p t (h d) -> p (t h) d", d=HD),
                                            ps[:, R_BANK + half_g, :].rearrange("p (a d) -> p a d", d=HD),
                                            pev0[:, :].unsqueeze(1).broadcast_to([P, 2 * HEADS, HD]), ALU.add
                                            ).then_inc(s_vc, 1)
            for n in range(1, XUNITS, 2):
                dve.wait_ge(s_xw, n + 1)
                dst, src, scale = unit_copies(n)
                nc.vector.tensor_scalar(dst, src, scale, None, ALU.mult).then_inc(s_xwc[1], 1)
            dve.wait_ge(s_gu, 48)
            nc.vector.memset(zb[:, :], 0.0).then_inc(s_z, 1)
            dve.wait_ge(s_tab, 16 * 11)

            def minimum(b, i, h):
                n = head_no(b, i, h)
                w0 = max(0, i - 2) * P
                K = (i + 1) * P
                dve.wait_ge(s_s, n + 1)
                if h % 4 == 0:
                    dve.wait_ge(s_b[h // 4], b * (16 * TPB) + (16 * i + 16))
                first = BIG
                if i > 2:
                    nc.vector.tensor_reduce(far[:, h % 2:h % 2 + 1], score(i, h)[:, 0:w0], AX.X, ALU.min
                                            ).then_inc(s_far, 1)
                    dve.wait_ge(s_far, b * ((TPB - 3) * HEADS) + ((i - 3) * HEADS + h + 1))
                    first = far[:, h % 2:h % 2 + 1]
                dve.sem_inc(s_go["dve"], 1)
                s = score(i, h)[:, w0:K]
                nc.vector.tensor_tensor_reduce(s, s, bias[:, h, BAND - (K - w0):BAND], 1.0, first,
                                               ALU.add, ALU.min, low[:, h % 4:h % 4 + 1]).then_inc(s_min, 1)

            def copy_t(b, i, h):
                for bank, k0, k1 in banks_of(i, h):
                    if bank == 0:
                        dve.wait_ge(s_t[0], use(b, i, h))
                        dve.wait_ge(s_av, b * (TPB * QUADS) + (i * QUADS + h // 4 + 1))
                        dve.wait_ge(s_rv, b * (4 * TPB) + (4 * i + 4))
                        for to, a, z in transposed(i, h, k0, k1):
                            ins = nc.vector.tensor_copy(to, ps[:, T_BANK, (a - k0) * P:(z - k0) * P].rearrange(
                                "p (k n) -> p k n", n=P))
                        ins.then_inc(s_tc[0], 1)

            def pick(b, i, g):
                dve.wait_ge(s_rv, b * (4 * TPB) + (4 * i + g + 9))
                if i > 0:
                    dve.wait_ge(s_fo, b * TPB + i)
                nc.vector.tensor_tensor(
                    picked[:, :, 16 * g:16 * g + 16].rearrange("p h (g q) -> p g h q", q=4),
                    ps[:, quarter_bank(i, g), 0:256].rearrange("p (g h q) -> p g h q", g=4, q=4),
                    diag_sb[:, :].rearrange("p (h q) -> p h q", q=4).unsqueeze(1).broadcast_to([P, 4, HEADS, 4]),
                    ALU.mult).then_inc(s_pick, 1)

            def add_folded(b, i):
                dve.wait_ge(s_fo, b * TPB + (i + 1))
                dve.wait_ge(s_oc, b * TPB + (i + 2))
                nc.vector.tensor_tensor(oTs[:, i % 2, :], ps[:, R_BANK, :], oTs[:, i % 2, :], ALU.add).then_inc(s_fa, 1)

            def invert(b, i):
                nc.vector.reciprocal(rrec[:, i % 2, :], rsum[:, i % 2, :]).then_inc(s_rr, 1)

            def finish(b, i):
                dve.wait_ge(s_rr, b * TPB + (i + 1))
                dve.wait_ge(s_of, b * TPB + (i + 1))
                nc.vector.tensor_tensor(
                    x1[:, bass.ds(b * TPB + i, 1), :].rearrange("p o (h d) -> p (o h) d", d=HD),
                    ps[:, R_BANK, :].rearrange("p (h r) -> p h r", r=32)[:, :, 0:HD],
                    rrec[:, i % 2, :].unsqueeze(2).broadcast_to([P, HEADS, HD]), ALU.mult).then_inc(s_on, 1)

            with dve.Fori(0, BATCH) as b:
                for h in range(depth(0)):
                    minimum(b, 0, h)
                for i in range(TPB):
                    for h in range(HEADS):
                        if ahead(i, h):
                            minimum(b, *ahead(i, h))
                        copy_t(b, i, h)
                        if h == 0 and i > 1:
                            add_folded(b, i - 2)
                        if h == 1 and i > 1:
                            finish(b, i - 2)
                        if h == 2 and i > 0:
                            invert(b, i - 1)
                        if h in QUARTER_AT and i > 0:
                            pick(b, i - 1, QUARTER_AT.index(h))
                add_folded(b, TPB - 2)
                finish(b, TPB - 2)
                for g in range(4):
                    pick(b, TPB - 1, g)
                invert(b, TPB - 1)
                add_folded(b, TPB - 1)
                finish(b, TPB - 1)

            dve.wait_ge(s_on, TILES + 1)

            def copy_o(g):
                dve.wait_ge(s_t[0], LAST_USE + g + 1)
                if g >= 2:
                    dve.wait_ge(s_att, g - 1)
                nc.vector.tensor_copy(oT[:, g % 2, 0, :], ps[:, T_BANK, :]).then_inc(s_tc[0], 1)

            def copy_h2(g):
                dve.wait_ge(s_h2t[0], g + 1)
                nc.vector.tensor_copy(h2T[:, 0, g * BANK:(g + 1) * BANK], ps[:, 0, :]).then_inc(s_h2tc[0], 1)

            copy_o(0)
            for g in range(GROUPS):
                dve.wait_ge(s_att, g + 1)
                dve.wait_ge(s_xr[g % 2], 16 * (g // 2 + 1))
                for k in range(2):
                    t = GT * g + 2 * k
                    ins = nc.vector.tensor_tensor(x1[:, t:t + 2, :].rearrange("p t d -> p (t d)"), ps[:, 6 + k, :],
                                                  xr[:, g % 2, 2 * k:2 * k + 2, :].rearrange("p t d -> p (t d)"),
                                                  ALU.add)
                ins.then_inc(s_add1, 1)
                if g + 1 < GROUPS:
                    copy_o(g + 1)
                dve.wait_ge(s_add1, g + 1)
                for s in range(GT):
                    nc.vector.bn_stats(st2[:, s, :], x1[:, GT * g + s, :]).then_inc(s_stat2, 1)
                dve.wait_ge(s_stat2, GT * (g + 1))
                for s in range(GT):
                    ins = nc.vector.bn_aggr(mv2[:, g % 2, s, :], st2[:, s, :])
                ins.then_inc(s_agg2, 1)
                if g >= 1:
                    copy_h2(g - 1)
                dve.wait_ge(s_rstd2, g + 1)
                for s in range(GT):
                    ins = nc.vector.tensor_scalar(h2[:, g % 2, s, :], x1[:, GT * g + s, :], mv2[:, g % 2, s, 0:1],
                                                  rstd2[:, g % 2, s:s + 1], ALU.subtract, ALU.mult)
                ins.then_inc(s_h2, 1)
            copy_h2(GROUPS - 1)

            dve.sem_inc(s_xc[0], 1)
            dve.sem_inc(s_xc[1], 1)
            dve.sem_inc(s_x2, 2)

            def cross_low(j, u):
                for n, (h0, h1) in enumerate(XBANKS):
                    dve.wait_ge(s_s2, j * 6 + (3 * u + n + 7))
                    nc.vector.tensor_reduce(xlow[:, u, h0:h1],
                                            ps[:, n, 0:(h1 - h0) * NCTX].rearrange("p (h k) -> p h k", k=NCTX),
                                            AX.X, ALU.min).then_inc(s_xl, 1)

            def cross_normalise(j, u):
                for n, (h0, h1) in enumerate(XBANKS):
                    dve.wait_ge(s_xe, j * 6 + (3 * u + n + 4))
                    nc.vector.reciprocal(xrec[:, h0:h1], xsum[:, u, h0:h1]).then_inc(s_xs, 1)
                    dve.wait_ge(s_xs, j * 6 + (3 * u + n + 1))
                    p3 = xp[:, u, h0 * NCTX:h1 * NCTX].rearrange("p (h k) -> p h k", k=NCTX)
                    nc.vector.tensor_tensor(p3, p3, xrec[:, h0:h1].unsqueeze(2).broadcast_to([P, h1 - h0, NCTX]),
                                            ALU.mult).then_inc(s_xn, 1)

            def cross_step(j, u, following):
                for n in range(2):
                    dve.wait_ge(s_xt, j * 6 + (3 * u + n + 7))
                    dve.wait_ge(s_xu, j * 2 + (u + 1))
                    nc.vector.tensor_copy(xpT[:, u, 4 * n:4 * n + 4, :].rearrange("p c n -> p (c n)"), ps[:, 3 + n, :]
                                          ).then_inc(s_xc[n], 1)
                if following is not None:
                    cross_low(*following)
                    cross_normalise(*following)
                dve.wait_ge(s_xu, j * 2 + (u + 3))
                xt = x1[:, bass.ds(j + TPB * u, 1), :].rearrange("p o d -> p (o d)")
                nc.vector.tensor_tensor(xt, ps[:, 6 + u, 0:D], xt, ALU.add).then_inc(s_x2, 1)
                dve.wait_ge(s_x2, j * 2 + (u + 3))
                nc.vector.bn_stats(st3[:, :], xt).then_inc(s_stat3, 1)
                dve.wait_ge(s_stat3, j * 2 + (u + 1))
                dve.sem_inc(s_go["dve"], 1)
                nc.vector.bn_aggr(mvs[:, :], st3[:, :]).then_inc(s_agg3, 1)
                dve.wait_ge(s_agg3, j * 2 + (u + 1))
                nc.vector.tensor_copy(mv3[:, bass.ds(j + TPB * u, 1), :].rearrange("p o d -> p (o d)"), mvs[:, :]
                                      ).then_inc(s_mv3, 1)

            dve.wait_ge(s_x1b, GROUPS)
            cross_low(0, 0)
            cross_normalise(0, 0)
            with dve.Fori(0, TPB - 1) as j:
                cross_step(j, 0, (j, 1))
                cross_step(j, 1, (j + 1, 0))
            cross_step(TPB - 1, 0, (TPB - 1, 1))
            cross_step(TPB - 1, 1, None)

            dve.sem_inc(s3_w, 1)
            dve.sem_inc(s3_acc, 9)
            nc.vector.memset(count[:, :], 0.0).then_inc(s_cnt0, 1)
            dve.wait_ge(s_cnt0, 1)
            dve.wait_ge(s_we, 16 * 6)
            nc.vector.tensor_copy(earlier_b[:, :], earlier_sb[:, :]).then_inc(s_cnt0, 1)
            nc.vector.tensor_copy(ones_b[:, :], ones_sb[:, :]).then_inc(s_cnt0, 1)
            dve.wait_ge(s_rstd3, 1)

            def rows(j, v):
                dve.wait_ge(s3_t, j + 1)
                for u in range(2):
                    t = 2 * j + u
                    ins = nc.vector.tensor_scalar(h3[:, v, u, :],
                                                  x1[:, bass.ds(t, 1), :].rearrange("p o d -> p (o d)"),
                                                  mv3[:, bass.ds(t, 1), 0:1].rearrange("p o d -> p (o d)"),
                                                  rstd3[:, bass.ds(t, 1)], ALU.subtract, ALU.mult)
                ins.then_inc(s3_h, 1)

            def choose(j, v):
                step = [0]

                def link(ins):
                    step[0] += 1
                    ins.then_inc(s3_r, 1)
                    dve.wait_ge(s3_r, j * RSTEPS + step[0])

                lg = ps[:, 5, 0:2 * EXPERTS].rearrange("p (u e) -> p u e", e=EXPERTS)
                e_row = e8[:, :].unsqueeze(1).broadcast_to([P, 2, EXPERTS])
                dve.wait_ge(s3_l, j + 1)
                link(nc.vector.tensor_reduce(top[:, :], lg, AX.X, ALU.max))
                link(nc.vector.tensor_tensor(below[:, :, :], lg, top[:, :].unsqueeze(2).broadcast_to([P, 2, EXPERTS]),
                                             ALU.subtract))
                link(nc.vector.scalar_tensor_tensor(out=cand[:, :, :], in0=below[:, :, :], scalar=0.0, in1=e_row,
                                                    op0=ALU.is_ge, op1=ALU.mult))
                link(nc.vector.tensor_reduce(first_e[:, :], cand[:, :, :], AX.X, ALU.min))
                nc.vector.tensor_tensor(chosen[:, v, :, :], e_row,
                                        first_e[:, :].unsqueeze(2).broadcast_to([P, 2, EXPERTS]), ALU.is_equal
                                        ).then_inc(s3_o, 1)
                dve.wait_ge(s3_e, j + 1)
                link(nc.vector.tensor_reduce(den[:, :], expb[:, :, :], AX.X, ALU.add))
                link(nc.vector.reciprocal(gate[:, :], den[:, :]))
                dve.wait_ge(s3_o, j + 1)

            def weigh(j, v):
                step = [6]

                def link(ins):
                    step[0] += 1
                    ins.then_inc(s3_r, 1)
                    dve.wait_ge(s3_r, j * RSTEPS + step[0])

                dve.wait_ge(s3_c, j + 1)
                at = ps[:, 5, 16:16 + 2 * EXPERTS].rearrange("p (u e) -> p u e", e=EXPERTS)
                link(nc.vector.tensor_tensor(place[:, :, :], at, count[:, :].unsqueeze(1).broadcast_to([P, 2, EXPERTS]),
                                             ALU.add))
                link(nc.vector.tensor_tensor(count[:, :], ps[:, 5, 32:32 + EXPERTS], count[:, :], ALU.add))
                link(nc.vector.scalar_tensor_tensor(out=kept[:, :, :], in0=place[:, :, :], scalar=float(CAP),
                                                    in1=chosen[:, v, :, :], op0=ALU.is_lt, op1=ALU.mult))
                link(nc.vector.tensor_tensor(expw[:, :, :], kept[:, :, :],
                                             gate[:, :].unsqueeze(2).broadcast_to([P, 2, EXPERTS]), ALU.mult))
                nc.vector.tensor_copy(wgt[:, v, :, :], expw[:, :, :]).then_inc(s3_w, 1)
                dve.wait_ge(s3_w, j + 2)

            def add_bias(j, u):
                dve.wait_ge(s3_b, j + 1)
                xt = x1[:, bass.ds(2 * j + u, 1), :].rearrange("p o d -> p (o d)")
                nc.vector.tensor_tensor(xt, ps[:, 7, u * D:(u + 1) * D], xt, ALU.add).then_inc(s3_acc, 1)
                dve.wait_ge(s3_acc, j * 18 + (9 * u + 10))

            def add_experts(j, v, u, q):
                dve.wait_ge(s3_y, j * 8 + (4 * u + q + 17))
                xt = x1[:, bass.ds(2 * j + u, 1), :].rearrange("p o d -> p (o d)")
                for e in range(2):
                    nc.vector.scalar_tensor_tensor(out=xt, in0=ps[:, q, e * D:(e + 1) * D],
                                                   scalar=wgt[:, v, u, 2 * q + e:2 * q + e + 1], in1=xt,
                                                   op0=ALU.mult, op1=ALU.add).then_inc(s3_acc, 1)
                    dve.wait_ge(s3_acc, j * 18 + (9 * u + 2 * q + e + 11))

            def experts_step(j, v, last):
                if not last:
                    rows(j + 1, 1 - v)
                add_bias(j, 0)
                add_experts(j, v, 0, 0)
                add_experts(j, v, 0, 1)
                add_experts(j, v, 0, 2)
                if not last:
                    choose(j + 1, 1 - v)
                add_experts(j, v, 0, 3)
                add_bias(j, 1)
                add_experts(j, v, 1, 0)
                add_experts(j, v, 1, 1)
                if not last:
                    weigh(j + 1, 1 - v)
                add_experts(j, v, 1, 2)
                add_experts(j, v, 1, 3)

            rows(0, 0)
            choose(0, 0)
            weigh(0, 0)
            with dve.Fori(0, TILES // 4 - 1) as jj:
                experts_step(2 * jj, 0, False)
                experts_step(2 * jj + 1, 1, False)
            experts_step(TILES // 2 - 2, 0, False)
            experts_step(TILES // 2 - 1, 1, True)

        @block.tensor
        def _(pe):
            pe.sem_inc(s_av, 2)
            pe.sem_inc(s_rv, 8)
            pe.wait_ge(s_cst, 80)
            pe.wait_ge(s_w, 48)

            def turn_normalised(g):
                pe.wait_ge(s_h, g + 1)
                for kc in range(KC):
                    if g >= 1:
                        pe.wait_ge(s_tc[kc], g)
                    for s in range(GT):
                        mm = pe.transpose(ps[:, T_BANK + kc, s * P:(s + 1) * P], hg[:, s, kc * P:(kc + 1) * P],
                                          idf[:, :])
                    mm.then_inc(s_t[kc], 1)

            turn_normalised(0)
            for g in range(GROUPS):
                for kc in range(KC):
                    pe.wait_ge(s_tc[kc], g + 1)
                for j in range(4):
                    if g >= 1:
                        pe.wait_ge(s_full, 4 * (g - 1) + j + 1)
                    w = (wq_sb, wk_sb)[j // 2]
                    for kc in range(KC):
                        mm = pe.matmul(ps[:, S_BANK + j, :], w[:, kc, (j % 2) * P:(j % 2 + 1) * P],
                                       hT[:, g % 2, kc, :], start=(kc == 0), stop=(kc == KC - 1))
                    mm.then_inc(s_proj, 1)
                if g + 1 < GROUPS:
                    turn_normalised(g + 1)
                for half_g in range(2):
                    if g >= 1:
                        pe.wait_ge(s_vc, 2 * (g - 1) + half_g + 1)
                    for s in range(2):
                        for kc in range(KC):
                            mm = pe.matmul(ps[:, R_BANK + half_g, s * D:(s + 1) * D],
                                           hT[:, g % 2, kc, (2 * half_g + s) * P:(2 * half_g + s + 1) * P],
                                           wv_sb[:, kc, :], start=(kc == 0), stop=(kc == KC - 1))
                    mm.then_inc(s_v, 1)
            pe.wait_ge(s_full, 4 * GROUPS)
            pe.wait_ge(s_vc, 2 * GROUPS)
            pe.wait_ge(s_xin, 16 * 5)
            for n, what in enumerate(units):
                if n >= 4:
                    pe.wait_ge(s_xwc[n % 2], (n - 4) // 2 + 1)
                if n == XKV:
                    for k in range(2):
                        pe.wait_ge(s_xwc[k], (XKV + 1 - k) // 2)
                bank = S_BANK + n % 4
                if what[0] in "kv":
                    w = xk_w if what[0] == "k" else xv_w
                    for m in range(what[1], what[2]):
                        at = (m - what[1]) * CK
                        for kc in range(2):
                            mm = pe.matmul(ps[:, bank, at:at + CK], w[:, kc, m * P:(m + 1) * P], ctx_sb[:, kc, :],
                                           start=(kc == 0), stop=(kc == 1))
                elif what[0] == "g":
                    _, kc, hs = what
                    for at, h in enumerate(hs):
                        rows = slice(XD * (h % 2), XD * (h % 2) + XD)
                        mm = pe.matmul(ps[:, bank, at * CK:(at + 1) * CK],
                                       xq_w[rows, h // 2, kc * P:(kc + 1) * P], xkT[rows, h // 2, :],
                                       start=True, stop=True)
                else:
                    _, b_, hs = what
                    for at, h in enumerate(hs):
                        rows = slice(XD * (h % 2), XD * (h % 2) + XD)
                        mm = pe.matmul(ps[0:NCTX, bank, at * D:(at + 1) * D],
                                       xvT[rows, h // 2, b_ * NCTX:(b_ + 1) * NCTX], xo_w[rows, h // 2, :],
                                       start=True, stop=True)
                mm.then_inc(s_xw, 1)
            for k in range(2):
                pe.wait_ge(s_xwc[k], (XUNITS + 1 - k) // 2)
            pe.wait_ge(s_tab, 16 * 11)

            def rel_scores(b, i, pair):
                if pair == 0:
                    pe.wait_ge(s_q[i % 2], b * (16 * len(Q_SLOTS) * TPB // 2) + 16 * len(Q_SLOTS) * (i // 2 + 1))
                if i > 0:
                    pe.wait_ge(s_rc, b * (TPB * PAIRS) + (i * PAIRS + pair + 1))
                elif pair > 1:
                    pe.wait_ge(s_rc, b * (TPB * PAIRS) + pair)
                if i >= 2:
                    done = sum(at < PAIR_AT[pair] for at in QUARTER_AT)
                    pe.wait_ge(s_pick, b * (4 * TPB) + (4 * (i - 2) + done + 1))
                if i >= 3 and pair == 0:
                    pe.wait_ge(s_on, b * TPB + (i - 1))
                for s in range(2):
                    mm = pe.matmul(ps[:, pair_bank(i, pair), s * REL:(s + 1) * REL], q6[:, i % 2, 2 * pair + s, :],
                                   p6[:, :], start=True, stop=True)
                mm.then_inc(s_r, 1)

            def scores(b, i, h):
                if i == 0 and h < 4:
                    if h == 0:
                        pe.wait_ge(s_exp, head_no(b, 0, 0) + 2)
                elif i < 4:
                    pe.wait_ge(s_exp, head_no(b, i, h) - 1)
                else:
                    pe.wait_ge(s_exp, head_no(b, i, h) + 1)
                K = (i + 1) * P
                for n0 in range(0, K, BANK):
                    n1 = min(K, n0 + BANK)
                    mm = pe.matmul(score(i, h)[:, n0:n1], q6[:, i % 2, h, :], k6[:, h, n0:n1],
                                   start=True, stop=True)
                mm.then_inc(s_s, 1)

            def transposes(b, i, h):
                pe.wait_ge(s_exp, head_no(b, i, h) + 3)
                for bank, k0, k1 in banks_of(i, h):
                    pe.wait_ge(s_tc[bank], use(b, i, h) - 1)
                    for kb in range(k0, k1):
                        mm = pe.transpose(ps[:, T_BANK + bank, (kb - k0) * P:(kb - k0 + 1) * P],
                                          probs_of(i, h, kb * P, (kb + 1) * P), idf[:, :])
                    mm.then_inc(s_t[bank], 1)

            def zero_out(b, i):
                pe.wait_ge(s_oc, b * TPB + (i + 1))
                pe.matmul(ps[:, O_BANK, :], zb[:, 0:P], zb[:, :], start=True, stop=False, skip_group_check=True)

            def values(b, i, c, k0, k1):
                if k0 == k1:
                    return
                for bank in range(2):
                    pe.wait_ge(s_tc[bank], use(b, i, 4 * c + 3))
                for kb in range(k0, k1):
                    for k in range(4):
                        h = 4 * c + k
                        probs = pT[:, c % 2, k, kb, :] if kb < i - 2 else bandT[:, i % 2, kb + 2 - i, h, :]
                        mm = pe.matmul(ps[32 * k:32 * k + HD, O_BANK, c * P:(c + 1) * P],
                                       v_b[:, kb, h * HD:(h + 1) * HD], probs,
                                       start=False, stop=False, skip_group_check=True)
                if k1 == i + 1:
                    mm.then_inc(s_av, 1)

            def rel_values(b, i, g):
                first = max(0, 2 - i)
                if i + 1 < TPB:
                    pe.wait_ge(s_pick, b * (4 * TPB) + (4 * i + g + 1))
                if i + 2 < TPB:
                    done = sum(at < QUARTER_AT[g] for at in PAIR_AT)
                    pe.wait_ge(s_rc, b * (TPB * PAIRS) + ((i + 2) * PAIRS + done + 1))
                if 1 <= i < TPB - 1 and g == 0:
                    pe.wait_ge(s_on, b * TPB + (i + 1))
                for a in range(4):
                    for blk in range(first, 3):
                        for e in range(2):
                            q = 8 * (4 * g + a) + 4 * e
                            mm = pe.matmul(ps[64 * e:64 * e + 64, quarter_bank(i, g), a * 64:(a + 1) * 64].rearrange(
                                               "p (h q) -> p h q", q=4),
                                           pvt[:, blk, (P - 4 - q) * HD:(P - q) * HD], bandT[:, i % 2, blk, :, q:q + 4],
                                           start=(blk == first), stop=(blk == 2))
                mm.then_inc(s_rv, 1)

            def fold_values(b, i):
                pe.wait_ge(s_pick, b * (4 * TPB) + (4 * i + 5))
                if i + 1 == TPB:
                    pe.wait_ge(s_on, b * TPB + (i + 1))
                if i + 2 < TPB:
                    pe.wait_ge(s_rc, b * (TPB * PAIRS) + ((i + 3) * PAIRS + 1))
                for k in range(4):
                    for e in range(2):
                        to = ps[32 * k:32 * k + HD, R_BANK, :].rearrange("p (c g e q) -> p c g e q", c=QUADS, e=2, q=4)
                        mm = pe.matmul(to[:, :, :, e, :], fold_sb[:, e, :],
                                       picked[:, k:HEADS:4, :].rearrange("p c (g q) -> p c g q", q=4),
                                       start=True, stop=True)
                mm.then_inc(s_fo, 1)

            def turn_back(b, i):
                pe.wait_ge(s_fa, b * TPB + (i + 1))
                for c in range(QUADS):
                    mm = pe.transpose(ps[:, R_BANK, c * P:(c + 1) * P], oTs[:, i % 2, c * P:(c + 1) * P], idf[:, :])
                mm.then_inc(s_of, 1)

            with pe.Fori(0, BATCH) as b:
                pe.wait_ge(s_vb, b + 1)
                pe.wait_ge(s_on, b * TPB + 1)
                pe.sem_inc(s_go["pe"], 1)
                for pair in range(PAIRS):
                    rel_scores(b, 0, pair)
                pe.wait_ge(s_k, b * (16 * len(K_SLOTS)) + 16 * len(K_SLOTS))
                for h in range(depth(0)):
                    scores(b, 0, h)
                pe.wait_ge(s_rc, b * (TPB * PAIRS) + (PAIRS + 1))
                pe.wait_ge(s_z, 1)
                for i in range(TPB):
                    for h in range(HEADS):
                        if ahead(i, h):
                            scores(b, *ahead(i, h))
                        transposes(b, i, h)
                        if h in PAIR_AT and i + 1 < TPB:
                            rel_scores(b, i + 1, PAIR_AT.index(h))
                        if h in QUARTER_AT and i > 0:
                            rel_values(b, i - 1, QUARTER_AT.index(h))
                        if h == 0 and i > 1:
                            fold_values(b, i - 2)
                        if h == 1 and i > 1:
                            turn_back(b, i - 2)
                        c, k = h // 4, h % 4
                        if h in (0, 1) and i > 0:
                            values(b, i - 1, QUADS - 1, i * h // 2, i * (h + 1) // 2)
                        if c > 0:
                            if h == 4:
                                zero_out(b, i)
                            values(b, i, c - 1, (i + 1) * k // 4, (i + 1) * (k + 1) // 4)
                fold_values(b, TPB - 2)
                values(b, TPB - 1, QUADS - 1, 0, TPB)
                turn_back(b, TPB - 2)
                for g in range(4):
                    rel_values(b, TPB - 1, g)
                fold_values(b, TPB - 1)
                turn_back(b, TPB - 1)

            pe.wait_ge(s_on, TILES + 1)
            pe.wait_ge(s_wo, 32)

            def turn_o(g):
                for kc in range(KC):
                    pe.wait_ge(s_tc[kc], LAST_USE + g)
                    for s in range(GT):
                        mm = pe.transpose(ps[:, T_BANK + kc, s * P:(s + 1) * P],
                                          x1[:, GT * g + s, kc * P:(kc + 1) * P], idf[:, :])
                    mm.then_inc(s_t[kc], 1)

            def turn_h2(g):
                pe.wait_ge(s_h2, g + 1)
                for kc in range(KC):
                    if g >= 1:
                        pe.wait_ge(s_h2tc[kc], g)
                    for s in range(GT):
                        mm = pe.transpose(ps[:, kc, s * P:(s + 1) * P], h2[:, g % 2, s, kc * P:(kc + 1) * P],
                                          idf[:, :])
                    mm.then_inc(s_h2t[kc], 1)

            turn_o(0)
            for g in range(GROUPS):
                for kc in range(KC):
                    pe.wait_ge(s_tc[kc], LAST_USE + g + 1)
                if g >= 1:
                    pe.wait_ge(s_add1, g)
                for s in range(GT):
                    for kc in range(KC):
                        mm = pe.matmul(ps[:, 6 + s // 2, (s % 2) * D:(s % 2 + 1) * D],
                                       oT[:, g % 2, kc, s * P:(s + 1) * P], wo_sb[:, kc, :],
                                       start=(kc == 0), stop=(kc == KC - 1))
                mm.then_inc(s_att, 1)
                if g + 1 < GROUPS:
                    turn_o(g + 1)
                if g >= 1:
                    turn_h2(g - 1)
            turn_h2(GROUPS - 1)
            for kc in range(KC):
                pe.wait_ge(s_h2tc[kc], GROUPS)

            pe.sem_inc(s_s2, 6)
            pe.sem_inc(s_xt, 6)
            pe.sem_inc(s_xu, 2)
            pe.wait_ge(s_g, 16)
            pe.wait_ge(s_u, 64)

            def cross_scores(j, u):
                pe.wait_ge(s_h2s, j * 2 + (u + 1))
                for n, (h0, h1) in enumerate(XBANKS):
                    pe.wait_ge(s_xe, j * 6 + (3 * u + n + 1))
                    for kc in range(KC):
                        mm = pe.matmul(ps[:, n, 0:(h1 - h0) * NCTX], h2s[:, u, kc, :],
                                       g_sb[:, kc, u, h0 * NCTX:h1 * NCTX], start=(kc == 0), stop=(kc == KC - 1))
                    mm.then_inc(s_s2, 1)

            def cross_step(j, u, following):
                normalised = 0
                for n in range(3):
                    pe.wait_ge(s_xc[n], j * 2 + (u + 1))
                    for c in range(4 * n, min(4 * n + 4, XCH)):
                        w = P if c < XCH - 1 else XTAIL
                        need = max(m for m, (h0, h1) in enumerate(XBANKS) if h0 * NCTX < c * P + w) + 1
                        if need > normalised:
                            pe.wait_ge(s_xn, j * 6 + (3 * u + need))
                            normalised = need
                        mm = pe.transpose(ps[0:w, 3 + n, (c - 4 * n) * P:(c - 4 * n + 1) * P],
                                          xp[:, u, c * P:c * P + w], idf[:, :])
                    mm.then_inc(s_xt, 1)
                if following is not None:
                    cross_scores(*following)
                for n in range(3):
                    pe.wait_ge(s_xc[n], j * 2 + (u + 2))
                pe.wait_ge(s_x2, j * 2 + (u + 1))
                for c in range(XCH):
                    w = P if c < XCH - 1 else XTAIL
                    mm = pe.matmul(ps[:, 6 + u, 0:D], xpT[0:w, u, c, :], u_sb[0:w, u, c, :],
                                   start=(c == 0), stop=(c == XCH - 1))
                mm.then_inc(s_xu, 1)

            cross_scores(0, 0)
            with pe.Fori(0, TPB - 1) as j:
                cross_step(j, 0, (j, 1))
                cross_step(j, 1, (j + 1, 0))
            cross_step(TPB - 1, 0, (TPB - 1, 1))
            cross_step(TPB - 1, 1, None)

            pe.sem_inc(s3_t, 1)
            pe.sem_inc(s3_y, 16)
            pe.wait_ge(s_we, 16 * 6)
            pe.wait_ge(s_cnt0, 3)
            pe.wait_ge(s_x2, TILES + 2)

            def turn_rows(j, v):
                pe.wait_ge(s3_h, j + 1)
                pe.wait_ge(s3_tc, j + 1)
                for kc in range(KC):
                    for u in range(2):
                        at = (2 * kc + u) * P
                        mm = pe.transpose(ps[:, 4, at:at + P], h3[:, v, u, kc * P:(kc + 1) * P], idf[:, :])
                mm.then_inc(s3_t, 1)

            def logits(j, v):
                pe.wait_ge(s3_tc, j + 2)
                pe.wait_ge(s3_w, j + 1)
                for u in range(2):
                    for kc in range(KC):
                        at = (2 * kc + u) * P
                        mm = pe.matmul(ps[:, 5, u * EXPERTS:(u + 1) * EXPERTS], h3T[:, v, at:at + P], wg_sb[:, kc, :],
                                       start=(kc == 0), stop=(kc == KC - 1))
                mm.then_inc(s3_l, 1)

            def counts(j, v):
                pe.wait_ge(s3_o, j + 1)
                pe.matmul(ps[:, 5, 16:24], earlier_b[:, :], chosen[:, v, 0, :], start=True, stop=True)
                pe.matmul(ps[:, 5, 24:32], earlier_b[:, :], chosen[:, v, 1, :], start=True, stop=False)
                pe.matmul(ps[:, 5, 24:32], ones_b[:, :], chosen[:, v, 0, :], start=False, stop=True)
                pe.matmul(ps[:, 5, 32:40], ones_b[:, :], chosen[:, v, 0, :], start=True, stop=False)
                pe.matmul(ps[:, 5, 32:40], ones_b[:, :], chosen[:, v, 1, :], start=False, stop=True
                          ).then_inc(s3_c, 1)

            def turn_weights(j, v):
                pe.wait_ge(s3_w, j + 2)
                pe.wait_ge(s3_wc, j + 1)
                for u in range(2):
                    mm = pe.transpose(ps[0:EXPERTS, 6, u * P:(u + 1) * P], wgt[:, v, u, :], idf[:, :])
                mm.then_inc(s3_wt, 1)

            def biases(j, v):
                pe.wait_ge(s3_wc, j + 2)
                pe.wait_ge(s3_acc, j * 18 + 1)
                for u in range(2):
                    mm = pe.matmul(ps[:, 7, u * D:(u + 1) * D], wgtT[:, v, u * P:(u + 1) * P], be_sb[:, :],
                                   start=True, stop=True)
                mm.then_inc(s3_b, 1)

            def experts_out(j, v, u, q):
                pe.wait_ge(s3_acc, j * 18 + (9 * u + 2 * q + 3))
                for kc in range(KC):
                    at = (2 * kc + u) * P
                    mm = pe.matmul(ps[:, q, :], h3T[:, v, at:at + P], we_sb[:, kc, q * BANK:(q + 1) * BANK],
                                   start=(kc == 0), stop=(kc == KC - 1))
                mm.then_inc(s3_y, 1)

            def experts_step(j, v, last):
                experts_out(j, v, 0, 0)
                biases(j, v)
                experts_out(j, v, 0, 1)
                if not last:
                    turn_rows(j + 1, 1 - v)
                experts_out(j, v, 0, 2)
                if not last:
                    logits(j + 1, 1 - v)
                experts_out(j, v, 0, 3)
                experts_out(j, v, 1, 0)
                experts_out(j, v, 1, 1)
                if not last:
                    counts(j + 1, 1 - v)
                experts_out(j, v, 1, 2)
                experts_out(j, v, 1, 3)
                if not last:
                    turn_weights(j + 1, 1 - v)

            turn_rows(0, 0)
            logits(0, 0)
            counts(0, 0)
            turn_weights(0, 0)
            with pe.Fori(0, TILES // 4 - 1) as jj:
                experts_step(2 * jj, 0, False)
                experts_step(2 * jj + 1, 1, False)
            experts_step(TILES // 2 - 2, 0, False)
            experts_step(TILES // 2 - 1, 1, True)


def kernel(**inputs):
    import numpy as _np
    import concourse.bacc as _bacc
    from concourse import mybir as _mybir
    from concourse.bass_utils import run_bass_kernel_spmd as _run

    a = {k: _np.asarray(v) for k, v in inputs.items()}
    arange = _np.arange
    arrays = {
        "x": a["x"].reshape(TOKENS, D),
        "ctxT": a["ctx_768"].reshape(BATCH * NCTX, DCTX).T,
        "wqT": a["L0_attn_Wq"].T,
        "wkT": a["L0_attn_Wk"].T,
        "wvT": a["L0_attn_Wv"].T,
        "woT": a["L0_attn_Wo"].T,
        "pekT": a["L0_attn_pek"].T,
        "pek0": _np.tile(a["L0_attn_pek"][0], P // HD).reshape(P, 1),
        "pev": a["L0_attn_pev"],
        "xwqT": a["L0_xattn_Wq"].T,
        "xwk": a["L0_xattn_Wk"],
        "xwv": a["L0_xattn_Wv"],
        "xwo": a["L0_xattn_Wo"],
        "xbo": a["L0_xattn_bo"].reshape(1, D),
        "wg": a["L0_ffn_wg"],
        "weT": a["L0_ffn_W"].transpose(2, 0, 1),
        "be": a["L0_ffn_b"],
        "ident": _np.eye(P, dtype=_np.float32),
        "ones": _np.ones((P, P), _np.float32),
        "diag": (3 - arange(P)[:, None] // HD % 4 == arange(4 * HEADS)[None, :] % 4).astype(_np.float32),
        "fold": _np.stack([(arange(P)[:, None] % HD == arange(HD)[None, :]) & (arange(P)[:, None] // 64 == e)
                           for e in range(2)], axis=1).astype(_np.float32),
        "earlier": (arange(P)[:, None] < arange(P)[None, :]).astype(_np.float32),
        "experts": _np.broadcast_to(arange(EXPERTS, dtype=_np.float32) - EXPERTS, (P, EXPERTS)),
    }
    nc = _bacc.Bacc("TRN2", target_bir_lowering=False, num_devices=1)
    ins, args = {}, []
    for name, v in arrays.items():
        v = _np.ascontiguousarray(v)
        ins[f"in_{name}"] = v
        args.append(nc.dram_tensor(f"in_{name}", v.shape, _mybir.dt.from_np(v.dtype), kind="ExternalInput").ap())
    out = nc.dram_tensor("out_0", (TOKENS, D), _mybir.dt.float32, kind="ExternalOutput").ap()
    decoder_layer(nc, *args, out)
    r = _run(nc, [ins], core_ids=[0])
    return r.results[0]["out_0"].reshape(BATCH, SEQ, D)
```
